# Optimizing a Trainium2 kernel written in Bass

```python
import numpy as np
import jax
import jax.numpy as jnp

def _softmax(x, axis=-1):
    return jax.nn.softmax(x, axis=axis)

def _gelu(x):
    return jax.nn.gelu(x, approximate=True)

def _silu(x):
    return jax.nn.silu(x)

def _sigmoid(x):
    return jax.nn.sigmoid(x)

def _layernorm(x, axis=-1, eps=1e-05):
    m = jnp.mean(x, axis=axis, keepdims=True)
    v = jnp.var(x, axis=axis, keepdims=True)
    return (x - m) / jnp.sqrt(v + eps)

def _scatter_add(tgt, idx, src, axis=0):
    return tgt.at[idx].add(src)

def _segment_sum(src, seg, n):
    return jax.ops.segment_sum(src, seg, n)
kernel_name = 'mk_perceiver_d2_seqx_r8_4eccc6'

def setup_inputs(seed: int=0):
    np.random.seed(seed)
    _w = jnp.asarray

    def _rec_inputs():
        import jax
        import jax.numpy as jnp
        _rk = jax.random.key(seed)
        x = -0.000125 + 0.9999 * jax.random.normal(jax.random.fold_in(_rk, 1), (8, 32, 256), jnp.float32)
        _lenS = 32 - jax.random.randint(jax.random.fold_in(_rk, 7), (8,), 0, max(1, 32 // 4) + 1, jnp.int32)
        _lenS2 = 512 - jax.random.randint(jax.random.fold_in(_rk, 8), (8,), 0, max(1, 512 // 4) + 1, jnp.int32)
        _ctx_2048P = jax.random.normal(jax.random.fold_in(_rk, 11), (8, 16, 256), jnp.float32)
        _ctx_2048c = jax.random.dirichlet(jax.random.fold_in(_rk, 511), 0.3 * jnp.ones((16,), jnp.float32), (8, 512))
        _ctx_2048t = jnp.einsum('bsk,bkd->bsd', _ctx_2048c, _ctx_2048P)
        _ctx_2048t = _ctx_2048t * jax.lax.rsqrt(jnp.mean(jnp.square(_ctx_2048t)) + 1e-12) * 0.953939
        ctx_2048 = -0.000514642 + 1.00011 * (_ctx_2048t + 0.3 * jax.random.normal(jax.random.fold_in(_rk, 611), (8, 512, 256), jnp.float32))
        _validS = jnp.arange(32)[None, :] < _lenS[:, None]
        _validS2 = jnp.arange(512)[None, :] < _lenS2[:, None]
        _causal = jnp.tril(jnp.ones((32, 32), dtype=bool))
        mask_BxS2_bk0 = jnp.logical_not(jnp.broadcast_to(_validS2[:, :], (8, 512)))
        return (x, ctx_2048, mask_BxS2_bk0)
    x, ctx_2048, mask_BxS2_bk0 = _rec_inputs()

    def _L0_xattn_setup():
        import jax, jax.numpy as jnp
        import numpy as np
        key = jax.random.key(seed)
        k1, k2, k3 = jax.random.split(key, 3)
        B, S, D, M = (8, 256, 256, 128)
        hidden_states = jax.random.normal(k1, (B, S, D), dtype=jnp.float32)
        memory_tokens = jax.random.normal(k2, (B, M, D), dtype=jnp.float32)
        memory_mask = jax.random.randint(k3, (B, M), 0, 2).astype(jnp.bool_)
        return {'hidden_states': hidden_states, 'memory_tokens': memory_tokens, 'memory_mask': memory_mask}
    _L0_xattn_all = _L0_xattn_setup()
    _L0_xattn_in = {k: v for k, v in _L0_xattn_all.items() if k in ()}
    del _L0_xattn_all

    def _L0_attn_setup():
        import jax, jax.numpy as jnp
        import numpy as np
        DIM = 256
        STATE = 64
        DT_RANK = 128
        CHUNK = 64
        key = jax.random.key(seed)
        ks = jax.random.split(key, 8)
        B, L, D, N, R = (4, 256, DIM, STATE, DT_RANK)
        x = jax.random.normal(ks[0], (B, L, D), dtype=jnp.float32)
        norm_w = jnp.ones((D,), jnp.float32)
        norm_b = jnp.zeros((D,), jnp.float32)
        x_proj_w = jax.random.normal(ks[1], (R + 2 * N, D), jnp.float32) * (1.0 / np.sqrt(D))
        dt_proj_w = jax.random.normal(ks[2], (D, R), jnp.float32) * (1.0 / np.sqrt(R))
        dt_proj_b = jax.random.normal(ks[3], (D,), jnp.float32) * 0.01
        A_log = jnp.log(jnp.tile(jnp.arange(1, N + 1, dtype=jnp.float32)[None, :], (D, 1)))
        D_param = jnp.ones((D,), jnp.float32)
        out_proj_w = jax.random.normal(ks[4], (D, D), jnp.float32) * (1.0 / np.sqrt(D))
        return {'x': x, 'norm_w': norm_w, 'norm_b': norm_b, 'x_proj_w': x_proj_w, 'dt_proj_w': dt_proj_w, 'dt_proj_b': dt_proj_b, 'A_log': A_log, 'D_param': D_param, 'out_proj_w': out_proj_w}
    _L0_attn_all = _L0_attn_setup()
    _L0_attn_in = {k: v for k, v in _L0_attn_all.items() if k in ('norm_w', 'norm_b', 'x_proj_w', 'dt_proj_w', 'dt_proj_b', 'A_log', 'D_param', 'out_proj_w')}
    del _L0_attn_all

    def _L0_ffn_setup():
        import jax, jax.numpy as jnp
        import numpy as np
        E, K, H, F = (64, 6, 256, 96)
        G, KG = (8, 4)
        SHARED_F = 96
        SCALE = 2.5
        T = 2 * 128
        CAP = 2 * (T * K // E)

        def _grouped_topk(logits, bias):
            scores = jax.nn.sigmoid(logits.astype(jnp.float32))
            scores_b = scores + bias[None, :]
            gs = scores_b.reshape(-1, G, E // G)
            group_scores = jnp.sum(jax.lax.top_k(gs, 2)[0], axis=-1)
            gidx = jax.lax.top_k(group_scores, KG)[1]
            rows = jnp.arange(group_scores.shape[0])[:, None]
            group_mask = jnp.zeros_like(group_scores).at[rows, gidx].set(1.0)
            score_mask = jnp.repeat(group_mask, E // G, axis=-1) > 0
            tmp = jnp.where(score_mask, scores_b, -jnp.inf)
            topk_ids = jax.lax.top_k(tmp, K)[1]
            topk_w = jnp.take_along_axis(scores, topk_ids, axis=-1)
            topk_w = topk_w / jnp.sum(topk_w, axis=-1, keepdims=True)
            return (topk_w * SCALE, topk_ids)

        def _routed_moe(x, topk_w, topk_ids, w_gate, w_up, w_down):
            Tn = x.shape[0]
            flat_e = topk_ids.reshape(-1)
            order = jnp.argsort(flat_e)
            se = flat_e[order]
            pos = jnp.arange(Tn * K) - jnp.searchsorted(se, se, side='left')
            tok = order // K
            valid = pos < CAP
            slot = jnp.where(valid, pos, CAP)
            buf = jnp.zeros((E, CAP + 1, H), x.dtype).at[se, slot].set(x[tok])[:, :CAP]
            h = jax.nn.silu(jnp.einsum('ech,ehf->ecf', buf, w_gate)) * jnp.einsum('ech,ehf->ecf', buf, w_up)
            out = jnp.einsum('ecf,efh->ech', h, w_down)
            gathered = out[se, jnp.minimum(pos, CAP - 1)] * valid.astype(x.dtype)[:, None]
            w = topk_w.reshape(-1)[order].astype(x.dtype)[:, None]
            return jax.ops.segment_sum(gathered * w, tok, num_segments=Tn)
        key = jax.random.key(seed)
        ks = jax.random.split(key, 9)
        s = 0.02
        return dict(hidden_states=jax.random.normal(ks[0], (2, 128, H), jnp.float32), gate_w=jax.random.normal(ks[1], (H, E), jnp.float32) * s, bias=jax.random.normal(ks[2], (E,), jnp.float32) * s, w_gate=jax.random.normal(ks[3], (E, H, F), jnp.float32) * s, w_up=jax.random.normal(ks[4], (E, H, F), jnp.float32) * s, w_down=jax.random.normal(ks[5], (E, F, H), jnp.float32) * s, ws_gate=jax.random.normal(ks[6], (H, SHARED_F), jnp.float32) * s, ws_up=jax.random.normal(ks[7], (H, SHARED_F), jnp.float32) * s, ws_down=jax.random.normal(ks[8], (SHARED_F, H), jnp.float32) * s)
    _L0_ffn_all = _L0_ffn_setup()
    _L0_ffn_in = {k: v for k, v in _L0_ffn_all.items() if k in ('gate_w', 'bias', 'w_gate', 'w_up', 'w_down', 'ws_gate', 'ws_up', 'ws_down')}
    del _L0_ffn_all

    def _L1_xattn_setup():
        import jax, jax.numpy as jnp
        import numpy as np
        D_MODEL = 256
        NUM_HEADS = 16
        HEAD_DIM = D_MODEL // NUM_HEADS

        def _fq_sym(x, axis):
            s = jnp.max(jnp.abs(x), axis=axis, keepdims=True) / 127.0
            s = jnp.maximum(s, 1e-08)
            q = jnp.clip(jnp.round(x / s), -127.0, 127.0) * s
            return x + jax.lax.stop_gradient(q - x)

        def _fq_unsigned(x, axis):
            s = jnp.max(x, axis=axis, keepdims=True) / 255.0
            s = jnp.maximum(s, 1e-08)
            q = jnp.clip(jnp.round(x / s), 0.0, 255.0) * s
            return x + jax.lax.stop_gradient(q - x)
        key = jax.random.key(seed)
        ks = jax.random.split(key, 8)
        B, N, M, C = (2, 256, 64, D_MODEL)
        return {'x': jax.random.normal(ks[0], (B, N, C), jnp.float32), 'cond': jax.random.normal(ks[1], (B, M, C), jnp.float32), 'Wq': jax.random.normal(ks[2], (C, C), jnp.float32) * 0.02, 'bq': jnp.zeros((C,), jnp.float32), 'Wkv': jax.random.normal(ks[3], (C, 2 * C), jnp.float32) * 0.02, 'bkv': jnp.zeros((2 * C,), jnp.float32), 'Wp': jax.random.normal(ks[4], (C, C), jnp.float32) * 0.02, 'bp': jnp.zeros((C,), jnp.float32)}
    _L1_xattn_all = _L1_xattn_setup()
    _L1_xattn_in = {k: v for k, v in _L1_xattn_all.items() if k in ('Wq', 'bq', 'Wkv', 'bkv', 'Wp', 'bp')}
    del _L1_xattn_all

    def _L1_attn_setup():
        import jax, jax.numpy as jnp
        import numpy as np
        from jax import lax
        D_MODEL = 256
        D_INNER = 512
        D_CONV = 4
        B, T = (4, 256)

        def _rmsnorm(h):
            n = jnp.sqrt(jnp.sum(h * h, axis=-1, keepdims=True))
            return h / jnp.maximum(n, 1e-12) * h.shape[-1] ** 0.5

        def _mamba_fallback(h, W_in, conv_w, conv_b, W_out):
            xz = jnp.einsum('btd,ed->bte', h, W_in)
            xp, z = jnp.split(xz, 2, axis=-1)
            xc = lax.conv_general_dilated(xp.transpose(0, 2, 1), conv_w, window_strides=(1,), padding=[(D_CONV - 1, 0)], dimension_numbers=('NCH', 'OIH', 'NCH'), feature_group_count=D_INNER) + conv_b[None, :, None]
            xc = xc.transpose(0, 2, 1)
            y = jax.nn.silu(xc) * jax.nn.silu(z)
            return jnp.einsum('bte,de->btd', y, W_out)
        key = jax.random.key(seed)
        ks = jax.random.split(key, 7)
        std = 0.02
        return {'x': jax.random.normal(ks[0], (B, T, D_MODEL), jnp.float32), 'W_in': jax.random.normal(ks[1], (2 * D_INNER, D_MODEL), jnp.float32) * std, 'conv_w': jax.random.normal(ks[2], (D_INNER, 1, D_CONV), jnp.float32) * std, 'conv_b': jnp.zeros((D_INNER,), jnp.float32), 'W_out': jax.random.normal(ks[3], (D_MODEL, D_INNER), jnp.float32) * std, 'W_mlp1': jax.random.normal(ks[4], (4 * D_MODEL, D_MODEL), jnp.float32) * std, 'W_mlp2': jax.random.normal(ks[5], (D_MODEL, 4 * D_MODEL), jnp.float32) * std}
    _L1_attn_all = _L1_attn_setup()
    _L1_attn_in = {k: v for k, v in _L1_attn_all.items() if k in ('W_in', 'conv_w', 'conv_b', 'W_out', 'W_mlp1', 'W_mlp2')}
    del _L1_attn_all

    def _L1_ffn_setup():
        import jax, jax.numpy as jnp
        import numpy as np
        TOP_K = 4
        key = jax.random.key(seed)
        ks = jax.random.split(key, 8)
        B, S, H, E, F = (1, 256, 256, 16, 176)
        Fs = 2 * F
        s = 0.02
        return {'hidden_states': jax.random.normal(ks[0], (B, S, H), jnp.float32), 'gate_weight': jax.random.normal(ks[1], (E, H), jnp.float32) * s, 'w_gate': jax.random.normal(ks[2], (E, H, F), jnp.float32) * s, 'w_up': jax.random.normal(ks[3], (E, H, F), jnp.float32) * s, 'w_down': jax.random.normal(ks[4], (E, F, H), jnp.float32) * s, 'ws_gate': jax.random.normal(ks[5], (H, Fs), jnp.float32) * s, 'ws_up': jax.random.normal(ks[6], (H, Fs), jnp.float32) * s, 'ws_down': jax.random.normal(ks[7], (Fs, H), jnp.float32) * s}
    _L1_ffn_all = _L1_ffn_setup()
    _L1_ffn_in = {k: v for k, v in _L1_ffn_all.items() if k in ('gate_weight', 'w_gate', 'w_up', 'w_down', 'ws_gate', 'ws_up', 'ws_down')}
    del _L1_ffn_all
    return {'x': x, 'ctx_2048': ctx_2048, 'mask_BxS2_bk0': mask_BxS2_bk0, 'L0_attn_norm_w': _L0_attn_in['norm_w'], 'L0_attn_norm_b': _L0_attn_in['norm_b'], 'L0_attn_x_proj_w': _L0_attn_in['x_proj_w'], 'L0_attn_dt_proj_w': _L0_attn_in['dt_proj_w'], 'L0_attn_dt_proj_b': _L0_attn_in['dt_proj_b'], 'L0_attn_A_log': _L0_attn_in['A_log'], 'L0_attn_D_param': _L0_attn_in['D_param'], 'L0_attn_out_proj_w': _L0_attn_in['out_proj_w'], 'L0_ffn_gate_w': _L0_ffn_in['gate_w'], 'L0_ffn_bias': _L0_ffn_in['bias'], 'L0_ffn_w_gate': _L0_ffn_in['w_gate'], 'L0_ffn_w_up': _L0_ffn_in['w_up'], 'L0_ffn_w_down': _L0_ffn_in['w_down'], 'L0_ffn_ws_gate': _L0_ffn_in['ws_gate'], 'L0_ffn_ws_up': _L0_ffn_in['ws_up'], 'L0_ffn_ws_down': _L0_ffn_in['ws_down'], 'L1_xattn_Wq': _L1_xattn_in['Wq'], 'L1_xattn_bq': _L1_xattn_in['bq'], 'L1_xattn_Wkv': _L1_xattn_in['Wkv'], 'L1_xattn_bkv': _L1_xattn_in['bkv'], 'L1_xattn_Wp': _L1_xattn_in['Wp'], 'L1_xattn_bp': _L1_xattn_in['bp'], 'L1_attn_W_in': _L1_attn_in['W_in'], 'L1_attn_conv_w': _L1_attn_in['conv_w'], 'L1_attn_conv_b': _L1_attn_in['conv_b'], 'L1_attn_W_out': _L1_attn_in['W_out'], 'L1_attn_W_mlp1': _L1_attn_in['W_mlp1'], 'L1_attn_W_mlp2': _L1_attn_in['W_mlp2'], 'L1_ffn_gate_weight': _L1_ffn_in['gate_weight'], 'L1_ffn_w_gate': _L1_ffn_in['w_gate'], 'L1_ffn_w_up': _L1_ffn_in['w_up'], 'L1_ffn_w_down': _L1_ffn_in['w_down'], 'L1_ffn_ws_gate': _L1_ffn_in['ws_gate'], 'L1_ffn_ws_up': _L1_ffn_in['ws_up'], 'L1_ffn_ws_down': _L1_ffn_in['ws_down']}

def reference(x, ctx_2048, mask_BxS2_bk0, L0_attn_norm_w, L0_attn_norm_b, L0_attn_x_proj_w, L0_attn_dt_proj_w, L0_attn_dt_proj_b, L0_attn_A_log, L0_attn_D_param, L0_attn_out_proj_w, L0_ffn_gate_w, L0_ffn_bias, L0_ffn_w_gate, L0_ffn_w_up, L0_ffn_w_down, L0_ffn_ws_gate, L0_ffn_ws_up, L0_ffn_ws_down, L1_xattn_Wq, L1_xattn_bq, L1_xattn_Wkv, L1_xattn_bkv, L1_xattn_Wp, L1_xattn_bp, L1_attn_W_in, L1_attn_conv_w, L1_attn_conv_b, L1_attn_W_out, L1_attn_W_mlp1, L1_attn_W_mlp2, L1_ffn_gate_weight, L1_ffn_w_gate, L1_ffn_w_up, L1_ffn_w_down, L1_ffn_ws_gate, L1_ffn_ws_up, L1_ffn_ws_down):
    import jax
    import jax.numpy as jnp

    def _L0_xattn_ref(hidden_states, memory_tokens, memory_mask):
        import jax, jax.numpy as jnp
        import numpy as np
        B, S, D = hidden_states.shape
        scale = 1.0 / jnp.sqrt(jnp.asarray(D, hidden_states.dtype))
        scores = jnp.einsum('bsd,bmd->bsm', hidden_states, memory_tokens) * scale
        neg_inf = jnp.asarray(-1e+30, scores.dtype)
        scores = jnp.where(memory_mask[:, None, :], scores, neg_inf)
        attn = jax.nn.softmax(scores, axis=-1)
        readout = jnp.einsum('bsm,bmd->bsd', attn, memory_tokens)
        valid_b = jnp.any(memory_mask, axis=-1)
        out = jnp.where(valid_b[:, None, None], readout, jnp.zeros_like(readout))
        return out

    def _L0_attn_ref(x, norm_w, norm_b, x_proj_w, dt_proj_w, dt_proj_b, A_log, D_param, out_proj_w):
        import jax, jax.numpy as jnp
        import numpy as np
        DIM = 256
        STATE = 64
        DT_RANK = 128
        CHUNK = 64
        B, L, D = x.shape
        N = STATE
        mu = jnp.mean(x, axis=-1, keepdims=True)
        var = jnp.var(x, axis=-1, keepdims=True)
        xn = (x - mu) / jnp.sqrt(var + 1e-05) * norm_w + norm_b
        proj = xn @ x_proj_w.T
        R = dt_proj_w.shape[1]
        delta, B_ssm, C_ssm = jnp.split(proj, [R, R + N], axis=-1)
        delta = jax.nn.softplus(delta @ dt_proj_w.T + dt_proj_b)
        A = -jnp.exp(A_log)
        c_idx = jnp.arange(L) % CHUNK
        C_used = C_ssm[:, c_idx, :]

        def step(h, inp):
            dt, b, xt, c = inp
            dA = jnp.exp(dt[:, :, None] * A)
            h = dA * h + dt[:, :, None] * b[:, None, :] * xt[:, :, None]
            y = jnp.einsum('bdn,bn->bd', h, c)
            return (h, y)
        h0 = jnp.zeros((B, D, N), x.dtype)
        xs = (jnp.moveaxis(delta, 1, 0), jnp.moveaxis(B_ssm, 1, 0), jnp.moveaxis(xn, 1, 0), jnp.moveaxis(C_used, 1, 0))
        _, ys = jax.lax.scan(step, h0, xs)
        y = jnp.moveaxis(ys, 0, 1)
        return (y + x * D_param) @ out_proj_w.T

    def _L0_ffn_ref(hidden_states, gate_w, bias, w_gate, w_up, w_down, ws_gate, ws_up, ws_down):
        import jax, jax.numpy as jnp
        import numpy as np
        E, K, H, F = (64, 6, 256, 96)
        G, KG = (8, 4)
        SHARED_F = 96
        SCALE = 2.5
        T = 2 * 128
        CAP = 2 * (T * K // E)

        def _grouped_topk(logits, bias):
            scores = jax.nn.sigmoid(logits.astype(jnp.float32))
            scores_b = scores + bias[None, :]
            gs = scores_b.reshape(-1, G, E // G)
            group_scores = jnp.sum(jax.lax.top_k(gs, 2)[0], axis=-1)
            gidx = jax.lax.top_k(group_scores, KG)[1]
            rows = jnp.arange(group_scores.shape[0])[:, None]
            group_mask = jnp.zeros_like(group_scores).at[rows, gidx].set(1.0)
            score_mask = jnp.repeat(group_mask, E // G, axis=-1) > 0
            tmp = jnp.where(score_mask, scores_b, -jnp.inf)
            topk_ids = jax.lax.top_k(tmp, K)[1]
            topk_w = jnp.take_along_axis(scores, topk_ids, axis=-1)
            topk_w = topk_w / jnp.sum(topk_w, axis=-1, keepdims=True)
            return (topk_w * SCALE, topk_ids)

        def _routed_moe(x, topk_w, topk_ids, w_gate, w_up, w_down):
            Tn = x.shape[0]
            flat_e = topk_ids.reshape(-1)
            order = jnp.argsort(flat_e)
            se = flat_e[order]
            pos = jnp.arange(Tn * K) - jnp.searchsorted(se, se, side='left')
            tok = order // K
            valid = pos < CAP
            slot = jnp.where(valid, pos, CAP)
            buf = jnp.zeros((E, CAP + 1, H), x.dtype).at[se, slot].set(x[tok])[:, :CAP]
            h = jax.nn.silu(jnp.einsum('ech,ehf->ecf', buf, w_gate)) * jnp.einsum('ech,ehf->ecf', buf, w_up)
            out = jnp.einsum('ecf,efh->ech', h, w_down)
            gathered = out[se, jnp.minimum(pos, CAP - 1)] * valid.astype(x.dtype)[:, None]
            w = topk_w.reshape(-1)[order].astype(x.dtype)[:, None]
            return jax.ops.segment_sum(gathered * w, tok, num_segments=Tn)
        orig_shape = hidden_states.shape
        x = hidden_states.reshape(-1, H)
        router_logits = x @ gate_w
        topk_w, topk_ids = _grouped_topk(router_logits, bias)
        y = _routed_moe(x, topk_w, topk_ids, w_gate, w_up, w_down)
        shared = jax.nn.silu(x @ ws_gate) * (x @ ws_up) @ ws_down
        return (y + shared).reshape(orig_shape)

    def _L1_xattn_ref(x, cond, Wq, bq, Wkv, bkv, Wp, bp):
        import jax, jax.numpy as jnp
        import numpy as np
        D_MODEL = 256
        NUM_HEADS = 16
        HEAD_DIM = D_MODEL // NUM_HEADS

        def _fq_sym(x, axis):
            s = jnp.max(jnp.abs(x), axis=axis, keepdims=True) / 127.0
            s = jnp.maximum(s, 1e-08)
            q = jnp.clip(jnp.round(x / s), -127.0, 127.0) * s
            return x + jax.lax.stop_gradient(q - x)

        def _fq_unsigned(x, axis):
            s = jnp.max(x, axis=axis, keepdims=True) / 255.0
            s = jnp.maximum(s, 1e-08)
            q = jnp.clip(jnp.round(x / s), 0.0, 255.0) * s
            return x + jax.lax.stop_gradient(q - x)
        B, N, C = x.shape
        H, hd = (NUM_HEADS, HEAD_DIM)
        q = (x @ Wq + bq).reshape(1, B * N, H, hd)
        kv = (cond @ Wkv + bkv).reshape(1, -1, 2, H, hd)
        k, v = (kv[:, :, 0], kv[:, :, 1])
        scale = 1.0 / np.sqrt(hd).astype(np.float32)
        q = jnp.transpose(q * scale, (0, 2, 1, 3))
        k = jnp.transpose(k, (0, 2, 1, 3))
        v = jnp.transpose(v, (0, 2, 1, 3))
        q = _fq_sym(q, axis=-1)
        k = _fq_sym(k, axis=-1)
        v = _fq_sym(v, axis=2)
        attn = jnp.einsum('bhqd,bhkd->bhqk', q, k)
        attn = jax.nn.softmax(attn.astype(jnp.float32), axis=-1)
        attn = _fq_unsigned(attn, axis=-1)
        out = jnp.einsum('bhqk,bhkd->bhqd', attn, v)
        out = jnp.transpose(out, (0, 2, 1, 3)).reshape(B, N, C)
        return out @ Wp + bp

    def _L1_attn_ref(x, W_in, conv_w, conv_b, W_out, W_mlp1, W_mlp2):
        import jax, jax.numpy as jnp
        import numpy as np
        from jax import lax
        D_MODEL = 256
        D_INNER = 512
        D_CONV = 4
        B, T = (4, 256)

        def _rmsnorm(h):
            n = jnp.sqrt(jnp.sum(h * h, axis=-1, keepdims=True))
            return h / jnp.maximum(n, 1e-12) * h.shape[-1] ** 0.5

        def _mamba_fallback(h, W_in, conv_w, conv_b, W_out):
            xz = jnp.einsum('btd,ed->bte', h, W_in)
            xp, z = jnp.split(xz, 2, axis=-1)
            xc = lax.conv_general_dilated(xp.transpose(0, 2, 1), conv_w, window_strides=(1,), padding=[(D_CONV - 1, 0)], dimension_numbers=('NCH', 'OIH', 'NCH'), feature_group_count=D_INNER) + conv_b[None, :, None]
            xc = xc.transpose(0, 2, 1)
            y = jax.nn.silu(xc) * jax.nn.silu(z)
            return jnp.einsum('bte,de->btd', y, W_out)
        h = _rmsnorm(x)
        x = x + _mamba_fallback(h, W_in, conv_w, conv_b, W_out)
        h = _rmsnorm(x)
        m = jnp.einsum('bte,de->btd', jax.nn.relu(jnp.einsum('btd,ed->bte', h, W_mlp1)), W_mlp2)
        return x + m

    def _L1_ffn_ref(hidden_states, gate_weight, w_gate, w_up, w_down, ws_gate, ws_up, ws_down):
        import jax, jax.numpy as jnp
        import numpy as np
        TOP_K = 4
        B, S, H = hidden_states.shape
        E = gate_weight.shape[0]
        x = hidden_states.reshape(-1, H)
        T = x.shape[0]
        logits = jnp.einsum('th,eh->te', x.astype(jnp.float32), gate_weight.astype(jnp.float32))
        probs = jax.nn.softmax(logits, axis=1)
        top_vals, top_idx = jax.lax.top_k(probs, TOP_K)
        dense_w = jnp.zeros((T, E), probs.dtype).at[jnp.arange(T)[:, None], top_idx].add(top_vals)
        g = jnp.einsum('th,ehf->tef', x, w_gate)
        u = jnp.einsum('th,ehf->tef', x, w_up)
        a = jax.nn.silu(g) * u
        routed = jnp.einsum('te,tef,efh->th', dense_w.astype(x.dtype), a, w_down)
        shared = jnp.einsum('tf,fh->th', jax.nn.silu(x @ ws_gate) * (x @ ws_up), ws_down)
        out = (routed + shared).reshape(B, S, H)
        return out
    x = x + _L0_xattn_ref(_layernorm(x, axis=-1), ctx_2048, mask_BxS2_bk0)
    x = x + _L0_attn_ref(_layernorm(x, axis=-1), L0_attn_norm_w, L0_attn_norm_b, L0_attn_x_proj_w, L0_attn_dt_proj_w, L0_attn_dt_proj_b, L0_attn_A_log, L0_attn_D_param, L0_attn_out_proj_w)
    x = x + _L0_ffn_ref(_layernorm(x, axis=-1), L0_ffn_gate_w, L0_ffn_bias, L0_ffn_w_gate, L0_ffn_w_up, L0_ffn_w_down, L0_ffn_ws_gate, L0_ffn_ws_up, L0_ffn_ws_down)
    x = x + _L1_xattn_ref(_layernorm(x, axis=-1), ctx_2048, L1_xattn_Wq, L1_xattn_bq, L1_xattn_Wkv, L1_xattn_bkv, L1_xattn_Wp, L1_xattn_bp)
    x = x + _L1_attn_ref(_layernorm(x, axis=-1), L1_attn_W_in, L1_attn_conv_w, L1_attn_conv_b, L1_attn_W_out, L1_attn_W_mlp1, L1_attn_W_mlp2)
    x = x + _L1_ffn_ref(_layernorm(x, axis=-1), L1_ffn_gate_weight, L1_ffn_w_gate, L1_ffn_w_up, L1_ffn_w_down, L1_ffn_ws_gate, L1_ffn_ws_up, L1_ffn_ws_down)
    return x

_drawn_inputs = setup_inputs


def setup_inputs(seed=0):
    import zlib

    import numpy as np

    out = dict(_drawn_inputs(seed))
    spreads = {'L0_attn_norm_w': (1.0, 0.2),
     'L0_attn_norm_b': (0.0, 0.1),
     'L0_attn_D_param': (1.0, 0.6),
     'L1_xattn_bq': (0.0, 0.8),
     'L1_xattn_bkv': (0.0, 0.8),
     'L1_xattn_bp': (0.0, 0.8),
     'L1_attn_conv_b': (0.0, 0.8)}
    factors = {'L0_attn_dt_proj_b': 8.0,
     'L0_ffn_gate_w': 8.0,
     'L0_ffn_bias': 8.0,
     'L0_ffn_w_gate': 8.0,
     'L0_ffn_w_up': 8.0,
     'L0_ffn_w_down': 8.0,
     'L0_ffn_ws_gate': 8.0,
     'L0_ffn_ws_up': 8.0,
     'L0_ffn_ws_down': 8.0,
     'L1_xattn_Wq': 8.0,
     'L1_xattn_Wkv': 8.0,
     'L1_xattn_Wp': 8.0,
     'L1_attn_W_in': 8.0,
     'L1_attn_conv_w': 8.0,
     'L1_attn_W_out': 8.0,
     'L1_attn_W_mlp1': 8.0,
     'L1_attn_W_mlp2': 6.461,
     'L1_ffn_gate_weight': 8.0,
     'L1_ffn_w_gate': 8.0,
     'L1_ffn_w_up': 8.0,
     'L1_ffn_w_down': 8.0,
     'L1_ffn_ws_gate': 8.0,
     'L1_ffn_ws_up': 8.0,
     'L1_ffn_ws_down': 8.0}
    for name, (base, spread) in spreads.items():
        noise = np.random.default_rng([zlib.crc32(name.encode()), seed]).standard_normal(out[name].shape)
        drawn = base * np.exp(spread * noise) if base else spread * noise
        out[name] = jnp.asarray(drawn.astype(out[name].dtype))
    for name, factor in factors.items():
        out[name] = (out[name] * factor).astype(out[name].dtype)
    return out
```

```python
import concourse.bass as bass
from concourse import mybir
from contextlib import ExitStack

F32 = mybir.dt.float32
BF16 = mybir.dt.bfloat16
I32 = mybir.dt.int32
ALU = mybir.AluOpType
ACT = mybir.ActivationFunctionType
AX = mybir.AxisListType
ds = bass.ds

P = 128
B, L, D = 8, 32, 256
T = B * L
TC = T // P
KC = D // P
S = 512
NK = B * S
NKC = NK // P
LN_EPS = 1e-5
NEG = 1e30
ROUND = 12582912.0

N = 64
RANK = 128

E0, K0, F0 = 64, 6, 96
G0, KG0 = 8, 4
CAP0 = 2 * (T * K0 // E0)
SCALE0 = 2.5
EPG0 = 4
W0 = EPG0 * F0
NG0 = E0 // EPG0

E1, K1, F1 = 16, 4, 176
EPG1 = 2
W1 = EPG1 * F1
NG1 = E1 // EPG1
DC = 3
SLOT0 = 2 * KC * W0 + DC * D
SLOT1 = 2 * KC * W1 + DC * D
SHARED0 = 2 * KC * F0 + D

RMAX = bass.bass_isa.ReduceOp.absmax
H, HD = 16, 16
INNER = 512
CONV = 4
MLP = 4 * D


class Steps:

    def __init__(self, eng, sem):
        self.eng, self.sem, self.n = eng, sem, 0

    def __call__(self, ins):
        self.n += 1
        ins.then_inc(self.sem, 1)
        self.eng.wait_ge(self.sem, self.n)


class LayerNorm:

    def __init__(self, nc, sb, sem, name):
        self.nc = nc
        self.stats = sb(name + "_stats", [P, TC, 6], F32)
        self.mv = sb(name + "_mean_var", [P, TC, 2], F32)
        self.ve = sb(name + "_var_eps", [P, TC], F32)
        self.std = sb(name + "_std", [P, TC], F32)
        self.rstd = sb(name + "_rstd", [P, TC], F32)
        self.var_ready = sem(name + "_var_ready")
        self.std_ready = sem(name + "_std_ready")

    def vector(self, dve, step, out, in_):
        nc = self.nc
        for t in range(TC):
            step(nc.vector.bn_stats(self.stats[:, t, :], in_[:, t, :]))
            step(nc.vector.bn_aggr(self.mv[:, t, :], self.stats[:, t, :]))
        nc.vector.tensor_scalar(self.ve[:, :], self.mv[:, :, 1], LN_EPS, None, ALU.add).then_inc(self.var_ready, 1)
        dve.wait_ge(self.std_ready, 1)
        step(nc.vector.reciprocal(self.rstd[:, :], self.std[:, :]))
        step(nc.vector.tensor_tensor(self.std[:, :], self.ve[:, :], self.rstd[:, :], ALU.mult))
        step(nc.vector.tensor_tensor(self.std[:, :], self.std[:, :], self.rstd[:, :], ALU.mult))
        step(nc.vector.tensor_scalar(self.std[:, :], self.std[:, :], -0.5, 1.5, ALU.mult, ALU.add))
        step(nc.vector.tensor_tensor(self.rstd[:, :], self.rstd[:, :], self.std[:, :], ALU.mult))
        for t in range(TC):
            step(nc.vector.tensor_scalar(out[:, t, :], in_[:, t, :], self.mv[:, t, 0:1], self.rstd[:, t:t + 1],
                                         ALU.subtract, ALU.mult))

    def scalar(self, act):
        act.wait_ge(self.var_ready, 1)
        self.nc.scalar.activation(self.std[:, :], self.ve[:, :], ACT.Sqrt).then_inc(self.std_ready, 1)


def transpose_tokens(nc, psum_bank, src, ident):
    out = psum_bank.rearrange("p (k t) -> p k t", k=KC)
    for t in range(TC):
        for k in range(KC):
            last = nc.tensor.transpose(out[:, k, t * P:(t + 1) * P], src[:, t, k * P:(k + 1) * P], ident[:, :])
    return last


def keep_warm(nc, g, bank, count):
    four = g["onesb"][:, :].unsqueeze(1).to_broadcast([P, 4, P])
    for _ in range(count):
        nc.tensor.matmul(bank.rearrange("p (a b) -> p a b", a=4), g["identb"][:, :], four, start=True, stop=True)


def scope(nc):
    ctx = ExitStack()

    def sb(name, shape, dt=F32):
        return ctx.enter_context(nc.sbuf_tensor(name, shape, dt))

    def banks(name):
        return ctx.enter_context(nc.psum_tensor(name, [P, 8, 512], F32))

    def sem(name):
        return ctx.enter_context(nc.semaphore(name))

    return ctx, sb, banks, sem



def setup_stage(nc, d, g, sb, sem):
    g["x"] = sb("x_residual", [P, TC, D])
    g["ident"] = sb("ident", [P, P])
    g["identb"] = sb("ident_bf16", [P, P], BF16)
    g["ones"] = sb("ones", [P, P])
    g["onesb"] = sb("ones_bf16", [P, P], BF16)
    g["before"] = sb("before_bf16", [P, P], BF16)
    g["zeros"] = sb("zeros", [P, P])
    g["w0_early"] = sb("w0_early", [P, 2, SLOT0])
    g["shared0"] = sb("shared0", [P, SHARED0])
    g["w0_in"] = [sem(f"w0_in{s}") for s in range(4)]
    g["shared_in"] = [sem(f"shared_in{s}") for s in range(2)]
    g["const_sem"] = sem("constants_ready")
    g["x_in"] = sem("x_in")



def xattn0_stage(nc, d, g):
    ctx, sb, banks, sem = scope(nc)
    x, ident, identb = g["x"], g["ident"], g["identb"]
    with ctx:
        ctxT = sb("a_ctxT", [P, KC, NK])
        ctxk = sb("a_ctx", [P, NKC, D])
        mask_i = sb("a_mask_i", [P, TC, S], I32)
        mask = sb("a_mask", [P, TC, S])
        negm = sb("a_negm", [P, TC, S])
        valid = sb("a_valid", [P, TC])
        xn = sb("a_xn", [P, TC, D])
        xnT = sb("a_xnT", [P, KC, T])
        sc = sb("a_scores", [P, TC, S])
        ex = sb("a_exp", [P, TC, S])
        exT = sb("a_expT", [P, TC, S // P, P])
        nmax = sb("a_nmax", [P, TC])
        den = sb("a_den", [P, TC])
        rden = sb("a_rden", [P, TC])
        ps = banks("a_psum")
        ln = LayerNorm(nc, sb, sem, "a_ln")
        chain = sem("a_dve_chain")
        ctxT_in = [sem(f"a_ctxT_in{t}") for t in range(TC)]
        ctx_in = [sem(f"a_ctx_in{t}") for t in range(TC)]
        mask_in = sem("a_mask_in")
        xn_ready = sem("a_xn_ready")
        xnT_psum = sem("a_xnT_psum")
        xnT_ready = sem("a_xnT_ready")
        scores_ready = sem("a_scores_ready")
        max_ready = sem("a_max_ready")
        exp_ready = sem("a_exp_ready")
        expT_psum = sem("a_expT_psum")
        expT_ready = sem("a_expT_ready")
        read_ready = sem("a_read_ready")
        consts = g["const_sem"]
        g["spent"] = [chain, mask_in, xn_ready, xnT_psum, xnT_ready, scores_ready, max_ready, exp_ready, expT_psum,
                      expT_ready, read_ready, ln.var_ready, ln.std_ready] + ctxT_in + ctx_in

        with nc.Block() as block:
            @block.sync
            def _(sp):
                sp.dma_start(x[:, :, :], d["x"].rearrange("(t p) c -> p t c", p=P)).then_inc(g["x_in"], 16)
                sp.dma_start(mask_i[:, :, :], d["mask"]).then_inc(mask_in, 16)
                for t in range(TC):
                    half = slice(t * NK // TC, (t + 1) * NK // TC)
                    sp.dma_start(ctxT[:, :, half], d["ctxT"][:, :, half]).then_inc(ctxT_in[t], 16)
                for t in range(TC):
                    half = slice(t * NKC // TC, (t + 1) * NKC // TC)
                    sp.dma_start(ctxk[:, half, :], d["ctx"][:, half, :]).then_inc(ctx_in[t], 16)
                sp.dma_start(g["shared0"][:, :], d["shared0"]).then_inc(g["shared_in"][0], 16)
                for s in range(2):
                    sp.dma_start(g["w0_early"][:, s, :], d["w0"][s]).then_inc(g["w0_in"][s], 16)

            @block.gpsimd
            def _(pool):
                for m in (ident, identb, g["zeros"]):
                    nc.gpsimd.memset(m[:, :], 0.0).then_inc(consts, 1)
                for m in (g["ones"], g["onesb"], g["before"]):
                    nc.gpsimd.memset(m[:, :], 1.0).then_inc(consts, 1)
                pool.wait_ge(consts, 6)
                for m in (ident, identb):
                    nc.gpsimd.affine_select(out=m[:, :], in_=m[:, :], compare_op=ALU.not_equal, fill=1.0, base=0,
                                            pattern=[[-1, P]], channel_multiplier=1).then_inc(consts, 1)
                nc.gpsimd.affine_select(out=g["before"][:, :], in_=g["before"][:, :], compare_op=ALU.is_gt, fill=0.0,
                                        base=0, pattern=[[1, P]], channel_multiplier=-1).then_inc(consts, 1)
                pool.wait_ge(consts, 9)

            @block.vector
            def _(dve):
                step = Steps(dve, chain)
                dve.wait_ge(g["x_in"], 16)
                ln.vector(dve, step, xn, x)
                nc.vector.tensor_copy(nmax[:, :], ln.rstd[:, :]).then_inc(xn_ready, 1)
                dve.wait_ge(mask_in, 16)
                step(nc.vector.tensor_copy(mask[:, :, :], mask_i[:, :, :]))
                step(nc.vector.tensor_scalar(negm[:, :, :], mask[:, :, :], NEG, -NEG, ALU.mult, ALU.add))
                step(nc.vector.tensor_reduce(valid[:, :], mask[:, :, :], AX.X, ALU.max))
                for t in range(TC):
                    dve.wait_ge(scores_ready, t + 1)
                    step(nc.vector.scalar_tensor_tensor(sc[:, t, :], ps[:, t, :], D ** -0.5, mask[:, t, :],
                                                        ALU.mult, ALU.mult))
                    step(nc.vector.tensor_tensor(sc[:, t, :], sc[:, t, :], negm[:, t, :], ALU.add))
                    nc.vector.tensor_reduce(nmax[:, t:t + 1], sc[:, t, :], AX.X, ALU.max,
                                            negate=True).then_inc(max_ready, 1)
                for t in range(TC):
                    dve.wait_ge(exp_ready, t + 1)
                    step(nc.vector.reciprocal(rden[:, t:t + 1], den[:, t:t + 1]))
                    step(nc.vector.tensor_tensor(rden[:, t:t + 1], rden[:, t:t + 1], valid[:, t:t + 1], ALU.mult))
                    dve.wait_ge(read_ready, t + 1)
                    step(nc.vector.scalar_tensor_tensor(x[:, t, :], ps[:, 6 + t, 0:D], rden[:, t:t + 1], x[:, t, :],
                                                        ALU.mult, ALU.add))

            @block.scalar
            def _(act):
                ln.scalar(act)
                act.wait_ge(xnT_psum, 1)
                nc.scalar.activation(xnT[:, :, :], ps[:, 7, :].rearrange("p (k t) -> p k t", k=KC),
                                     ACT.Copy).then_inc(xnT_ready, 1)
                for t in range(TC):
                    act.wait_ge(max_ready, t + 1)
                    nc.scalar.activation(ex[:, t, :], sc[:, t, :], ACT.Exp, bias=nmax[:, t:t + 1],
                                         accum_out=den[:, t:t + 1]).then_inc(exp_ready, 1)
                for t in range(TC):
                    act.wait_ge(expT_psum, t + 1)
                    nc.scalar.activation(exT[:, t, :, :], ps[:, 2 + t, :].rearrange("p (c q) -> p c q", q=P),
                                         ACT.Copy).then_inc(expT_ready, 1)

            @block.tensor
            def _(pe):
                pe.wait_ge(consts, 9)
                pe.wait_ge(xn_ready, 1)
                transpose_tokens(nc, ps[:, 7, :], xn, ident).then_inc(xnT_psum, 1)
                pe.wait_ge(xnT_ready, 1)
                for t in range(TC):
                    pe.wait_ge(ctxT_in[t], 16)
                    for j in range(B // TC):
                        b = t * (B // TC) + j
                        for k in range(KC):
                            last = nc.tensor.matmul(ps[j * L:(j + 1) * L, t, :], xnT[:, k, b * L:(b + 1) * L],
                                                    ctxT[:, k, b * S:(b + 1) * S], start=(k == 0), stop=(k == KC - 1))
                    last.then_inc(scores_ready, 1)
                for t in range(TC):
                    pe.wait_ge(exp_ready, t + 1)
                    for c in range(S // P):
                        last = nc.tensor.transpose(ps[:, 2 + t, c * P:(c + 1) * P], ex[:, t, c * P:(c + 1) * P],
                                                   ident[:, :])
                    last.then_inc(expT_psum, 1)
                for t in range(TC):
                    pe.wait_ge(expT_ready, t + 1)
                    pe.wait_ge(ctx_in[t], 16)
                    for j in range(B // TC):
                        b = t * (B // TC) + j
                        for c in range(S // P):
                            last = nc.tensor.matmul(ps[j * L:(j + 1) * L, 6 + t, 0:D], exT[:, t, c, j * L:(j + 1) * L],
                                                    ctxk[:, b * (S // P) + c, :], start=(c == 0), stop=(c == S // P - 1))
                    last.then_inc(read_ready, 1)



def scan_stage(nc, d, g):
    ctx, sb, banks, sem = scope(nc)
    x, ident = g["x"], g["ident"]
    DCH = D // P
    NT = 4
    TILES = N // NT
    UN = 4
    with ctx:
        xpT = sb("b_xprojT", [P, KC, D])
        dtwT = sb("b_dtwT", [P, D])
        outwT = sb("b_outwT", [P, KC, D])
        cols = sb("b_cols", [P, 4, DCH])
        A = sb("b_A", [P, DCH, N])
        z = sb("b_z", [P, TC, D])
        zn = sb("b_zn", [P, TC, D])
        znT = sb("b_znT", [P, KC, T])
        zDT = sb("b_zDT", [P, KC, T])
        drT = sb("b_drT", [P, T])
        dtT = sb("b_dtT", [P, DCH, T])
        dtxT = sb("b_dtxT", [P, DCH, T])
        dtx = sb("b_dtx", [P, TC, D])
        bc = sb("b_bc", [P, TC, 2 * N])
        cT = sb("b_cT", [N, T])
        bdiag = [sb(f"b_bdiag{t}", [P, N, P]) for t in range(TC)]
        cb = sb("b_cb", [P, TILES, TC * NT * P])
        dA = [sb(f"b_dA{s}", [P, TC * NT * P]) for s in range(2)]
        h = [sb(f"b_h{s}", [P, TC * NT * P]) for s in range(UN)]
        sp_abs, sp_e, sp_u, sp_l, sp_z = (h[s][:, q * DCH * T:(q + 1) * DCH * T].rearrange("p (c t) -> p c t", c=DCH)
                                          for s, q in ((0, 0), (0, 1), (1, 0), (1, 1), (2, 0)))
        yT = sb("b_yT", [P, DCH, T])
        ps = banks("b_psum")
        lnA, lnB = LayerNorm(nc, sb, sem, "b_lnA"), LayerNorm(nc, sb, sem, "b_lnB")
        chain = sem("b_dve_chain")
        achain = sem("b_act_chain")
        w_in = sem("b_w_in")
        zn_ready = sem("b_zn_ready")
        zT_psum = sem("b_zT_psum")
        znT_ready = sem("b_znT_ready")
        proj_psum = sem("b_proj_psum")
        drT_ready = sem("b_drT_ready")
        bc_ready = sem("b_bc_ready")
        dt_psum = sem("b_dt_psum")
        cT_psum = sem("b_cT_psum")
        cT_ready = sem("b_cT_ready")
        cT_stored = sem("b_cT_stored")
        cb_in = sem("b_cb_in")
        spe_ready = sem("b_spe_ready")
        spu_ready = sem("b_spu_ready")
        spl_ready = sem("b_spl_ready")
        dt_ready = sem("b_dt_ready")
        dtxT_ready = sem("b_dtxT_ready")
        dtx_psum = sem("b_dtx_psum")
        dtx_ready = sem("b_dtx_ready")
        diag_ready = sem("b_diag_ready")
        edges_ready = sem("b_edges_ready")
        A_ready = sem("b_A_ready")
        u_ready = sem("b_u_ready")
        dA_ready = sem("b_dA_ready")
        h_ready = sem("b_h_ready")
        hc_ready = sem("b_hc_ready")
        y_added = sem("b_y_added")
        y_psum = sem("b_y_psum")
        yT_ready = sem("b_yT_ready")
        out_psum = sem("b_out_psum")

        def tiles_of(eng, body):
            for c in range(DCH):
                base = c * TILES
                with eng.Fori(0, TILES // UN - 1) as i:
                    for s in range(UN):
                        body(c, i * UN + s, i * UN + (base + s), s, True)
                for s in range(UN):
                    n = TILES - UN + s
                    body(c, n, base + n, s, s < UN - 2)

        with nc.Block() as block:
            @block.sync
            def _(sp):
                for dst, name in ((xpT, "xprojT"), (dtwT, "dtwT"), (cols, "cols0"), (A, "A_log"), (outwT, "outwT")):
                    sp.dma_start(dst[:], d[name]).then_inc(w_in, 16)
                sp.wait_ge(cT_ready, 1)
                sp.dma_start(d["c_scratch"], cT[:, :]).then_inc(cT_stored, 16)
                sp.wait_ge(cT_stored, 16)
                src = d["c_scratch"].rearrange("(g n) t -> g (n t)", n=NT)
                for q in range(4):
                    part = slice(q * TILES // 4, (q + 1) * TILES // 4)
                    sp.dma_start(cb[:, part, :], src[part, :].partition_broadcast(P)).then_inc(cb_in, 16)

            @block.gpsimd
            def _(pool):
                for spent in g["spent"]:
                    pool.sem_clear(spent)
                for s in range(2):
                    edge = dA[s][:, :].rearrange("p (s t) -> p s t", t=L)[:, :, 0:1]
                    nc.gpsimd.memset(edge, 0.0).then_inc(edges_ready, 1)
                pool.wait_ge(cb_in, 64)

                def scale_by_c(c, n, m, s, more):
                    pool.wait_ge(h_ready, m + (UN + 1))
                    hv = h[s][:, :].rearrange("p (t n q) -> p t n q", t=TC, n=NT)
                    cv = cb[:, ds(n, 1), :].rearrange("p o (n t q) -> p (o t) n q", t=TC, n=NT)
                    nc.gpsimd.tensor_tensor(hv, hv, cv, ALU.mult).then_inc(hc_ready, 1)
                tiles_of(pool, scale_by_c)

            @block.vector
            def _(dve):
                step = Steps(dve, chain)
                lnA.vector(dve, step, z, x)
                lnB.vector(dve, step, zn, z)
                nc.vector.tensor_copy(lnA.std[:, :], lnB.rstd[:, :]).then_inc(zn_ready, 1)
                dve.wait_ge(w_in, 80)
                dve.wait_ge(zT_psum, 1)
                for k in range(KC):
                    step(nc.vector.tensor_scalar(znT[:, k, :], ps[:, 0, k * T:(k + 1) * T], cols[:, 0, k:k + 1],
                                                 cols[:, 1, k:k + 1], ALU.mult, ALU.add))
                    step(nc.vector.tensor_scalar(zDT[:, k, :], ps[:, 1, k * T:(k + 1) * T], cols[:, 3, k:k + 1],
                                                 None, ALU.mult))
                nc.vector.tensor_copy(lnA.std[:, :], lnB.rstd[:, :]).then_inc(znT_ready, 1)
                dve.wait_ge(proj_psum, 1)
                nc.vector.tensor_copy(drT[:, :], ps[:, 2, 0:T]).then_inc(drT_ready, 1)
                nc.vector.tensor_copy(bc[:, :, :], ps[:, 3, 0:T].rearrange("p (t n) -> p t n", t=TC)).then_inc(bc_ready, 1)
                dve.wait_ge(cT_psum, 1)
                nc.vector.tensor_copy(cT[:, :], ps[0:N, 5, 0:T]).then_inc(cT_ready, 1)
                dve.wait_ge(bc_ready, 1)
                for t in range(TC):
                    idb = ident[:, :].unsqueeze(1).to_broadcast([P, N, P])
                    bb = bc[:, t, 0:N].unsqueeze(2).to_broadcast([P, N, P])
                    nc.vector.tensor_tensor(bdiag[t][:, :, :], idb, bb, ALU.mult).then_inc(diag_ready, 1)
                dve.wait_ge(spe_ready, DCH)
                nc.vector.tensor_scalar(sp_u[:, :, :], sp_e[:, :, :], 1.0, None, ALU.add).then_inc(spu_ready, 1)
                dve.wait_ge(spu_ready, 1)
                step(nc.vector.tensor_scalar(sp_abs[:, :, :], sp_u[:, :, :], 1.0, None, ALU.subtract))
                step(nc.vector.tensor_scalar(sp_z[:, :, :], sp_abs[:, :, :], 0.0, None, ALU.is_equal))
                step(nc.vector.tensor_tensor(sp_abs[:, :, :], sp_abs[:, :, :], sp_z[:, :, :], ALU.add))
                step(nc.vector.reciprocal(sp_abs[:, :, :], sp_abs[:, :, :]))
                dve.wait_ge(spl_ready, 1)
                step(nc.vector.tensor_tensor(sp_abs[:, :, :], sp_abs[:, :, :], sp_l[:, :, :], ALU.mult))
                step(nc.vector.tensor_tensor(sp_abs[:, :, :], sp_abs[:, :, :], sp_z[:, :, :], ALU.add))
                step(nc.vector.tensor_tensor(sp_e[:, :, :], sp_e[:, :, :], sp_abs[:, :, :], ALU.mult))
                for k in range(DCH):
                    step(nc.vector.tensor_scalar(sp_z[:, k, :], ps[:, 4, k * T:(k + 1) * T], cols[:, 2, k:k + 1], 0.0,
                                                 ALU.add, ALU.max))
                nc.vector.tensor_tensor(dtT[:, :, :], sp_z[:, :, :], sp_e[:, :, :], ALU.add).then_inc(dt_ready, 1)
                dve.wait_ge(dt_ready, 1)
                nc.vector.tensor_tensor(dtxT[:, :, :], dtT[:, :, :], znT[:, :, :], ALU.mult).then_inc(dtxT_ready, 1)
                dve.wait_ge(dtx_psum, 1)
                nc.vector.tensor_copy(dtx[:, :, :], ps[:, 6, :].rearrange("p (t c) -> p t c", t=TC)).then_inc(dtx_ready, 1)

                dve.wait_ge(dtx_ready, 1)
                nc.vector.tensor_copy(lnA.std[:, :], lnB.rstd[:, :]).then_inc(h_ready, UN)

                def scan(c, n, m, s, more):
                    dve.wait_ge(u_ready, m + 1)
                    dve.wait_ge(dA_ready, m * NT + NT)
                    dve.wait_ge(y_added, m + 1)
                    nc.vector.tensor_tensor_scan(h[s][:, :], dA[s % 2][:, :], ps[:, 2 * (s % 2):2 * (s % 2) + 2, :]
                                                 .rearrange("p a b -> p (a b)"), 0.0, ALU.mult, ALU.add).then_inc(h_ready, 1)
                tiles_of(dve, scan)
                for c in range(DCH):
                    dve.wait_ge(y_psum, c + 1)
                    nc.vector.tensor_copy(yT[:, c, :], ps[:, 4 + c, 0:T]).then_inc(yT_ready, 1)
                dve.wait_ge(out_psum, 1)
                step(nc.vector.tensor_tensor(x[:, :, :], x[:, :, :], ps[:, 6, :].rearrange("p (t c) -> p t c", t=TC), ALU.add))

            @block.scalar
            def _(act):
                astep = Steps(act, achain)
                lnA.scalar(act)
                lnB.scalar(act)
                act.wait_ge(w_in, 80)
                astep(nc.scalar.activation(A[:, :, :], A[:, :, :], ACT.Exp))
                astep(nc.scalar.activation(A[:, :, :], A[:, :, :], ACT.Copy, scale=-1.0))
                act.wait_ge(dt_psum, 1)
                for k in range(DCH):
                    astep(nc.scalar.activation(sp_l[:, k, :], ps[:, 4, k * T:(k + 1) * T], ACT.Abs,
                                               bias=cols[:, 2, k:k + 1]))
                for k in range(DCH):
                    nc.scalar.activation(sp_e[:, k, :], sp_l[:, k, :], ACT.Exp, scale=-1.0).then_inc(spe_ready, 1)
                act.wait_ge(spu_ready, 1)
                nc.scalar.activation(sp_l[:, :, :], sp_u[:, :, :], ACT.Ln).then_inc(spl_ready, 1)
                act.preload_act_table(ACT.Exp)
                act.wait_ge(dt_ready, 1)
                act.wait_ge(edges_ready, 2)

                def decay(c, n, m, s, more):
                    act.wait_ge(h_ready, m + (UN - 1))
                    out = dA[s % 2][:, :].rearrange("p (t n b l) -> p t n b l", t=TC, n=NT, l=L)
                    src = dtT[:, c, :].rearrange("p (t b l) -> p t b l", t=TC, l=L)[:, :, :, 1:L]
                    for j in range(NT):
                        nc.scalar.activation(out[:, :, j, :, 1:L], src, ACT.Exp,
                                             scale=A[:, c, ds(n * NT + j, 1)]).then_inc(dA_ready, 1)
                tiles_of(act, decay)

            @block.tensor
            def _(pe):
                pe.wait_ge(zn_ready, 1)
                transpose_tokens(nc, ps[:, 0, :], zn, ident)
                transpose_tokens(nc, ps[:, 1, :], z, ident).then_inc(zT_psum, 1)
                pe.wait_ge(znT_ready, 1)
                pe.wait_ge(w_in, 80)
                for k in range(KC):
                    nc.tensor.matmul(ps[:, 2, 0:T], xpT[:, k, 0:RANK], znT[:, k, :], start=(k == 0), stop=(k == KC - 1))
                for t in range(TC):
                    for k in range(KC):
                        last = nc.tensor.matmul(ps[:, 3, t * 2 * N:(t + 1) * 2 * N], znT[:, k, t * P:(t + 1) * P],
                                                xpT[:, k, RANK:D], start=(k == 0), stop=(k == KC - 1))
                last.then_inc(proj_psum, 1)
                pe.wait_ge(drT_ready, 1)
                for k in range(DCH):
                    last = nc.tensor.matmul(ps[:, 4, k * T:(k + 1) * T], dtwT[:, k * P:(k + 1) * P], drT[:, :],
                                            start=True, stop=True)
                last.then_inc(dt_psum, 1)
                pe.wait_ge(bc_ready, 1)
                for t in range(TC):
                    last = nc.tensor.transpose(ps[0:N, 5, t * P:(t + 1) * P], bc[:, t, N:2 * N], ident[:, :])
                last.then_inc(cT_psum, 1)
                pe.wait_ge(dtxT_ready, 1)
                for t in range(TC):
                    for k in range(DCH):
                        last = nc.tensor.transpose(ps[:, 6, t * D + k * P:t * D + (k + 1) * P],
                                                   dtxT[:, k, t * P:(t + 1) * P], ident[:, :])
                last.then_inc(dtx_psum, 1)
                pe.wait_ge(dtx_ready, 1)
                pe.wait_ge(diag_ready, TC)
                pe.wait_ge(cT_ready, 1)

                def drive(c, n, m, s):
                    for t in range(TC):
                        last = nc.tensor.matmul(ps[:, 2 * (s % 2) + t, :], dtx[:, t, c * P:(c + 1) * P],
                                                bdiag[t][:, ds(n * NT, NT), :], start=True, stop=True)
                    last.then_inc(u_ready, 1)

                def sum_states(c, n, m, s, more):
                    if more:
                        pe.wait_ge(h_ready, m + (UN + 1))
                        drive(c, n + 2, m + 2, s)
                    pe.wait_ge(hc_ready, m + 1)
                    hv = h[s][:, :].rearrange("p (t n q) -> p n t q", t=TC, n=NT)
                    for j in range(NT):
                        last = nc.tensor.matmul(ps[:, 4 + c, 0:T], ident[:, :], hv[:, j], start=False, stop=False,
                                                skip_group_check=True)
                    last.then_inc(y_added, 1)

                for c in range(DCH):
                    base = c * TILES
                    if c:
                        pe.wait_ge(h_ready, UN + base)
                    first = nc.tensor.matmul(ps[:, 4 + c, 0:T], ident[:, :], zDT[:, c, :], start=True, stop=False,
                                             skip_group_check=True)
                    if c == 0:
                        first.then_inc(y_added, UN)
                    for n in range(2):
                        drive(c, n, base + n, n)
                    with pe.Fori(0, TILES // UN - 1) as i:
                        for s in range(UN):
                            sum_states(c, i * UN + s, i * UN + (base + s), s, True)
                    for s in range(UN):
                        n = TILES - UN + s
                        sum_states(c, n, base + n, s, s < UN - 2)
                    nc.tensor.matmul(ps[:, 4 + c, 0:T], g["zeros"][:, :], zDT[:, c, :], start=False, stop=True,
                                     skip_group_check=True).then_inc(y_psum, 1)
                pe.wait_ge(yT_ready, DCH)
                for t in range(TC):
                    for k in range(DCH):
                        last = nc.tensor.matmul(ps[:, 6, t * D:(t + 1) * D], yT[:, k, t * P:(t + 1) * P], outwT[:, k, :],
                                                start=(k == 0), stop=(k == DCH - 1))
                last.then_inc(out_psum, 1)

class Moe:

    def __init__(self, name, groups, per, width, shared, unroll):
        self.name, self.groups, self.per, self.width = name, groups, per, width
        self.shared, self.unroll = shared, unroll

    def parts(self, w, width):
        n = KC * width
        return (w[:, 0:n].rearrange("p (k f) -> p k f", k=KC), w[:, n:2 * n].rearrange("p (k f) -> p k f", k=KC),
                w[:, 2 * n:].rearrange("p (c m) -> p c m", m=D))


MOE0 = Moe("c", NG0, EPG0, W0, F0, 4)
MOE1 = Moe("f", NG1, EPG1, W1, W1, 1)


def row_chunks(width):
    return [(c, min(P, width - c * P)) for c in range(-(-width // P))]


def route0(nc, dve, step, r, sem_logits, sem_sel, sem_count, g):
    dve.wait_ge(sem_logits, 1)
    step(nc.vector.tensor_tensor(r.ext[:, :, 0:E0], r.scores[:, :, :],
                                 r.bias[:, :].unsqueeze(1).to_broadcast([P, TC, E0]), ALU.add))
    per = E0 // G0
    for t in range(TC):
        for q in range(G0):
            last = nc.vector.max(r.m8[:, t, q, :], r.ext[:, t, q * per:(q + 1) * per])
    step(last)
    step(nc.vector.tensor_tensor(r.gext[:, :, 0:G0], r.m8[:, :, :, 0], r.m8[:, :, :, 1], ALU.add))
    for t in range(TC):
        step(nc.vector.max(r.top[:, t, :], r.gext[:, t, :]))
        step(nc.vector.match_replace(r.grep[:, t, :], r.top[:, t, :], r.gext[:, t, :], -NEG))
    step(nc.vector.tensor_tensor(r.gmask[:, :, :], r.grep[:, :, 0:G0], r.gext[:, :, 0:G0], ALU.not_equal))
    step(nc.vector.tensor_scalar(r.gneg[:, :, :], r.gmask[:, :, :], NEG, -NEG, ALU.mult, ALU.add))
    e4 = r.ext[:, :, 0:E0].rearrange("p t (q e) -> p t q e", q=G0)
    step(nc.vector.tensor_tensor(e4, e4, r.gmask[:, :, :].unsqueeze(3).to_broadcast([P, TC, G0, per]), ALU.mult))
    step(nc.vector.tensor_tensor(e4, e4, r.gneg[:, :, :].unsqueeze(3).to_broadcast([P, TC, G0, per]), ALU.add))
    for t in range(TC):
        step(nc.vector.max(r.top[:, t, :], r.ext[:, t, :]))
        step(nc.vector.match_replace(r.rep[:, t, :], r.top[:, t, :], r.ext[:, t, :], -3e38))
    step(nc.vector.tensor_tensor(r.sel[:, :, :], r.rep[:, :, 0:E0], r.ext[:, :, 0:E0], ALU.not_equal))
    nc.vector.tensor_copy(r.selb[:, :, :], r.sel[:, :, :]).then_inc(sem_sel, 1)
    step(nc.vector.tensor_tensor(r.w[:, :, :], r.sel[:, :, :], r.scores[:, :, :], ALU.mult))
    step(nc.vector.tensor_reduce(r.sum[:, :], r.w[:, :, :], AX.X, ALU.add))
    step(nc.vector.reciprocal(r.sum[:, :], r.sum[:, :]))
    step(nc.vector.tensor_scalar(r.sum[:, :], r.sum[:, :], SCALE0, None, ALU.mult))
    step(nc.vector.tensor_tensor(r.w[:, :, :], r.w[:, :, :], r.sum[:, :].unsqueeze(2).to_broadcast([P, TC, E0]), ALU.mult))
    dve.wait_ge(sem_count, 1)
    step(nc.vector.tensor_scalar(r.keep[:, :, :], r.count_psum, float(CAP0), None, ALU.is_lt))
    step(nc.vector.tensor_tensor(r.w[:, :, :], r.w[:, :, :], r.keep[:, :, :], ALU.mult))


def route1(nc, dve, step, r, sem_exp, sem_max, g):
    dve.wait_ge(r.logits_ready, 1)
    step(nc.vector.tensor_reduce(r.nmax[:, :], r.logits_psum, AX.X, ALU.max, negate=True))
    step(nc.vector.tensor_tensor(r.scores[:, :, :], r.logits_psum,
                                 r.nmax[:, :].unsqueeze(2).to_broadcast([P, TC, E1]), ALU.add))
    nc.vector.tensor_copy(r.logit[:, :, :], r.scores[:, :, :]).then_inc(sem_max, 1)
    dve.wait_ge(sem_exp, 1)
    step(nc.vector.tensor_reduce(r.sum[:, :], r.scores[:, :, :], AX.X, ALU.add))
    step(nc.vector.reciprocal(r.sum[:, :], r.sum[:, :]))
    step(nc.vector.tensor_tensor(r.ext[:, :, 0:E1], r.scores[:, :, :],
                                 r.sum[:, :].unsqueeze(2).to_broadcast([P, TC, E1]), ALU.mult))
    for t in range(TC):
        step(nc.vector.max(r.top[:, t, :], r.ext[:, t, :]))
        step(nc.vector.match_replace(r.rep[:, t, :], r.top[:, t, :], r.ext[:, t, :], -1.0))
    step(nc.vector.tensor_tensor(r.sel[:, :, :], r.rep[:, :, 0:E1], r.ext[:, :, 0:E1], ALU.not_equal))
    step(nc.vector.tensor_tensor(r.w[:, :, :], r.sel[:, :, :], r.ext[:, :, 0:E1], ALU.mult))


class Space:
    pass


def moe_stage(nc, d, g, moe):
    ctx, sb, banks, sem = scope(nc)
    x, ident = g["x"], g["ident"]
    nm = moe.name
    first = moe is MOE0
    experts, top = (E0, K0) if first else (E1, K1)
    W, UN = moe.width, moe.unroll
    rc = row_chunks(W)
    rc_shared = row_chunks(moe.shared)
    with ctx:
        gate_w = sb(nm + "_gate_w", [P, KC, experts])
        xn = sb(nm + "_xn", [P, TC, D])
        xnT = sb(nm + "_xnT", [P, KC, T])
        silu = [sb(f"{nm}_silu{t}", [P, W]) for t in range(TC)]
        prod = [sb(f"{nm}_prod{t}", [P, W]) for t in range(TC)]
        a = [sb(f"{nm}_a{t}", [P, W]) for t in range(TC)]
        aT = [sb(f"{nm}_aT{t}", [P, DC, P]) for t in range(TC)]
        r = Space()
        r.scores = sb(nm + "_scores", [P, TC, experts])
        r.logit = sb(nm + "_logit", [P, TC, experts])
        pad = 8 - top
        r.ext = sb(nm + "_ext", [P, TC, experts + pad])
        r.rep = sb(nm + "_rep", [P, TC, experts + pad])
        r.sel = sb(nm + "_sel", [P, TC, experts])
        r.w = sb(nm + "_w", [P, TC, experts])
        r.top = sb(nm + "_top", [P, TC, 8])
        r.sum = sb(nm + "_sum", [P, TC])
        r.nmax = sb(nm + "_nmax", [P, TC])
        if first:
            r.bias = sb(nm + "_bias", [P, E0])
            r.m8 = sb(nm + "_m8", [P, TC, G0, 8])
            r.gext = sb(nm + "_gext", [P, TC, G0 + 8 - KG0])
            r.grep = sb(nm + "_grep", [P, TC, G0 + 8 - KG0])
            r.gmask = sb(nm + "_gmask", [P, TC, G0])
            r.gneg = sb(nm + "_gneg", [P, TC, G0])
            r.selb = sb(nm + "_selb", [P, TC, E0], BF16)
            r.keep = sb(nm + "_keep", [P, TC, E0])
            late = sb("w0_late", [P, 2, SLOT0])
            slots = [g["w0_early"][:, 0, :], g["w0_early"][:, 1, :], late[:, 0, :], late[:, 1, :]]
            shared_w = g["shared0"]
        else:
            shared_w = g["shared1"]
        ps = banks(nm + "_psum")
        GU = [[ps[:, 2 * t + u, :] for u in range(2)] for t in range(TC)]
        AT = [ps[:, 4 + t, :] for t in range(TC)]
        ACC = [ps[:, 6 + t, 0:D] for t in range(TC)]
        r.logits_psum = ps[:, 4, 0:TC * experts].rearrange("p (t e) -> p t e", t=TC)
        r.count_psum = ps[:, 5, 0:TC * experts].rearrange("p (t e) -> p t e", t=TC)
        ln = LayerNorm(nc, sb, sem, nm + "_ln")
        chain = sem(nm + "_dve_chain")
        small_in = sem(nm + "_small_in")
        pads_ready = sem(nm + "_pads_ready")
        xn_ready = sem(nm + "_xn_ready")
        xnT_psum = sem(nm + "_xnT_psum")
        xnT_ready = sem(nm + "_xnT_ready")
        r.logits_ready = sem(nm + "_logits_ready")
        score_ready = sem(nm + "_score_ready")
        max_ready = sem(nm + "_max_ready")
        sel_ready = sem(nm + "_sel_ready")
        count_ready = sem(nm + "_count_ready")
        w_ready = sem(nm + "_w_ready")
        gu_ready = sem(nm + "_gu_ready")
        silu_ready = sem(nm + "_silu_ready")
        prod_ready = sem(nm + "_prod_ready")
        a_ready = sem(nm + "_a_ready")
        aT_psum = sem(nm + "_aT_psum")
        aT_ready = sem(nm + "_aT_ready")
        down_done = sem(nm + "_down_done")
        consts = g["const_sem"]

        def half_steps(eng, body):
            rounds = moe.groups // UN
            with eng.Fori(0, rounds - 1) as i:
                for s in range(UN):
                    for t in range(TC):
                        body(i * UN + s, s, t, i * (2 * UN) + (2 + 2 * s + t), i, False)
            for s in range(UN):
                grp = (rounds - 1) * UN + s
                for t in range(TC):
                    body(grp, s, t, 2 + 2 * grp + t, rounds - 1, s == UN - 1)

        with nc.Block() as block:
            @block.sync
            def _(sp):
                sp.dma_start(gate_w[:, :, :], d[f"gate{nm}"]).then_inc(small_in, 16)
                if first:
                    sp.dma_start(r.bias[:, :], d["bias0"]).then_inc(small_in, 16)
                    for s in range(2, UN):
                        sp.dma_start(slots[s], d["w0"][s]).then_inc(g["w0_in"][s], 16)
                    with sp.Fori(0, moe.groups // UN - 1) as i:
                        for s in range(UN):
                            sp.wait_ge(down_done, i * (2 * UN) + (4 + 2 * s))
                            sp.dma_start(slots[s].unsqueeze(1), d["w0"][ds(i * UN + (UN + s), 1), :, :]
                                         .rearrange("o p f -> p o f")).then_inc(g["w0_in"][s], 16)

            @block.gpsimd
            def _(pool):
                nc.gpsimd.memset(r.ext[:, :, experts:], NEG).then_inc(pads_ready, 1)
                if first:
                    nc.gpsimd.memset(r.gext[:, :, G0:], NEG).then_inc(pads_ready, 1)

            @block.vector
            def _(dve):
                step = Steps(dve, chain)
                ln.vector(dve, step, xn, x)
                nc.vector.tensor_copy(ln.std[:, :], ln.rstd[:, :]).then_inc(xn_ready, 1)
                for t in range(TC):
                    dve.wait_ge(silu_ready, t + 1)
                    nc.vector.tensor_tensor(a[t][:, 0:moe.shared], silu[t][:, 0:moe.shared], GU[t][1][:, 0:moe.shared],
                                            ALU.mult).then_inc(a_ready, 1)
                dve.wait_ge(pads_ready, 2 if first else 1)
                dve.wait_ge(small_in, 32 if first else 16)
                if first:
                    route0(nc, dve, step, r, score_ready, sel_ready, count_ready, g)
                else:
                    route1(nc, dve, step, r, score_ready, max_ready, g)
                nc.vector.tensor_copy(r.nmax[:, :], r.sum[:, :]).then_inc(w_ready, 1)

                def weigh(grp, s, t, q, i, end):
                    dve.wait_ge(silu_ready, q + 1)
                    nc.vector.tensor_tensor(prod[t][:, :], silu[t][:, :], GU[t][1][:, 0:W], ALU.mult).then_inc(prod_ready, 1)
                    dve.wait_ge(prod_ready, q - 1)
                    dve.wait_ge(aT_psum, q - 1)
                    wv = r.w[:, t, ds(grp * moe.per, moe.per)].unsqueeze(2).to_broadcast([P, moe.per, W // moe.per])
                    nc.vector.tensor_tensor(a[t][:, :].rearrange("p (e f) -> p e f", e=moe.per),
                                            prod[t][:, :].rearrange("p (e f) -> p e f", e=moe.per), wv,
                                            ALU.mult).then_inc(a_ready, 1)
                half_steps(dve, weigh)
                dve.wait_ge(down_done, 2 + 2 * moe.groups)
                for t in range(TC):
                    step(nc.vector.tensor_tensor(x[:, t, :], x[:, t, :], ACC[t], ALU.add))

            @block.scalar
            def _(act):
                ln.scalar(act)
                act.wait_ge(xnT_psum, 1)
                nc.scalar.activation(xnT[:, :, :], ps[:, 6, :].rearrange("p (k t) -> p k t", k=KC),
                                     ACT.Copy).then_inc(xnT_ready, 1)
                if first:
                    act.wait_ge(r.logits_ready, 1)
                    nc.scalar.activation(r.scores[:, :, :], r.logits_psum, ACT.Sigmoid).then_inc(score_ready, 1)
                act.preload_act_table(ACT.Silu)
                for t in range(TC):
                    act.wait_ge(gu_ready, t + 1)
                    nc.scalar.activation(silu[t][:, 0:moe.shared], GU[t][0][:, 0:moe.shared], ACT.Silu).then_inc(silu_ready, 1)
                if not first:
                    act.wait_ge(max_ready, 1)
                    nc.scalar.activation(r.scores[:, :, :], r.logit[:, :, :], ACT.Exp).then_inc(score_ready, 1)
                    act.preload_act_table(ACT.Silu)

                def copy_aT(t, q, rows):
                    act.wait_ge(aT_psum, q + 1)
                    av = AT[t].rearrange("p (c m) -> p c m", m=P)
                    full = [c for c, k in rows if k == P]
                    if full:
                        last = nc.scalar.activation(aT[t][:, 0:len(full), :], av[:, 0:len(full), :], ACT.Copy)
                    if len(full) < len(rows):
                        c, k = rows[-1]
                        last = nc.scalar.activation(aT[t][0:k, c, :], av[0:k, c, :], ACT.Copy)
                    last.then_inc(aT_ready, 1)

                def silu_of(t, q):
                    act.wait_ge(gu_ready, q + 1)
                    nc.scalar.activation(silu[t][:, :], GU[t][0][:, 0:W], ACT.Silu).then_inc(silu_ready, 1)

                for t in range(TC):
                    copy_aT(t, t, rc_shared)
                    silu_of(t, 2 + t)

                def half(grp, s, t, q, i, end):
                    act.wait_ge(down_done, q - 1)
                    copy_aT(t, q, rc)
                    if not end:
                        silu_of(t, q + 2)
                half_steps(act, half)

            @block.tensor
            def _(pe):
                pe.wait_ge(xn_ready, 1)
                transpose_tokens(nc, ps[:, 6, :], xn, ident).then_inc(xnT_psum, 1)
                pe.wait_ge(xnT_ready, 1)
                pe.wait_ge(small_in, 32 if first else 16)
                for t in range(TC):
                    for k in range(KC):
                        last = nc.tensor.matmul(r.logits_psum[:, t, :], xnT[:, k, t * P:(t + 1) * P], gate_w[:, k, :],
                                                start=(k == 0), stop=(k == KC - 1))
                last.then_inc(r.logits_ready, 1)

                def gate_up(t, parts, width):
                    for u in range(2):
                        for k in range(KC):
                            last = nc.tensor.matmul(GU[t][u][:, 0:width], xnT[:, k, t * P:(t + 1) * P], parts[u][:, k, :],
                                                    start=(k == 0), stop=(k == KC - 1))
                    last.then_inc(gu_ready, 1)

                def turn(t, q, rows):
                    pe.wait_ge(a_ready, q + 1)
                    for c, k in rows:
                        last = nc.tensor.transpose(AT[t][0:k, c * P:(c + 1) * P], a[t][:, c * P:c * P + k], ident[:, :])
                    last.then_inc(aT_psum, 1)

                def down(t, q, rows, parts, start, stop):
                    pe.wait_ge(aT_ready, q + 1)
                    for c, k in rows:
                        last = nc.tensor.matmul(ACC[t], aT[t][0:k, c, :], parts[2][0:k, c, :], start=(start and c == 0),
                                                stop=(stop and c == rows[-1][0]), skip_group_check=True)
                    last.then_inc(down_done, 1)

                def weights(grp, s):
                    if first:
                        return moe.parts(slots[s], W)
                    return [v.rearrange("p o k f -> p (o k) f") for v in (
                        g["w1"][:, ds(grp, 1), 0:KC * W].rearrange("p o (k f) -> p o k f", k=KC),
                        g["w1"][:, ds(grp, 1), KC * W:2 * KC * W].rearrange("p o (k f) -> p o k f", k=KC),
                        g["w1"][:, ds(grp, 1), 2 * KC * W:].rearrange("p o (k f) -> p o k f", k=DC))]

                def arrived(s, rnd):
                    if first:
                        pe.wait_ge(g["w0_in"][s], rnd * 16 + 16)

                sparts = moe.parts(shared_w[:, :], moe.shared)
                pe.wait_ge(g["shared_in"][0 if first else 1], 16)
                if not first:
                    pe.wait_ge(g["w1_in"], 16 * NG1)
                for t in range(TC):
                    gate_up(t, sparts, moe.shared)
                if first:
                    pe.wait_ge(sel_ready, 1)
                    for t in range(TC):
                        if t:
                            nc.tensor.matmul(r.count_psum[:, t, :], g["onesb"][:, :], r.selb[:, 0, :], start=True, stop=False)
                        last = nc.tensor.matmul(r.count_psum[:, t, :], g["before"][:, :], r.selb[:, t, :],
                                                start=(t == 0), stop=True)
                    last.then_inc(count_ready, 1)
                    pe.wait_ge(w_ready, 1)
                else:
                    pe.wait_ge(score_ready, 1)
                for t in range(TC):
                    turn(t, t, rc_shared)
                    if t == 0:
                        arrived(0, 0)
                    gate_up(t, weights(0, 0), W)
                    down(t, t, rc_shared, sparts, True, False)

                def half(grp, s, t, q, i, end):
                    turn(t, q, rc)
                    if not end:
                        if t == 0:
                            arrived((s + 1) % UN, i + (1 if s == UN - 1 else 0))
                        gate_up(t, weights(grp + 1, (s + 1) % UN), W)
                    down(t, q, rc, weights(grp, s), False, end)
                half_steps(pe, half)

K_PARTS = 3
KPS = 2


def layer1_memory(nc, d, g, sb, sem):
    g["v"] = sb("v", [P, NKC, D])
    g["vam"] = sb("v_absmax", [P, D])
    g["w1"] = sb("w1", [P, NG1, SLOT1])
    g["shared1"] = sb("shared1", [P, SLOT1])
    g["w1_in"] = sem("w1_in")


def quantize(nc, step, out, scaled, src, s, rs, absmax, axes, rounded=None):
    step(nc.vector.tensor_reduce(absmax, src, AX.X, ALU.max, apply_absolute_value=True))
    step(nc.vector.tensor_scalar(s, absmax, 1.0 / 127.0, 1e-8, ALU.mult, ALU.max))
    step(nc.vector.reciprocal(rs, s))
    step(nc.vector.tensor_tensor(scaled, src, rs.unsqueeze(2).to_broadcast(axes), ALU.mult))
    step(nc.vector.tensor_scalar(scaled, scaled, ROUND, ROUND, ALU.add, ALU.subtract))
    return nc.vector.tensor_tensor(out, scaled, s.unsqueeze(2).to_broadcast(axes), ALU.mult)


def kv_stage(nc, d, g):
    ctx, sb, banks, sem = scope(nc)
    identb = g["identb"]
    STEPS = NKC // KPS
    KEYS = KPS * P
    with ctx:
        wkv = sb("k_wkv", [P, KC, 2 * D])
        bkv = sb("k_bkv", [P, 2 * D])
        cT = [sb(f"k_ctxT{s}", [P, KC, KEYS]) for s in range(2)]
        v, vam = g["v"], g["vam"]
        bias_part = [sb(f"k_bias_part{q}", [P, 2 * D], BF16) for q in range(K_PARTS)]
        bias_rest = [sb(f"k_bias_rest{q}", [P, 2 * D]) for q in range(2)]
        bias_rows = sb("k_bias_rows", [K_PARTS * 32, 2 * D], BF16)
        vstep = sb("k_v_step_max", [P, D])
        ki = sb("k_ki", [P, KPS, D])
        kq = [sb(f"k_kq{s}", [P, KPS, D]) for s in range(2)]
        rest = [sb(f"k_rest{s}", [P, KPS, D]) for s in range(2)]
        parts = [sb(f"k_parts{s}", [P, K_PARTS, KPS, D], BF16) for s in range(2)]
        kT = [sb(f"k_kT{s}", [P, K_PARTS * KC, KEYS], BF16) for s in range(2)]
        am = sb("k_absmax", [P, KPS * H])
        sc = sb("k_scale", [P, KPS * H])
        rs = sb("k_rscale", [P, KPS * H])
        ps = banks("k_psum")
        w_in = sem("k_w_in")
        cT_in = [sem(f"k_ctxT_in{s}") for s in range(2)]
        chain = sem("k_dve_chain")
        kv_psum = sem("k_kv_psum")
        k_read = sem("k_read")
        v_read = sem("k_v_read")
        bias_ready = sem("k_bias_ready")
        vmax_ready = sem("k_vmax_ready")
        kq_ready = sem("k_kq_ready")
        part0_ready = sem("k_part0_ready")
        rest_ready = sem("k_rest_ready")
        part1_ready = sem("k_part1_ready")
        part2_ready = sem("k_part2_ready")
        kT_psum = sem("k_kT_psum")
        kT_ready = sem("k_kT_ready")
        kT_stored = [sem(f"k_kT_stored{s}") for s in range(2)]
        CH = 5

        def all_steps(eng, body):
            for s in range(2):
                body(s, s, 0, True)
            with eng.Fori(1, STEPS // 2 - 1) as i:
                for s in range(2):
                    body(i * 2 + s, s, i, True)
            for s in range(2):
                body(STEPS - 2 + s, s, STEPS // 2 - 1, False)

        def psum_kv(s, part):
            return ps[:, 2 * s + part, :].rearrange("p (c n) -> p c n", n=D)

        psT = [ps[:, 4 + 2 * s:6 + 2 * s, :].rearrange("p a b -> p (a b)").bitcast(BF16)[:, 0:K_PARTS * KC * KEYS]
               .rearrange("p (q n) -> p q n", n=KEYS) for s in range(2)]

        with nc.Block() as block:
            @block.sync
            def _(sp):
                sp.dma_start(wkv[:, :, :], d["wkv"]).then_inc(w_in, 16)
                sp.dma_start(bkv[:, :], d["bkv"]).then_inc(w_in, 16)
                for s in range(2):
                    sp.dma_start(cT[s][:, :, :], d["ctxT"][:, :, s * KEYS:(s + 1) * KEYS]).then_inc(cT_in[s], 16)

                def load(m, s, i, more):
                    if more:
                        ahead = m * KEYS + 2 * KEYS
                        if not isinstance(m, int):
                            ahead = sp.snap(ahead)
                        sp.wait_ge(kv_psum, m + 1)
                        sp.dma_start(cT[s][:, :, :], d["ctxT"][:, :, ds(ahead, KEYS)]).then_inc(cT_in[s], 16)
                all_steps(sp, load)

            @block.vector
            def _(dve):
                step = Steps(dve, chain)
                dve.sem_inc(k_read, 2)
                nc.vector.memset(vam[:, :], 0.0).then_inc(vmax_ready, 1)
                step(nc.vector.memset(bias_rows[:, :], 0.0))
                dve.wait_ge(w_in, 32)
                rest_ = [bkv] + bias_rest
                for q in range(K_PARTS):
                    step(nc.vector.tensor_copy(bias_part[q][:, :], rest_[q][:, :]))
                    if q < K_PARTS - 1:
                        step(nc.vector.tensor_tensor(rest_[q + 1][:, :], rest_[q][:, :], bias_part[q][:, :], ALU.subtract))
                for q in range(K_PARTS):
                    row = slice(32 * q, 32 * q + 1)
                    nc.vector.tensor_copy(bias_rows[row, :], bias_part[q][row, :]).then_inc(bias_ready, 1)
                lead = step.n

                def quantize_keys(m, s, i, more):
                    step.n = m * CH + lead
                    k4 = psum_kv(s, 0).rearrange("p c (h e) -> p c h e", e=HD)
                    i3 = ki[:, :, :].rearrange("p c (h e) -> p (c h) e", e=HD)
                    i4 = ki[:, :, :].rearrange("p c (h e) -> p c h e", e=HD)
                    am4 = am[:, :].rearrange("p (c h) -> p c h", c=KPS)
                    rs4 = rs[:, :].rearrange("p (c h) -> p c h", c=KPS)
                    dve.wait_ge(kv_psum, m + 1)
                    step(nc.vector.tensor_reduce(am4, k4, AX.X, ALU.max, apply_absolute_value=True))
                    step(nc.vector.tensor_scalar(sc[:, :], am[:, :], 1.0 / 127.0, 1e-8, ALU.mult, ALU.max))
                    step(nc.vector.reciprocal(rs[:, :], sc[:, :]))
                    nc.vector.tensor_tensor(i4, k4, rs4.unsqueeze(3).to_broadcast([P, KPS, H, HD]), ALU.mult).then_inc(k_read, 1)
                    dve.wait_ge(k_read, m + 3)
                    step(nc.vector.tensor_scalar(i3, i3, ROUND, ROUND, ALU.add, ALU.subtract))
                    dve.wait_ge(rest_ready, m + 1)
                    nc.vector.tensor_tensor(kq[s][:, :, :].rearrange("p c (h e) -> p (c h) e", e=HD), i3,
                                            sc[:, :].unsqueeze(2).to_broadcast([P, KPS * H, HD]), ALU.mult).then_inc(kq_ready, 1)
                    dve.wait_ge(v_read, m + 3)
                    dve.wait_ge(vmax_ready, m + 1)
                    step(nc.vector.tensor_reduce(vstep[:, :], v[:, ds(m * KPS, KPS), :].rearrange("p c n -> p n c"), AX.X,
                                                 ALU.max, apply_absolute_value=True))
                    nc.vector.tensor_tensor(vam[:, :], vam[:, :], vstep[:, :], ALU.max).then_inc(vmax_ready, 1)
                all_steps(dve, quantize_keys)
                dve.wait_ge(vmax_ready, STEPS + 1)

            @block.gpsimd
            def _(pool):
                pool.sem_inc(rest_ready, 2)

                def split(m, s, i, more):
                    pool.wait_ge(part0_ready, m + 1)
                    nc.gpsimd.tensor_tensor(rest[s][:, :, :], kq[s][:, :, :], parts[s][:, 0], ALU.subtract).then_inc(rest_ready, 1)
                    pool.wait_ge(part1_ready, m + 1)
                    nc.gpsimd.tensor_tensor(parts[s][:, 2], rest[s][:, :, :], parts[s][:, 1], ALU.subtract).then_inc(part2_ready, 1)
                all_steps(pool, split)

            @block.scalar
            def _(act):
                act.preload_act_table(ACT.Copy)
                act.sem_inc(kT_ready, 2)
                act.sem_inc(v_read, 2)

                def copy_values(m, s):
                    act.wait_ge(kv_psum, m + 1)
                    nc.scalar.activation(v[:, ds(m * KPS, KPS), :], psum_kv(s, 1), ACT.Copy).then_inc(v_read, 1)

                def copy_turned(m, s, i):
                    act.wait_ge(kT_psum, m + 3)
                    act.wait_ge(kT_stored[s], i * 16 + 16)
                    nc.scalar.activation(kT[s][:, :, :], psT[s], ACT.Copy).then_inc(kT_ready, 1)

                def store(m, s):
                    act.wait_ge(kT_ready, m + 3)
                    act.dma_start(g["kT_store"][:, :, ds(m * KEYS, KEYS)], kT[s][:, :, :]).then_inc(kT_stored[s], 16)

                def split(m, s, i, more):
                    act.wait_ge(kq_ready, m + 1)
                    act.wait_ge(kT_psum, m + 1)
                    nc.scalar.activation(parts[s][:, 0], kq[s][:, :, :], ACT.Copy).then_inc(part0_ready, 1)
                    if more or s == 0:
                        copy_values(m + 1, 1 - s)
                    before = not (isinstance(m, int) and m == 0)
                    if before:
                        copy_turned(m - 1, 1 - s, i - 1 + s)
                    act.wait_ge(rest_ready, m + 3)
                    nc.scalar.activation(parts[s][:, 1], rest[s][:, :, :], ACT.Copy).then_inc(part1_ready, 1)
                    if before:
                        store(m - 1, 1 - s)
                for s in range(2):
                    act.sem_inc(kT_stored[s], 16)
                copy_values(0, 0)
                all_steps(act, split)
                copy_turned(STEPS - 1, 1, STEPS // 2 - 1)
                store(STEPS - 1, 1)
                for s in range(2):
                    act.wait_ge(kT_stored[s], 16 * (STEPS // 2 + 1))
                act.wait_ge(v_read, STEPS + 2)

            @block.tensor
            def _(pe):
                pe.wait_ge(w_in, 32)
                pe.sem_inc(kT_psum, 2)

                def project(m, s, i):
                    pe.wait_ge(cT_in[s], i * 16 + 16)
                    pe.wait_ge(k_read, m + 1)
                    pe.wait_ge(v_read, m + 1)
                    for part in range(2):
                        cols = slice(part * D, (part + 1) * D)
                        for j in range(KPS):
                            for k in range(KC):
                                nc.tensor.matmul(psum_kv(s, part)[:, j, :], cT[s][:, k, j * P:(j + 1) * P], wkv[:, k, cols],
                                                 start=(k == 0), stop=False)
                            last = nc.tensor.matmul(psum_kv(s, part)[:, j, :], g["onesb"][0:K_PARTS * 32, :],
                                                    bias_rows[:, cols], start=False, stop=True)
                    last.then_inc(kv_psum, 1)

                def turn(m, s, i, more):
                    if more:
                        project(m + 2, s, i + 1)
                    pe.wait_ge(part2_ready, m + 1)
                    pe.wait_ge(kT_ready, m + 1)
                    for q in range(K_PARTS):
                        for k in range(KC):
                            for j in range(KPS):
                                last = nc.tensor.transpose(psT[s][:, q * KC + k, j * P:(j + 1) * P],
                                                           parts[s][:, q, j, k * P:(k + 1) * P], identb[:, :])
                    last.then_inc(kT_psum, 1)
                pe.wait_ge(bias_ready, K_PARTS)
                for s in range(2):
                    project(s, s, 0)
                all_steps(pe, turn)

PRODUCTS = ((0, 0), (1, 0), (2, 0), (0, 1), (1, 1), (0, 2))
QROWS = len(PRODUCTS) * HD
LOG255 = 5.541263545158426


def xattn1_stage(nc, d, g):
    ctx, sb, banks, sem = scope(nc)
    x, ident, identb = g["x"], g["ident"], g["identb"]
    ROWS = QROWS + K_PARTS
    QT = 4
    QUARTER = NK // QT
    APH = TC * QT
    CPT = 4
    TPH = NKC // CPT
    with ctx:
        wq = sb("d_wq", [P, KC, D])
        wp = sb("d_wp", [P, KC, D])
        bq = sb("d_bq", [P, D])
        bp = sb("d_bp", [P, D])
        xn = sb("d_xn", [P, TC, D])
        xnT = sb("d_xnT", [P, KC, T])
        spent = g["w0_early"][:, :, :].rearrange("p s f -> p (s f)")
        qf, qi, qq, qr = (spent[:, at * TC * D:(at + 1) * TC * D].rearrange("p (t c) -> p t c", t=TC) for at in range(4))
        junk = [spent[:, 4 * TC * D:].bitcast(BF16)[:, f * QUARTER:(f + 1) * QUARTER] for f in range(QT)]
        am = sb("d_absmax", [P, TC * H])
        sc = sb("d_scale", [P, TC * H])
        rs = sb("d_rscale", [P, TC * H])
        qs = sb("d_qs", [P, TC, H, 100], BF16)
        qT = sb("d_qT", [P, H, T], BF16)
        kst = [sb(f"d_kst{s}", [ROWS, NK], BF16) for s in range(2)]
        nm = sb("d_nmax", [P, TC, H, QT])
        zp = sb("d_zpart", [P, TC, H, QT])
        mm = sb("d_mm", [P, TC, H])
        mr = sb("d_mrest", [P, TC, H])
        rz = sb("d_rz", [P, TC, H])
        dm = sb("d_dm", [P, TC, H, QT])
        e = [sb(f"d_e{s}", [P, CPT * T]) for s in range(2)]
        pr = [sb(f"d_probs{s}", [P, CPT * T], BF16) for s in range(4)]
        vall = sb("d_v_absmax", [P, D])
        sv = sb("d_v_scale", [P, D])
        rsv = sb("d_v_rscale", [P, D])
        vhf = [sb(f"d_vh_scaled{s}", [P, NKC, HD]) for s in range(2)]
        vh = [sb(f"d_vh{s}", [P, NKC, HD], BF16) for s in range(2)]
        o = sb("d_o", [P, TC, D])
        oT = sb("d_oT", [P, KC, T])
        ps = banks("d_psum")
        flat = ps[:, :, :].rearrange("p a b -> p (a b)")
        flatb = flat.bitcast(BF16)
        ln = LayerNorm(nc, sb, sem, "d_ln")
        chain = sem("d_dve_chain")
        w_in = sem("d_w_in")
        k_in = [sem(f"d_k_in{s}") for s in range(2)]
        ones_ready = sem("d_ones_ready")
        xn_ready = sem("d_xn_ready")
        xnT_psum = sem("d_xnT_psum")
        xnT_ready = sem("d_xnT_ready")
        q_psum = sem("d_q_psum")
        qs_ready = sem("d_qs_ready")
        qT_psum = sem("d_qT_psum")
        qT_ready = sem("d_qT_ready")
        sA_ready = sem("d_sA_ready")
        nm_ready = sem("d_nm_ready")
        zp_ready = sem("d_zp_ready")
        dm_ready = sem("d_dm_ready")
        de_ready = sem("d_de_ready")
        sB_ready = sem("d_sB_ready")
        e_ready = sem("d_e_ready")
        p_ready = sem("d_p_ready")
        av_done = sem("d_av_done")
        vall_ready = sem("d_vall_ready")
        rsv_ready = sem("d_rsv_ready")
        vhf_ready = sem("d_vhf_ready")
        vh_ready = sem("d_vh_ready")
        o_ready = sem("d_o_ready")
        oT_psum = sem("d_oT_psum")
        oT_ready = sem("d_oT_ready")
        out_psum = sem("d_out_psum")

        def heads(eng, body):
            with eng.Fori(0, H // 2 - 1) as i:
                for s in range(2):
                    body(i * 2 + s, s, i, True)
            for s in range(2):
                body(H - 2 + s, s, H // 2 - 1, False)

        def transpose_q(pe, rows):
            for hd in range(H):
                for t in range(TC):
                    q = hd * TC + t
                    last = nc.tensor.transpose(flatb[0:rows, q * P:(q + 1) * P], qs[:, t, hd, 0:rows], identb[:, :])
            return last

        with nc.Block() as block:
            @block.sync
            def _(sp):
                for dst, name in ((wq, "wq"), (wp, "wp"), (bq, "bq"), (bp, "bp")):
                    sp.dma_start(dst[:], d[name]).then_inc(w_in, 16)

                def load_keys(row, s):
                    for j, (_, part) in enumerate(PRODUCTS):
                        sp.dma_start(kst[s][j * HD:(j + 1) * HD, :], d["kT_scratch"][ds(row + part * D, HD), :])\
                          .then_inc(k_in[s], 16)
                for s in range(2):
                    load_keys(s * HD, s)
                sp.dma_start(g["shared1"][:, :], d["shared1"]).then_inc(g["shared_in"][1], 16)
                for q in range(NG1):
                    sp.dma_start(g["w1"][:, q, :], d["w1"][q]).then_inc(g["w1_in"], 16)

                def refill_a(m, s, i, more):
                    if more:
                        rows = [sp.snap(m * HD + (2 * HD + part * D)) for part in range(K_PARTS)]
                    sp.wait_ge(sA_ready, m * APH + APH)
                    for j, (_, part) in enumerate(PRODUCTS):
                        row = rows[part] if more else s * HD + part * D
                        sp.dma_start(kst[s][j * HD:(j + 1) * HD, :], d["kT_scratch"][ds(row, HD), :]).then_inc(k_in[s], 16)
                heads(sp, refill_a)

                def refill_b(m, s, i, more):
                    if more:
                        rows = [sp.snap(m * HD + (2 * HD + part * D)) for part in range(K_PARTS)]
                        sp.wait_ge(sB_ready, m * TPH + TPH)
                        for j, (_, part) in enumerate(PRODUCTS):
                            sp.dma_start(kst[s][j * HD:(j + 1) * HD, :], d["kT_scratch"][ds(rows[part], HD), :])\
                              .then_inc(k_in[s], 16)
                heads(sp, refill_b)

            @block.gpsimd
            def _(pool):
                for s in range(2):
                    nc.gpsimd.memset(kst[s][QROWS:ROWS, :], 1.0).then_inc(ones_ready, 1)
                pool.wait_ge(ones_ready, 2)
                nc.gpsimd.partition_all_reduce(vall[:, :], g["vam"][:, :], P, RMAX).then_inc(vall_ready, 1)
                pool.wait_ge(rsv_ready, 1)
                for s in range(2):
                    nc.gpsimd.tensor_tensor(vhf[s][:, :, :], g["v"][:, :, s * HD:(s + 1) * HD],
                                            rsv[:, s * HD:(s + 1) * HD].unsqueeze(1).to_broadcast([P, NKC, HD]),
                                            ALU.mult).then_inc(vhf_ready, 1)

                def scale_values(m, s, i, more):
                    if more:
                        at = pool.snap(m * HD + 2 * HD)
                        pool.wait_ge(vh_ready, m + 1)
                        nc.gpsimd.tensor_tensor(vhf[s][:, :, :], g["v"][:, :, ds(at, HD)],
                                                rsv[:, ds(at, HD)].unsqueeze(1).to_broadcast([P, NKC, HD]),
                                                ALU.mult).then_inc(vhf_ready, 1)
                heads(pool, scale_values)

            @block.vector
            def _(dve):
                step = Steps(dve, chain)
                ln.vector(dve, step, xn, x)
                nc.vector.tensor_copy(ln.std[:, :], ln.rstd[:, :]).then_inc(xn_ready, 1)
                dve.wait_ge(w_in, 64)
                dve.wait_ge(q_psum, 1)
                q_psum_v = ps[:, 1, :].rearrange("p (t c) -> p t c", t=TC)
                step(nc.vector.tensor_tensor(qf[:, :, :], q_psum_v, bq[:, :].unsqueeze(1).to_broadcast([P, TC, D]), ALU.add))
                step(nc.vector.tensor_scalar(qf[:, :, :], qf[:, :, :], HD ** -0.5, None, ALU.mult))
                f3, i3, q3, r3 = (a[:, :, :].rearrange("p t (h e) -> p (t h) e", e=HD) for a in (qf, qi, qq, qr))
                step(quantize(nc, step, q3, i3, f3, sc[:, :], rs[:, :], am[:, :], [P, TC * H, HD]))

                def part_to(src, part):
                    for j, (pq, _) in enumerate(PRODUCTS):
                        if pq == part:
                            step(nc.vector.tensor_copy(qs[:, :, :, j * HD:(j + 1) * HD].rearrange("p t h e -> p (t h) e"), src))
                            first = qs[:, :, :, j * HD:(j + 1) * HD].rearrange("p t h e -> p (t h) e")
                    return first
                p0 = part_to(q3, 0)
                step(nc.vector.tensor_tensor(r3, q3, p0, ALU.subtract))
                p1 = part_to(r3, 1)
                step(nc.vector.tensor_tensor(q3, r3, p1, ALU.subtract))
                part_to(q3, 2)
                nc.vector.tensor_copy(ln.std[:, :], ln.rstd[:, :]).then_inc(qs_ready, 1)

                dve.wait_ge(vall_ready, 1)
                step(nc.vector.tensor_scalar(sv[:, :], vall[:, :], 1.0 / 127.0, 1e-8, ALU.mult, ALU.max))
                nc.vector.reciprocal(rsv[:, :], sv[:, :]).then_inc(rsv_ready, 1)

                def search(m, s, i, more):
                    for t in range(TC):
                        for f in range(QT):
                            dve.wait_ge(sA_ready, m * APH + (QT * t + f + 1))
                            nc.vector.tensor_reduce(nm[:, t, ds(m, 1), f:f + 1], flat[:, f * QUARTER:(f + 1) * QUARTER].unsqueeze(1),
                                                    AX.X, ALU.max, negate=True).then_inc(nm_ready, 1)
                heads(dve, search)
                dve.wait_ge(nm_ready, APH * H)
                step(nc.vector.tensor_reduce(mm[:, :, :], nm[:, :, :, :], AX.X, ALU.min))
                nc.vector.tensor_tensor(dm[:, :, :, :], mm[:, :, :].unsqueeze(3).to_broadcast([P, TC, H, QT]), nm[:, :, :, :],
                                        ALU.subtract).then_inc(dm_ready, 1)
                dve.wait_ge(dm_ready, 1)
                step(nc.vector.tensor_scalar(mm[:, :, :], mm[:, :, :], LOG255, None, ALU.add))
                for q in range(K_PARTS):
                    step(nc.vector.tensor_copy(qs[:, :, :, QROWS + q], mm[:, :, :]))
                    if q < K_PARTS - 1:
                        step(nc.vector.tensor_tensor(mr[:, :, :], mm[:, :, :], qs[:, :, :, QROWS + q], ALU.subtract))
                        step(nc.vector.tensor_copy(mm[:, :, :], mr[:, :, :]))
                nc.vector.tensor_copy(ln.std[:, :], ln.rstd[:, :]).then_inc(qs_ready, 1)
                dve.wait_ge(de_ready, 1)
                dve.wait_ge(zp_ready, APH * H + QT)
                step(nc.vector.tensor_tensor(zp[:, :, :, :], zp[:, :, :, :], dm[:, :, :, :], ALU.mult))
                step(nc.vector.tensor_reduce(rz[:, :, :], zp[:, :, :, :], AX.X, ALU.add))
                step(nc.vector.tensor_scalar(rz[:, :, :], rz[:, :, :], 255.0, None, ALU.mult))
                step(nc.vector.reciprocal(rz[:, :, :], rz[:, :, :]))
                dve.sem_inc(p_ready, 2)

                def round_values(m, s):
                    dve.wait_ge(vhf_ready, m + 1)
                    nc.vector.tensor_scalar(vh[s][:, :, :], vhf[s][:, :, :], ROUND, ROUND, ALU.add, ALU.subtract)\
                      .then_inc(vh_ready, 1)
                for s in range(2):
                    round_values(s, s)

                def rounds(m, s, i, more):
                    for u in range(TPH):
                        b = m * TPH + u
                        dve.wait_ge(e_ready, b + 1)
                        dve.wait_ge(av_done, b + 1)
                        nc.vector.tensor_scalar(pr[u % 4][:, :], e[u % 2][:, :], ROUND, ROUND, ALU.add,
                                                ALU.subtract).then_inc(p_ready, 1)
                    dve.wait_ge(av_done, m * TPH + (TPH + 4))
                    nc.vector.tensor_tensor(o[:, :, ds(m * HD, HD)], ps[:, 4 + 2 * s:6 + 2 * s, 0:HD],
                                            rz[:, :, ds(m, 1)].to_broadcast([P, TC, HD]), ALU.mult).then_inc(o_ready, 1)
                    if more:
                        round_values(m + 2, s)
                heads(dve, rounds)
                dve.wait_ge(o_ready, H)
                nc.vector.tensor_tensor(o[:, :, :], o[:, :, :], sv[:, :].unsqueeze(1).to_broadcast([P, TC, D]),
                                        ALU.mult).then_inc(o_ready, 1)
                step(nc.vector.tensor_tensor(x[:, :, :], x[:, :, :], bp[:, :].unsqueeze(1).to_broadcast([P, TC, D]), ALU.add))
                dve.wait_ge(out_psum, 1)
                step(nc.vector.tensor_tensor(x[:, :, :], x[:, :, :], ps[:, 1, :].rearrange("p (t c) -> p t c", t=TC), ALU.add))

            @block.scalar
            def _(act):
                ln.scalar(act)
                act.wait_ge(xnT_psum, 1)
                nc.scalar.activation(xnT[:, :, :], ps[:, 0, :].rearrange("p (k t) -> p k t", k=KC),
                                     ACT.Copy).then_inc(xnT_ready, 1)
                act.preload_act_table(ACT.Exp)
                act.wait_ge(qT_psum, 1)
                nc.scalar.activation(qT[0:QROWS, :, :], flatb[0:QROWS, 0:H * T].rearrange("p (h t) -> p h t", h=H),
                                     ACT.Copy).then_inc(qT_ready, 1)
                act.sem_inc(zp_ready, QT)

                def sums(m, s, i, more):
                    for t in range(TC):
                        for f in range(QT):
                            act.wait_ge(nm_ready, m * APH + (QT * t + f + 1))
                            act.wait_ge(zp_ready, m * APH + (QT * t + f + 1))
                            nc.scalar.activation(junk[f].unsqueeze(1), flat[:, f * QUARTER:(f + 1) * QUARTER].unsqueeze(1), ACT.Exp,
                                                 bias=nm[:, t, ds(m, 1), f], accum_out=zp[:, t, ds(m, 1), f])\
                              .then_inc(zp_ready, 1)
                heads(act, sums)
                act.wait_ge(dm_ready, 1)
                nc.scalar.activation(dm[:, :, :, :], dm[:, :, :, :], ACT.Exp).then_inc(de_ready, 1)
                act.wait_ge(qT_psum, 2)
                nc.scalar.activation(qT[0:ROWS, :, :], flatb[0:ROWS, 0:H * T].rearrange("p (h t) -> p h t", h=H),
                                     ACT.Copy).then_inc(qT_ready, 1)

                def exps(m, s, i, more):
                    for u in range(TPH):
                        b = m * TPH + u
                        act.wait_ge(sB_ready, b + 1)
                        act.wait_ge(p_ready, b + 1)
                        nc.scalar.activation(e[u % 2][:, :], flat[:, (u % 2) * CPT * T:(u % 2 + 1) * CPT * T],
                                             ACT.Exp).then_inc(e_ready, 1)
                heads(act, exps)
                act.wait_ge(oT_psum, 1)
                nc.scalar.activation(oT[:, :, :], ps[:, 0, :].rearrange("p (k t) -> p k t", k=KC),
                                     ACT.Copy).then_inc(oT_ready, 1)

            @block.tensor
            def _(pe):
                pe.wait_ge(xn_ready, 1)
                transpose_tokens(nc, ps[:, 0, :], xn, ident).then_inc(xnT_psum, 1)
                pe.wait_ge(xnT_ready, 1)
                pe.wait_ge(w_in, 64)
                for t in range(TC):
                    for k in range(KC):
                        last = nc.tensor.matmul(ps[:, 1, t * D:(t + 1) * D], xnT[:, k, t * P:(t + 1) * P], wq[:, k, :],
                                                start=(k == 0), stop=(k == KC - 1))
                last.then_inc(q_psum, 1)
                pe.wait_ge(qs_ready, 1)
                transpose_q(pe, QROWS).then_inc(qT_psum, 1)
                keep_warm(nc, g, ps[:, 7, :], 12)
                pe.wait_ge(qT_ready, 1)

                def scores_a(m, s, i, more):
                    pe.wait_ge(k_in[s], i * 96 + 96)
                    for t in range(TC):
                        for f in range(QT):
                            pe.wait_ge(zp_ready, m * APH + (QT * t + f + 1))
                            for c in range(QUARTER // 512):
                                at = f * QUARTER + c * 512
                                last = nc.tensor.matmul(flat[:, at:at + 512], qT[0:QROWS, ds(m, 1), t * P:(t + 1) * P],
                                                        kst[s][0:QROWS, at:at + 512], start=True, stop=True)
                            last.then_inc(sA_ready, 1)
                heads(pe, scores_a)
                pe.wait_ge(qs_ready, 2)
                pe.wait_ge(zp_ready, APH * H + QT)
                transpose_q(pe, ROWS).then_inc(qT_psum, 1)
                keep_warm(nc, g, ps[:, 7, :], 12)
                pe.wait_ge(qT_ready, 2)
                pe.wait_ge(ones_ready, 2)
                pe.sem_inc(av_done, 4)

                def tile_b(m, s, u):
                    for c in range(CPT):
                        key = (u * CPT + c) * P
                        last = nc.tensor.matmul(flat[:, (u % 2) * CPT * T + c * T:(u % 2) * CPT * T + (c + 1) * T],
                                                kst[s][0:ROWS, key:key + P], qT[0:ROWS, ds(m, 1), :], start=True, stop=True)
                    last.then_inc(sB_ready, 1)

                def values_b(m, s, u):
                    pe.wait_ge(p_ready, m * TPH + (u + 3))
                    if u == 0:
                        pe.wait_ge(vh_ready, m + 1)
                    for c in range(CPT):
                        for t in range(TC):
                            last = nc.tensor.matmul(ps[:, 4 + 2 * s + t, 0:HD], pr[u % 4][:, c * T + t * P:c * T + (t + 1) * P],
                                                    vh[s][:, u * CPT + c, :], start=(u == 0 and c == 0),
                                                    stop=(u == TPH - 1 and c == CPT - 1))
                    last.then_inc(av_done, 1)
                    keep_warm(nc, g, ps[:, 6 - 2 * s, :], 1)

                def head_b(m, s, i, more):
                    for u in range(TPH):
                        b = m * TPH + u
                        if u + 2 < TPH or more or s == 0:
                            pe.wait_ge(e_ready, b + 1)
                            if u + 2 < TPH:
                                tile_b(m, s, u + 2)
                            else:
                                if u + 2 == TPH:
                                    pe.wait_ge(k_in[1 - s], i * 96 + 96 * (H // 2 + 1 + s))
                                tile_b(m + 1, 1 - s, u + 2 - TPH)
                        if u > 0:
                            values_b(m, s, u - 1)
                    values_b(m, s, TPH - 1)
                pe.wait_ge(k_in[0], 96 * (H // 2 + 1))
                tile_b(0, 0, 0)
                tile_b(0, 0, 1)
                heads(pe, head_b)
                pe.wait_ge(o_ready, H + 1)
                transpose_tokens(nc, ps[:, 0, :], o, ident).then_inc(oT_psum, 1)
                pe.wait_ge(oT_ready, 1)
                for t in range(TC):
                    for k in range(KC):
                        last = nc.tensor.matmul(ps[:, 1, t * D:(t + 1) * D], oT[:, k, t * P:(t + 1) * P], wp[:, k, :],
                                                start=(k == 0), stop=(k == KC - 1))
                last.then_inc(out_psum, 1)

def rms_norm(nc, dve, step, out, in_, sq, ss, var_ready, std_ready, count):
    for t in range(TC):
        step(nc.vector.tensor_tensor(sq[:, t, :], in_[:, t, :], in_[:, t, :], ALU.mult))
    nc.vector.tensor_reduce(ss[:, :, 0], sq[:, :, :], AX.X, ALU.add).then_inc(var_ready, 1)
    dve.wait_ge(std_ready, count)
    step(nc.vector.tensor_scalar(ss[:, :, 1], ss[:, :, 1], 1e-12, None, ALU.max))
    step(nc.vector.reciprocal(ss[:, :, 1], ss[:, :, 1]))
    step(nc.vector.tensor_scalar(ss[:, :, 1], ss[:, :, 1], D ** 0.5, None, ALU.mult))
    step(nc.vector.tensor_tensor(out[:, :, :], in_[:, :, :], ss[:, :, 1:2].to_broadcast([P, TC, D]), ALU.mult))


def conv_stage(nc, d, g):
    ctx, sb, banks, sem = scope(nc)
    x, ident = g["x"], g["ident"]
    EC = INNER // P
    MC = MLP // P
    with ctx:
        w_in = sb("e_w_inT", [P, KC, 2 * INNER])
        w_out = sb("e_w_outT", [P, EC, D])
        mlp1 = sb("e_mlp1T", [P, KC, MLP])
        mlp2 = sb("e_mlp2T", [P, MC, D])
        conv = sb("e_conv", [P, EC, CONV + 1])
        y = sb("e_y", [P, TC, D])
        y1 = sb("e_y1", [P, TC, D])
        hn = sb("e_hn", [P, TC, D])
        sq = sb("e_sq", [P, TC, D])
        ss = sb("e_ss", [P, TC, 2])
        hT = sb("e_hT", [P, KC, T])
        h2T = sb("e_h2T", [P, KC, T])
        xc = sb("e_xc", [P, EC, T])
        sx = sb("e_sx", [P, EC, T])
        sz = sb("e_sz", [P, EC, T])
        gy = sb("e_gated", [P, EC, T])
        mh = sb("e_mlp_hidden", [P, MC, T])
        ps = banks("e_psum")
        ln = LayerNorm(nc, sb, sem, "e_ln")
        chain = sem("e_dve_chain")
        weights_in = sem("e_weights_in")
        ss_ready = sem("e_ss_ready")
        root_ready = sem("e_root_ready")
        hn_ready = sem("e_hn_ready")
        hT_psum = sem("e_hT_psum")
        hT_ready = sem("e_hT_ready")
        xz_psum = sem("e_xz_psum")
        xc_ready = sem("e_xc_ready")
        sx_ready = sem("e_sx_ready")
        sz_ready = sem("e_sz_ready")
        gy_ready = sem("e_gy_ready")
        out_psum = sem("e_out_psum")
        m_psum = sem("e_m_psum")
        mh_ready = sem("e_mh_ready")
        mlp_psum = sem("e_mlp_psum")

        def xz(c):
            return ps[:, c // 2, (c % 2) * T:(c % 2 + 1) * T]

        with nc.Block() as block:
            @block.sync
            def _(sp):
                for dst, name in ((w_in, "w_inT"), (w_out, "w_outT"), (mlp1, "mlp1T"), (mlp2, "mlp2T"), (conv, "conv")):
                    sp.dma_start(dst[:], d[name]).then_inc(weights_in, 16)

            @block.vector
            def _(dve):
                step = Steps(dve, chain)
                ln.vector(dve, step, y, x)
                rms_norm(nc, dve, step, hn, y, sq, ss, ss_ready, root_ready, 1)
                nc.vector.tensor_copy(ln.std[:, :], ln.rstd[:, :]).then_inc(hn_ready, 1)
                dve.wait_ge(weights_in, 80)
                dve.wait_ge(xz_psum, 1)
                for c in range(EC):
                    step(nc.vector.tensor_scalar(xc[:, c, :], xz(c), conv[:, c, CONV - 1:CONV], conv[:, c, CONV:CONV + 1],
                                                 ALU.mult, ALU.add))
                    acc = xc[:, c, :].rearrange("p (b l) -> p b l", l=L)
                    src = xz(c).rearrange("p (b l) -> p b l", l=L)
                    for j in range(1, CONV):
                        ins = nc.vector.scalar_tensor_tensor(acc[:, :, j:L], src[:, :, 0:L - j],
                                                             conv[:, c, CONV - 1 - j:CONV - j], acc[:, :, j:L],
                                                             ALU.mult, ALU.add)
                        if j < CONV - 1:
                            step(ins)
                    ins.then_inc(xc_ready, 1)
                for c in range(EC):
                    dve.wait_ge(sx_ready, c + 1)
                    dve.wait_ge(sz_ready, EC // 2)
                    nc.vector.tensor_tensor(gy[:, c, :], sx[:, c, :], sz[:, c, :], ALU.mult).then_inc(gy_ready, 1)
                dve.wait_ge(out_psum, 1)
                step(nc.vector.tensor_tensor(y1[:, :, :], y[:, :, :], ps[:, 4, :].rearrange("p (t c) -> p t c", t=TC), ALU.add))
                rms_norm(nc, dve, step, hn, y1, sq, ss, ss_ready, root_ready, 2)
                nc.vector.tensor_copy(ln.std[:, :], ln.rstd[:, :]).then_inc(hn_ready, 1)
                step(nc.vector.tensor_tensor(x[:, :, :], x[:, :, :], y1[:, :, :], ALU.add))
                for c in range(MC // 2):
                    dve.wait_ge(m_psum, c + 1)
                    nc.vector.tensor_scalar(mh[:, 2 * c:2 * c + 2, :], ps[:, c, :].rearrange("p (c t) -> p c t", c=2), 0.0,
                                            None, ALU.max).then_inc(mh_ready, 1)
                dve.wait_ge(mlp_psum, 1)
                step(nc.vector.tensor_tensor(x[:, :, :], x[:, :, :], ps[:, 5, :].rearrange("p (t c) -> p t c", t=TC), ALU.add))

            @block.scalar
            def _(act):
                def root(count):
                    act.wait_ge(ss_ready, count)
                    nc.scalar.activation(ss[:, :, 1], ss[:, :, 0], ACT.Sqrt).then_inc(root_ready, 1)

                def copy_hT(dst, count):
                    act.wait_ge(hT_psum, count)
                    nc.scalar.activation(dst[:, :, :], ps[:, 6 + count - 1, :].rearrange("p (k t) -> p k t", k=KC),
                                         ACT.Copy).then_inc(hT_ready, 1)
                ln.scalar(act)
                root(1)
                copy_hT(hT, 1)
                act.wait_ge(xz_psum, 2)
                for c in range(EC // 2):
                    nc.scalar.activation(sz[:, 2 * c:2 * c + 2, :], ps[:, 2 + c, :].rearrange("p (c t) -> p c t", c=2),
                                         ACT.Silu).then_inc(sz_ready, 1)
                for c in range(EC):
                    act.wait_ge(xc_ready, c + 1)
                    nc.scalar.activation(sx[:, c, :], xc[:, c, :], ACT.Silu).then_inc(sx_ready, 1)
                root(2)
                copy_hT(h2T, 2)

            @block.tensor
            def _(pe):
                pe.wait_ge(hn_ready, 1)
                transpose_tokens(nc, ps[:, 6, :], hn, ident).then_inc(hT_psum, 1)
                pe.wait_ge(hT_ready, 1)
                pe.wait_ge(weights_in, 80)
                for c in range(2 * EC):
                    for k in range(KC):
                        last = nc.tensor.matmul(xz(c), w_in[:, k, c * P:(c + 1) * P], hT[:, k, :], start=(k == 0),
                                                stop=(k == KC - 1))
                    if c % EC == EC - 1:
                        last.then_inc(xz_psum, 1)
                pe.wait_ge(gy_ready, EC)
                for t in range(TC):
                    for c in range(EC):
                        last = nc.tensor.matmul(ps[:, 4, t * D:(t + 1) * D], gy[:, c, t * P:(t + 1) * P], w_out[:, c, :],
                                                start=(c == 0), stop=(c == EC - 1))
                last.then_inc(out_psum, 1)
                pe.wait_ge(hn_ready, 2)
                transpose_tokens(nc, ps[:, 7, :], hn, ident).then_inc(hT_psum, 1)
                pe.wait_ge(hT_ready, 2)
                for c in range(MC):
                    for k in range(KC):
                        last = nc.tensor.matmul(xz(c), mlp1[:, k, c * P:(c + 1) * P], h2T[:, k, :], start=(k == 0),
                                                stop=(k == KC - 1))
                    if c % 2:
                        last.then_inc(m_psum, 1)
                pe.wait_ge(mh_ready, MC // 2)
                for t in range(TC):
                    for c in range(MC):
                        last = nc.tensor.matmul(ps[:, 5, t * D:(t + 1) * D], mh[:, c, t * P:(t + 1) * P], mlp2[:, c, :],
                                                start=(c == 0), stop=(c == MC - 1))
                last.then_inc(mlp_psum, 1)
def store_stage(nc, d, g):
    ctx, sb, banks, sem = scope(nc)
    with ctx:
        out_done = sem("out_done")
        with nc.Block() as block:
            @block.sync
            def _(sp):
                sp.dma_start(d["out"].rearrange("(t p) c -> p t c", p=P), g["x"][:, :, :]).then_inc(out_done, 16)
                sp.wait_ge(out_done, 16)




def build(nc, d):
    ctx, sb, banks, sem = scope(nc)
    g = {}
    with ctx:
        setup_stage(nc, d, g, sb, sem)
        d["kT_scratch"] = d["kT_scratch"].rearrange("q c n -> (q c) n")
        g["kT_store"] = d["kT_scratch"].rearrange("(a p) n -> p a n", p=P)
        stages = [xattn0_stage, scan_stage, lambda *a: moe_stage(*a, MOE0), kv_stage, xattn1_stage, conv_stage, lambda *a: moe_stage(*a, MOE1)]
        for stage in stages:
            if stage is kv_stage:
                layer1_memory(nc, d, g, sb, sem)
            stage(nc, d, g)
        store_stage(nc, d, g)


def kernel(**inputs):
    import numpy as np
    import concourse.bacc as bacc
    from concourse.bass_utils import run_bass_kernel_spmd

    def rows(a):
        return np.ascontiguousarray(np.broadcast_to(a.reshape(1, -1), (P, a.size)))

    def chunks(a):
        return np.ascontiguousarray(a.reshape(-1, P, a.shape[-1]).transpose(1, 0, 2))

    i = {k: np.asarray(v) for k, v in inputs.items()}
    ctxt = i["ctx_2048"].reshape(NK, D)
    mask = np.pad(i["mask_BxS2_bk0"].view(np.uint8)[..., None], ((0, 0), (0, 0), (0, 3))).view(np.int32)
    mask = mask.reshape(TC, B // TC, 1, S)
    arrays = {
        "x": np.ascontiguousarray(i["x"].reshape(T, D)),
        "ctx": chunks(ctxt),
        "ctxT": chunks(np.ascontiguousarray(ctxt.T)),
        "mask": np.ascontiguousarray(np.broadcast_to(mask, (TC, B // TC, L, S)).reshape(TC, P, S).transpose(1, 0, 2)),
    }
    def by_channel(*rows_):
        return np.ascontiguousarray(np.stack([r.reshape(KC, P) for r in rows_]).transpose(2, 0, 1))

    arrays |= {
        "xprojT": chunks(np.ascontiguousarray(i["L0_attn_x_proj_w"].T)),
        "dtwT": np.ascontiguousarray(i["L0_attn_dt_proj_w"].T),
        "outwT": chunks(np.ascontiguousarray(i["L0_attn_out_proj_w"].T)),
        "cols0": by_channel(i["L0_attn_norm_w"], i["L0_attn_norm_b"], i["L0_attn_dt_proj_b"], i["L0_attn_D_param"]),
        "A_log": chunks(i["L0_attn_A_log"]),
    }
    def groups(name, experts, per, f):
        n = experts // per
        gate, up = (i[name + w].reshape(n, per, KC, P, f).transpose(0, 3, 2, 1, 4).reshape(n, P, KC * per * f)
                    for w in ("gate", "up"))
        down = i[name + "down"].reshape(n, per * f, D)
        rows_ = -(-per * f // P) * P
        down = np.concatenate([down, np.zeros((n, rows_ - per * f, D), down.dtype)], axis=1)
        down = down.reshape(n, rows_ // P, P, D).transpose(0, 2, 1, 3).reshape(n, P, -1)
        return np.ascontiguousarray(np.concatenate([gate, up, down], axis=2))

    def shared(name):
        f = i[name + "gate"].shape[1]
        one = {name + w: i[name + w][None] for w in ("gate", "up", "down")}
        i.update(one)
        return groups(name, 1, 1, f)[0]

    arrays |= {
        "w_inT": chunks(np.ascontiguousarray(i["L1_attn_W_in"].T)),
        "w_outT": chunks(np.ascontiguousarray(i["L1_attn_W_out"].T)),
        "mlp1T": chunks(np.ascontiguousarray(i["L1_attn_W_mlp1"].T)),
        "mlp2T": chunks(np.ascontiguousarray(i["L1_attn_W_mlp2"].T)),
        "conv": chunks(np.ascontiguousarray(np.concatenate([i["L1_attn_conv_w"].reshape(INNER, CONV),
                                                            i["L1_attn_conv_b"].reshape(INNER, 1)], axis=1))),
        "gatef": chunks(np.ascontiguousarray(i["L1_ffn_gate_weight"].T)),
        "wq": chunks(i["L1_xattn_Wq"]),
        "bq": rows(i["L1_xattn_bq"]),
        "wp": chunks(i["L1_xattn_Wp"]),
        "bp": rows(i["L1_xattn_bp"]),
        "w1": groups("L1_ffn_w_", E1, EPG1, F1),
        "shared1": shared("L1_ffn_ws_"),
        "wkv": chunks(i["L1_xattn_Wkv"]),
        "bkv": rows(i["L1_xattn_bkv"]),
        "w0": groups("L0_ffn_w_", E0, EPG0, F0),
        "shared0": shared("L0_ffn_ws_"),
        "gatec": chunks(i["L0_ffn_gate_w"]),
        "bias0": rows(i["L0_ffn_bias"]),
    }
    nc = bacc.Bacc("TRN2", target_bir_lowering=False, num_devices=1)
    d = {n: nc.dram_tensor(f"in_{n}", a.shape, mybir.dt.from_np(a.dtype), kind="ExternalInput").ap()
         for n, a in arrays.items()}
    d["out"] = nc.dram_tensor("out", (T, D), F32, kind="ExternalOutput").ap()
    d["c_scratch"] = nc.dram_tensor("c_scratch", (N, T), F32).ap()
    d["kT_scratch"] = nc.dram_tensor("kT_scratch", (3, D, NK), BF16).ap()
    build(nc, d)
    r = run_bass_kernel_spmd(nc, [{f"in_{n}": a for n, a in arrays.items()}], core_ids=[0])
    return r.results[0]["out"].reshape(B, L, D)
```

```python
import concourse.bass as bass
from concourse import mybir
from contextlib import ExitStack

F32 = mybir.dt.float32
BF16 = mybir.dt.bfloat16
I32 = mybir.dt.int32
ALU = mybir.AluOpType
ACT = mybir.ActivationFunctionType
AX = mybir.AxisListType
ds = bass.ds

P = 128
B, L, D = 8, 32, 256
T = B * L
TC = T // P
KC = D // P
S = 512
NK = B * S
NKC = NK // P
LN_EPS = 1e-5
NEG = 1e30
ROUND = 12582912.0

N = 64
RANK = 128

E0, K0, F0 = 64, 6, 96
G0, KG0 = 8, 4
CAP0 = 2 * (T * K0 // E0)
SCALE0 = 2.5
EPG0 = 4
W0 = EPG0 * F0
NG0 = E0 // EPG0

E1, K1, F1 = 16, 4, 176
EPG1 = 2
W1 = EPG1 * F1
NG1 = E1 // EPG1
DC = 3
SLOT0 = 2 * KC * W0 + DC * D
SLOT1 = 2 * KC * W1 + DC * D
SHARED0 = 2 * KC * F0 + D

RMAX = bass.bass_isa.ReduceOp.absmax
H, HD = 16, 16
INNER = 512
CONV = 4
MLP = 4 * D


class Steps:

    def __init__(self, eng, sem):
        self.eng, self.sem, self.n = eng, sem, 0

    def __call__(self, ins):
        self.n += 1
        ins.then_inc(self.sem, 1)
        self.eng.wait_ge(self.sem, self.n)


class LayerNorm:

    def __init__(self, nc, sb, sem, name):
        self.nc = nc
        self.stats = sb(name + "_stats", [P, TC, 6], F32)
        self.mv = sb(name + "_mean_var", [P, TC, 2], F32)
        self.ve = sb(name + "_var_eps", [P, TC], F32)
        self.std = sb(name + "_std", [P, TC], F32)
        self.rstd = sb(name + "_rstd", [P, TC], F32)
        self.var_ready = sem(name + "_var_ready")
        self.std_ready = sem(name + "_std_ready")

    def vector(self, dve, step, out, in_, done=None, each=None):
        nc = self.nc
        for t in range(TC):
            last = nc.vector.bn_stats(self.stats[:, t, :], in_[:, t, :])
        step(last)
        for t in range(TC):
            last = nc.vector.bn_aggr(self.mv[:, t, :], self.stats[:, t, :])
        step(last)
        nc.vector.tensor_scalar(self.ve[:, :], self.mv[:, :, 1], LN_EPS, None, ALU.add).then_inc(self.var_ready, 1)
        dve.wait_ge(self.std_ready, 1)
        step(nc.vector.reciprocal(self.rstd[:, :], self.std[:, :]))
        step(nc.vector.scalar_tensor_tensor(self.std[:, :], self.ve[:, :], -0.5, self.rstd[:, :], ALU.mult, ALU.mult))
        step(nc.vector.tensor_tensor(self.std[:, :], self.std[:, :], self.rstd[:, :], ALU.mult))
        step(nc.vector.scalar_tensor_tensor(self.rstd[:, :], self.std[:, :], 1.5, self.rstd[:, :], ALU.add, ALU.mult))
        for t in range(TC):
            last = nc.vector.tensor_scalar(out[:, t, :], in_[:, t, :], self.mv[:, t, 0:1], self.rstd[:, t:t + 1],
                                           ALU.subtract, ALU.mult)
            if each is not None:
                last.then_inc(each, 1)
        if each is not None:
            return
        if done is None:
            step(last)
        else:
            last.then_inc(done, 1)

    def scalar(self, act):
        act.wait_ge(self.var_ready, 1)
        self.nc.scalar.activation(self.std[:, :], self.ve[:, :], ACT.Sqrt).then_inc(self.std_ready, 1)


def transpose_tokens(nc, psum_bank, src, ident):
    out = psum_bank.rearrange("p (k t) -> p k t", k=KC)
    for t in range(TC):
        for k in range(KC):
            last = nc.tensor.transpose(out[:, k, t * P:(t + 1) * P], src[:, t, k * P:(k + 1) * P], ident[:, :])
    return last


def keep_warm(nc, g, bank, count, width=4):
    moving = g["onesb"][:, :].unsqueeze(1).to_broadcast([P, width, P])
    for _ in range(count):
        nc.tensor.matmul(bank[:, 0:width * P].rearrange("p (a b) -> p a b", a=width), g["identb"][:, :], moving,
                         start=True, stop=True)


def scope(nc):
    ctx = ExitStack()

    def sb(name, shape, dt=F32):
        return ctx.enter_context(nc.sbuf_tensor(name, shape, dt))

    def banks(name):
        return ctx.enter_context(nc.psum_tensor(name, [P, 8, 512], F32))

    def sem(name):
        return ctx.enter_context(nc.semaphore(name))

    return ctx, sb, banks, sem



def setup_stage(nc, d, g, sb, sem):
    g["x"] = sb("x_residual", [P, TC, D])
    g["ident"] = sb("ident", [P, P])
    g["identb"] = sb("ident_bf16", [P, P], BF16)
    g["ones"] = sb("ones", [P, P])
    g["onesb"] = sb("ones_bf16", [P, P], BF16)
    g["before"] = sb("before_bf16", [P, P], BF16)
    g["zeros"] = sb("zeros", [P, P])
    g["w0_early"] = sb("w0_early", [P, 2, SLOT0])
    g["shared0"] = sb("shared0", [P, SHARED0])
    g["w0_in"] = [sem(f"w0_in{s}") for s in range(4)]
    g["shared_in"] = [sem(f"shared_in{s}") for s in range(2)]
    g["const_sem"] = sem("constants_ready")
    g["x_in"] = sem("x_in")



def xattn0_stage(nc, d, g):
    ctx, sb, banks, sem = scope(nc)
    x, ident, identb = g["x"], g["ident"], g["identb"]
    with ctx:
        ctxT = sb("a_ctxT", [P, KC, NK])
        ctxk = sb("a_ctx", [P, NKC, D])
        mask_i = sb("a_mask_i", [P, TC, S], I32)
        mask = sb("a_mask", [P, TC, S])
        negm = sb("a_negm", [P, TC, S])
        valid = sb("a_valid", [P, TC])
        xn = sb("a_xn", [P, TC, D])
        xnT = sb("a_xnT", [P, KC, T])
        sc = sb("a_scores", [P, TC, S])
        ex = sb("a_exp", [P, TC, S])
        exT = sb("a_expT", [P, TC, S // P, P])
        nmax = sb("a_nmax", [P, TC])
        den = sb("a_den", [P, TC])
        rden = sb("a_rden", [P, TC])
        ps = banks("a_psum")
        ln = LayerNorm(nc, sb, sem, "a_ln")
        chain = sem("a_dve_chain")
        ctxT_in = [sem(f"a_ctxT_in{t}") for t in range(TC)]
        ctx_in = [sem(f"a_ctx_in{t}") for t in range(TC)]
        mask_in = sem("a_mask_in")
        xn_ready = sem("a_xn_ready")
        xnT_psum = sem("a_xnT_psum")
        xnT_ready = sem("a_xnT_ready")
        scores_ready = sem("a_scores_ready")
        max_ready = sem("a_max_ready")
        exp_ready = sem("a_exp_ready")
        expT_psum = sem("a_expT_psum")
        expT_ready = sem("a_expT_ready")
        read_ready = sem("a_read_ready")
        consts = g["const_sem"]
        g["spent"] = [chain, mask_in, xn_ready, xnT_psum, xnT_ready, scores_ready, max_ready, exp_ready, expT_psum,
                      expT_ready, read_ready, ln.var_ready, ln.std_ready] + ctxT_in + ctx_in

        with nc.Block() as block:
            @block.sync
            def _(sp):
                sp.dma_start(x[:, :, :], d["x"].rearrange("(t p) c -> p t c", p=P)).then_inc(g["x_in"], 16)
                sp.dma_start(mask_i[:, :, :], d["mask"]).then_inc(mask_in, 16)
                for t in range(TC):
                    half = slice(t * NK // TC, (t + 1) * NK // TC)
                    sp.dma_start(ctxT[:, :, half], d["ctxT"][:, :, half]).then_inc(ctxT_in[t], 16)
                for t in range(TC):
                    half = slice(t * NKC // TC, (t + 1) * NKC // TC)
                    sp.dma_start(ctxk[:, half, :], d["ctx"][:, half, :]).then_inc(ctx_in[t], 16)
                sp.dma_start(g["shared0"][:, :], d["shared0"]).then_inc(g["shared_in"][0], 16)
                for s in range(2):
                    sp.dma_start(g["w0_early"][:, s, :], d["w0"][s]).then_inc(g["w0_in"][s], 16)

            @block.gpsimd
            def _(pool):
                for m in (ident, identb, g["zeros"]):
                    nc.gpsimd.memset(m[:, :], 0.0).then_inc(consts, 1)
                for m in (g["ones"], g["onesb"], g["before"]):
                    nc.gpsimd.memset(m[:, :], 1.0).then_inc(consts, 1)
                pool.wait_ge(consts, 6)
                for m in (ident, identb):
                    nc.gpsimd.affine_select(out=m[:, :], in_=m[:, :], compare_op=ALU.not_equal, fill=1.0, base=0,
                                            pattern=[[-1, P]], channel_multiplier=1).then_inc(consts, 1)
                nc.gpsimd.affine_select(out=g["before"][:, :], in_=g["before"][:, :], compare_op=ALU.is_gt, fill=0.0,
                                        base=0, pattern=[[1, P]], channel_multiplier=-1).then_inc(consts, 1)
                pool.wait_ge(consts, 9)

            @block.vector
            def _(dve):
                step = Steps(dve, chain)
                dve.wait_ge(g["x_in"], 16)
                ln.vector(dve, step, xn, x, xn_ready)
                dve.wait_ge(mask_in, 16)
                step(nc.vector.tensor_copy(mask[:, :, :], mask_i[:, :, :]))
                step(nc.vector.tensor_scalar(negm[:, :, :], mask[:, :, :], NEG, -NEG, ALU.mult, ALU.add))
                step(nc.vector.tensor_reduce(valid[:, :], mask[:, :, :], AX.X, ALU.max))
                for t in range(TC):
                    dve.wait_ge(scores_ready, t + 1)
                    step(nc.vector.scalar_tensor_tensor(sc[:, t, :], ps[:, t, :], D ** -0.5, mask[:, t, :],
                                                        ALU.mult, ALU.mult))
                    step(nc.vector.tensor_tensor(sc[:, t, :], sc[:, t, :], negm[:, t, :], ALU.add))
                    nc.vector.tensor_reduce(nmax[:, t:t + 1], sc[:, t, :], AX.X, ALU.max,
                                            negate=True).then_inc(max_ready, 1)
                for t in range(TC):
                    dve.wait_ge(exp_ready, t + 1)
                    step(nc.vector.reciprocal(rden[:, t:t + 1], den[:, t:t + 1]))
                    step(nc.vector.tensor_tensor(rden[:, t:t + 1], rden[:, t:t + 1], valid[:, t:t + 1], ALU.mult))
                    dve.wait_ge(read_ready, t + 1)
                    step(nc.vector.scalar_tensor_tensor(x[:, t, :], ps[:, 6 + t, 0:D], rden[:, t:t + 1], x[:, t, :],
                                                        ALU.mult, ALU.add))

            @block.scalar
            def _(act):
                ln.scalar(act)
                act.wait_ge(xnT_psum, 1)
                nc.scalar.activation(xnT[:, :, :], ps[:, 7, :].rearrange("p (k t) -> p k t", k=KC),
                                     ACT.Copy).then_inc(xnT_ready, 1)
                for t in range(TC):
                    act.wait_ge(max_ready, t + 1)
                    nc.scalar.activation(ex[:, t, :], sc[:, t, :], ACT.Exp, bias=nmax[:, t:t + 1],
                                         accum_out=den[:, t:t + 1]).then_inc(exp_ready, 1)
                for t in range(TC):
                    act.wait_ge(expT_psum, t + 1)
                    nc.scalar.activation(exT[:, t, :, :], ps[:, 2 + t, :].rearrange("p (c q) -> p c q", q=P),
                                         ACT.Copy).then_inc(expT_ready, 1)

            @block.tensor
            def _(pe):
                pe.wait_ge(consts, 9)
                pe.wait_ge(xn_ready, 1)
                transpose_tokens(nc, ps[:, 7, :], xn, ident).then_inc(xnT_psum, 1)
                pe.wait_ge(xnT_ready, 1)
                for t in range(TC):
                    pe.wait_ge(ctxT_in[t], 16)
                    for j in range(B // TC):
                        b = t * (B // TC) + j
                        for k in range(KC):
                            last = nc.tensor.matmul(ps[j * L:(j + 1) * L, t, :], xnT[:, k, b * L:(b + 1) * L],
                                                    ctxT[:, k, b * S:(b + 1) * S], start=(k == 0), stop=(k == KC - 1))
                    last.then_inc(scores_ready, 1)
                for t in range(TC):
                    pe.wait_ge(exp_ready, t + 1)
                    for c in range(S // P):
                        last = nc.tensor.transpose(ps[:, 2 + t, c * P:(c + 1) * P], ex[:, t, c * P:(c + 1) * P],
                                                   ident[:, :])
                    last.then_inc(expT_psum, 1)
                for t in range(TC):
                    pe.wait_ge(expT_ready, t + 1)
                    pe.wait_ge(ctx_in[t], 16)
                    for j in range(B // TC):
                        b = t * (B // TC) + j
                        for c in range(S // P):
                            last = nc.tensor.matmul(ps[j * L:(j + 1) * L, 6 + t, 0:D], exT[:, t, c, j * L:(j + 1) * L],
                                                    ctxk[:, b * (S // P) + c, :], start=(c == 0), stop=(c == S // P - 1))
                    last.then_inc(read_ready, 1)



def scan_stage(nc, d, g):
    ctx, sb, banks, sem = scope(nc)
    x, ident = g["x"], g["ident"]
    DCH = D // P
    NT = 4
    TILES = N // NT
    UN = 4
    EDGES = (0, 2 * NT, N // 2, 13 * NT, N)
    with ctx:
        xpT = sb("b_xprojT", [P, KC, D])
        dtwT = sb("b_dtwT", [P, D])
        outwT = sb("b_outwT", [P, KC, D])
        cols = sb("b_cols", [P, 4, DCH])
        A = sb("b_A", [P, DCH, N])
        z = sb("b_z", [P, TC, D])
        zn = sb("b_zn", [P, TC, D])
        znT = sb("b_znT", [P, KC, T])
        zDT = sb("b_zDT", [P, KC, T])
        drT = sb("b_drT", [P, T])
        dtT = sb("b_dtT", [P, DCH, T])
        dtxT = sb("b_dtxT", [P, DCH, T])
        dtx = sb("b_dtx", [P, TC, D])
        bc = sb("b_bc", [P, TC, 2 * N])
        cT = sb("b_cT", [N, T])
        bdiag = [sb(f"b_bdiag{t}", [P, N, P]) for t in range(TC)]
        cb = sb("b_cb", [P, TILES, TC * NT * P])
        dA = [sb(f"b_dA{s}", [P, TC * NT * P]) for s in range(2)]
        h = [sb(f"b_h{s}", [P, TC * NT * P]) for s in range(UN)]
        sp_abs, sp_e, sp_u, sp_l, sp_z = (h[s][:, q * DCH * T:(q + 1) * DCH * T].rearrange("p (c t) -> p c t", c=DCH)
                                          for s, q in ((0, 0), (0, 1), (1, 0), (1, 1), (2, 0)))
        yT = sb("b_yT", [P, DCH, T])
        ps = banks("b_psum")
        lnA, lnB = LayerNorm(nc, sb, sem, "b_lnA"), LayerNorm(nc, sb, sem, "b_lnB")
        chain = sem("b_dve_chain")
        achain = sem("b_act_chain")
        w_in = sem("b_w_in")
        zn_ready = sem("b_zn_ready")
        zT_psum = sem("b_zT_psum")
        znT_ready = sem("b_znT_ready")
        proj_psum = sem("b_proj_psum")
        drT_ready = sem("b_drT_ready")
        bc_ready = sem("b_bc_ready")
        dt_psum = sem("b_dt_psum")
        cT_psum = sem("b_cT_psum")
        cT_ready = sem("b_cT_ready")
        cT_stored = sem("b_cT_stored")
        cb_in = sem("b_cb_in")
        spe_ready = sem("b_spe_ready")
        spu_ready = sem("b_spu_ready")
        spl_ready = sem("b_spl_ready")
        dt_ready = sem("b_dt_ready")
        dtxT_ready = sem("b_dtxT_ready")
        dtx_psum = sem("b_dtx_psum")
        dtx_ready = sem("b_dtx_ready")
        diag_ready = sem("b_diag_ready")
        edges_ready = sem("b_edges_ready")
        A_ready = sem("b_A_ready")
        u_ready = sem("b_u_ready")
        dA_ready = sem("b_dA_ready")
        h_ready = sem("b_h_ready")
        hc_ready = sem("b_hc_ready")
        pair_ready = sem("b_pair_ready")
        late_diag_ready = sem("b_late_diag_ready")
        act_diag_ready = sem("b_act_diag_ready")
        y_added = sem("b_y_added")
        y_psum = sem("b_y_psum")
        yT_ready = sem("b_yT_ready")
        out_psum = sem("b_out_psum")
        spent_before = g["spent"]
        g["spent"] = [zn_ready, zT_psum, znT_ready, proj_psum, drT_ready, bc_ready, dt_psum, cT_psum, cT_ready, spe_ready,
                      spu_ready, spl_ready, dt_ready, dtxT_ready, dtx_psum, dtx_ready, yT_ready, y_psum, out_psum,
                      y_added, pair_ready, hc_ready, h_ready, dA_ready, u_ready, A_ready,
                      diag_ready, late_diag_ready, act_diag_ready, edges_ready, chain, achain, w_in]

        def tiles_of(eng, body):
            for c in range(DCH):
                base = c * TILES
                with eng.Fori(0, TILES // UN - 1) as i:
                    for s in range(UN):
                        body(c, i * UN + s, i * UN + (base + s), s, True)
                for s in range(UN):
                    n = TILES - UN + s
                    body(c, n, base + n, s, s < UN - 2)

        def diagonal(eng, done, t, lo, hi):
            axes = [P, hi - lo, P]
            eng.tensor_tensor(bdiag[t][:, lo:hi, :], ident[:, :].unsqueeze(1).to_broadcast(axes),
                              bc[:, t, lo:hi].unsqueeze(2).to_broadcast(axes), ALU.mult).then_inc(done, 1)

        with nc.Block() as block:
            @block.sync
            def _(sp):
                for dst, name in ((xpT, "xprojT"), (dtwT, "dtwT"), (cols, "cols0"), (A, "A_log"), (outwT, "outwT")):
                    sp.dma_start(dst[:], d[name]).then_inc(w_in, 16)
                sp.wait_ge(cT_ready, 1)
                sp.dma_start(d["c_scratch"], cT[:, :]).then_inc(cT_stored, 16)
                sp.wait_ge(cT_stored, 16)
                src = d["c_scratch"].rearrange("(g n) t -> g (n t)", n=NT)
                for q in range(4):
                    part = slice(q * TILES // 4, (q + 1) * TILES // 4)
                    sp.dma_start(cb[:, part, :], src[part, :].partition_broadcast(P)).then_inc(cb_in, 16)
                    sp.wait_ge(cb_in, 16 * (q + 1))

            @block.gpsimd
            def _(pool):
                for spent in spent_before:
                    pool.sem_clear(spent)
                for s in range(2):
                    edge = dA[s][:, :].rearrange("p (s t) -> p s t", t=L)[:, :, 0:1]
                    nc.gpsimd.memset(edge, 0.0).then_inc(edges_ready, 1)
                pool.wait_ge(bc_ready, 1)
                for lo, hi in (EDGES[1:3], EDGES[2:4]):
                    for t in range(TC):
                        diagonal(nc.gpsimd, late_diag_ready, t, lo, hi)

                def scale_by_c(c, n, m, s, more):
                    if c == 0 and s == 0:
                        pool.wait_ge(cb_in, n * (16 // UN) + 16)
                    pool.wait_ge(h_ready, m + (UN + 1))
                    hv = h[s][:, :].rearrange("p (t n q) -> p t n q", t=TC, n=NT)
                    cv = cb[:, ds(n, 1), :].rearrange("p o (n t q) -> p (o t) n q", t=TC, n=NT)
                    nc.gpsimd.tensor_tensor(hv, hv, cv, ALU.mult).then_inc(hc_ready, 1)
                tiles_of(pool, scale_by_c)

            @block.vector
            def _(dve):
                step = Steps(dve, chain)
                lnA.vector(dve, step, z, x)
                lnB.vector(dve, step, zn, z)
                nc.vector.tensor_copy(lnA.std[:, :], lnB.rstd[:, :]).then_inc(zn_ready, 1)
                dve.wait_ge(w_in, 80)
                dve.wait_ge(zT_psum, 1)
                for k in range(KC):
                    step(nc.vector.tensor_scalar(znT[:, k, :], ps[:, 0, k * T:(k + 1) * T], cols[:, 0, k:k + 1],
                                                 cols[:, 1, k:k + 1], ALU.mult, ALU.add))
                    step(nc.vector.tensor_scalar(zDT[:, k, :], ps[:, 1, k * T:(k + 1) * T], cols[:, 3, k:k + 1],
                                                 None, ALU.mult))
                nc.vector.tensor_copy(lnA.std[:, :], lnB.rstd[:, :]).then_inc(znT_ready, 1)
                dve.wait_ge(proj_psum, 1)
                nc.vector.tensor_copy(drT[:, :], ps[:, 2, 0:T]).then_inc(drT_ready, 1)
                nc.vector.tensor_copy(bc[:, :, :], ps[:, 3, 0:T].rearrange("p (t n) -> p t n", t=TC)).then_inc(bc_ready, 1)
                dve.wait_ge(cT_psum, 1)
                nc.vector.tensor_copy(cT[:, :], ps[0:N, 5, 0:T]).then_inc(cT_ready, 1)
                dve.wait_ge(bc_ready, 1)
                for t in range(TC):
                    diagonal(nc.vector, diag_ready, t, *EDGES[0:2])
                dve.wait_ge(spe_ready, DCH)
                nc.vector.tensor_scalar(sp_u[:, :, :], sp_e[:, :, :], 1.0, None, ALU.add).then_inc(spu_ready, 1)
                dve.wait_ge(spu_ready, 1)
                step(nc.vector.tensor_scalar(sp_abs[:, :, :], sp_u[:, :, :], 1.0, None, ALU.subtract))
                step(nc.vector.tensor_scalar(sp_z[:, :, :], sp_abs[:, :, :], 0.0, None, ALU.is_equal))
                step(nc.vector.tensor_tensor(sp_abs[:, :, :], sp_abs[:, :, :], sp_z[:, :, :], ALU.add))
                step(nc.vector.reciprocal(sp_abs[:, :, :], sp_abs[:, :, :]))
                dve.wait_ge(spl_ready, 1)
                step(nc.vector.tensor_tensor(sp_abs[:, :, :], sp_abs[:, :, :], sp_l[:, :, :], ALU.mult))
                step(nc.vector.tensor_tensor(sp_abs[:, :, :], sp_abs[:, :, :], sp_z[:, :, :], ALU.add))
                step(nc.vector.tensor_tensor(sp_e[:, :, :], sp_e[:, :, :], sp_abs[:, :, :], ALU.mult))
                for k in range(DCH):
                    step(nc.vector.tensor_scalar(sp_z[:, k, :], ps[:, 4, k * T:(k + 1) * T], cols[:, 2, k:k + 1], 0.0,
                                                 ALU.add, ALU.max))
                nc.vector.tensor_tensor(dtT[:, :, :], sp_z[:, :, :], sp_e[:, :, :], ALU.add).then_inc(dt_ready, 1)
                dve.wait_ge(dt_ready, 1)
                nc.vector.tensor_tensor(dtxT[:, :, :], dtT[:, :, :], znT[:, :, :], ALU.mult).then_inc(dtxT_ready, 1)
                dve.wait_ge(dtx_psum, 1)
                nc.vector.tensor_copy(dtx[:, :, :], ps[:, 6, :].rearrange("p (t c) -> p t c", t=TC)).then_inc(dtx_ready, 1)

                dve.wait_ge(dtx_ready, 1)
                nc.vector.tensor_copy(lnA.std[:, :], lnB.rstd[:, :]).then_inc(h_ready, UN)

                def scan(c, n, m, s, more):
                    dve.wait_ge(u_ready, m + 1)
                    dve.wait_ge(dA_ready, m * NT + NT)
                    dve.wait_ge(y_added, m + 1)
                    nc.vector.tensor_tensor_scan(h[s][:, :], dA[s % 2][:, :], ps[:, 2 * (s % 2):2 * (s % 2) + 2, :]
                                                 .rearrange("p a b -> p (a b)"), 0.0, ALU.mult, ALU.add).then_inc(h_ready, 1)

                def pair(c, n, m, s):
                    dve.wait_ge(hc_ready, m + 1)
                    hv = h[s][:, :].rearrange("p (t n q) -> p t n q", t=TC, n=NT)
                    nc.vector.tensor_tensor(hv[:, :, 0:NT // 2], hv[:, :, 0:NT // 2], hv[:, :, NT // 2:NT],
                                            ALU.add).then_inc(pair_ready, 1)

                def scan_ahead(c, n, m, s, more):
                    if more:
                        scan(c, n + 1, m + 1, (s + 1) % UN, True)
                    pair(c, n, m, s)
                for c in range(DCH):
                    base = c * TILES
                    if c == 0:
                        scan(c, 0, base, 0, True)
                    with dve.Fori(0, TILES // UN - 1) as i:
                        for s in range(UN):
                            scan_ahead(c, i * UN + s, i * UN + (base + s), s, True)
                    for s in range(UN):
                        n = TILES - UN + s
                        scan_ahead(c, n, base + n, s, s < UN - 1 or c < DCH - 1)
                for c in range(DCH):
                    dve.wait_ge(y_psum, c + 1)
                    nc.vector.tensor_copy(yT[:, c, :], ps[:, 4 + c, 0:T]).then_inc(yT_ready, 1)
                dve.wait_ge(out_psum, 1)
                step(nc.vector.tensor_tensor(x[:, :, :], x[:, :, :], ps[:, 6, :].rearrange("p (t c) -> p t c", t=TC), ALU.add))

            @block.scalar
            def _(act):
                astep = Steps(act, achain)
                lnA.scalar(act)
                lnB.scalar(act)
                act.wait_ge(w_in, 80)
                astep(nc.scalar.activation(A[:, :, :], A[:, :, :], ACT.Exp))
                astep(nc.scalar.activation(A[:, :, :], A[:, :, :], ACT.Copy, scale=-1.0))
                act.wait_ge(dt_psum, 1)
                for k in range(DCH):
                    astep(nc.scalar.activation(sp_l[:, k, :], ps[:, 4, k * T:(k + 1) * T], ACT.Abs,
                                               bias=cols[:, 2, k:k + 1]))
                for k in range(DCH):
                    nc.scalar.activation(sp_e[:, k, :], sp_l[:, k, :], ACT.Exp, scale=-1.0).then_inc(spe_ready, 1)
                act.wait_ge(spu_ready, 1)
                nc.scalar.activation(sp_l[:, :, :], sp_u[:, :, :], ACT.Ln).then_inc(spl_ready, 1)
                act.preload_act_table(ACT.Exp)
                act.wait_ge(bc_ready, 1)
                for t in range(TC):
                    with act.Fori(EDGES[3], EDGES[4]) as n:
                        nc.scalar.activation(bdiag[t][:, ds(n, 1), :], ident[:, :].unsqueeze(1), ACT.Copy,
                                             scale=bc[:, t, ds(n, 1)]).then_inc(act_diag_ready, 1)
                act.wait_ge(dt_ready, 1)
                act.wait_ge(edges_ready, 2)

                def decay(c, n, m, s, more):
                    act.wait_ge(h_ready, m + (UN - 1))
                    out = dA[s % 2][:, :].rearrange("p (t n b l) -> p t n b l", t=TC, n=NT, l=L)
                    src = dtT[:, c, :].rearrange("p (t b l) -> p t b l", t=TC, l=L)[:, :, :, 1:L]
                    for j in range(NT):
                        nc.scalar.activation(out[:, :, j, :, 1:L], src, ACT.Exp,
                                             scale=A[:, c, ds(n * NT + j, 1)]).then_inc(dA_ready, 1)
                tiles_of(act, decay)

            @block.tensor
            def _(pe):
                keep_warm(nc, g, ps[:, 7, :], 18)
                pe.wait_ge(zn_ready, 1)
                transpose_tokens(nc, ps[:, 0, :], zn, ident)
                transpose_tokens(nc, ps[:, 1, :], z, ident).then_inc(zT_psum, 1)
                keep_warm(nc, g, ps[:, 7, :], 13)
                pe.wait_ge(znT_ready, 1)
                pe.wait_ge(w_in, 80)
                for k in range(KC):
                    nc.tensor.matmul(ps[:, 2, 0:T], xpT[:, k, 0:RANK], znT[:, k, :], start=(k == 0), stop=(k == KC - 1))
                for t in range(TC):
                    for k in range(KC):
                        last = nc.tensor.matmul(ps[:, 3, t * 2 * N:(t + 1) * 2 * N], znT[:, k, t * P:(t + 1) * P],
                                                xpT[:, k, RANK:D], start=(k == 0), stop=(k == KC - 1))
                last.then_inc(proj_psum, 1)
                pe.wait_ge(drT_ready, 1)
                for k in range(DCH):
                    last = nc.tensor.matmul(ps[:, 4, k * T:(k + 1) * T], dtwT[:, k * P:(k + 1) * P], drT[:, :],
                                            start=True, stop=True)
                last.then_inc(dt_psum, 1)
                pe.wait_ge(bc_ready, 1)
                for t in range(TC):
                    last = nc.tensor.transpose(ps[0:N, 5, t * P:(t + 1) * P], bc[:, t, N:2 * N], ident[:, :])
                last.then_inc(cT_psum, 1)
                pe.wait_ge(spl_ready, 1)
                keep_warm(nc, g, ps[:, 7, :], 30)
                pe.wait_ge(dtxT_ready, 1)
                for t in range(TC):
                    for k in range(DCH):
                        last = nc.tensor.transpose(ps[:, 6, t * D + k * P:t * D + (k + 1) * P],
                                                   dtxT[:, k, t * P:(t + 1) * P], ident[:, :])
                last.then_inc(dtx_psum, 1)
                pe.wait_ge(dtx_ready, 1)
                pe.wait_ge(diag_ready, TC)
                pe.wait_ge(cT_ready, 1)

                def drive(c, n, m, s):
                    for t in range(TC):
                        last = nc.tensor.matmul(ps[:, 2 * (s % 2) + t, :], dtx[:, t, c * P:(c + 1) * P],
                                                bdiag[t][:, ds(n * NT, NT), :], start=True, stop=True)
                    last.then_inc(u_ready, 1)

                def sum_states(c, n, m, s, more):
                    if more:
                        pe.wait_ge(h_ready, m + (UN + 1))
                        nxt = c, n + 2
                        if isinstance(n, int) and n + 2 >= TILES:
                            nxt = c + 1, n + 2 - TILES
                        drive(*nxt, m + 2, s)
                    pe.wait_ge(pair_ready, m + 1)
                    hv = h[s][:, :].rearrange("p (t n q) -> p n t q", t=TC, n=NT)
                    for j in range(NT // 2):
                        last = nc.tensor.matmul(ps[:, 4 + c, 0:T], ident[:, :], hv[:, j], start=False, stop=False,
                                                skip_group_check=True)
                    last.then_inc(y_added, 1)

                for c in range(DCH):
                    base = c * TILES
                    first = nc.tensor.matmul(ps[:, 4 + c, 0:T], ident[:, :], zDT[:, c, :], start=True, stop=False,
                                             skip_group_check=True)
                    if c == 0:
                        first.then_inc(y_added, UN)
                    if c == 0:
                        for n in range(2):
                            drive(c, n, base + n, n)
                        pe.wait_ge(late_diag_ready, 2 * TC)
                        pe.wait_ge(act_diag_ready, TC * (EDGES[4] - EDGES[3]))
                    with pe.Fori(0, TILES // UN - 1) as i:
                        for s in range(UN):
                            sum_states(c, i * UN + s, i * UN + (base + s), s, True)
                    for s in range(UN):
                        n = TILES - UN + s
                        sum_states(c, n, base + n, s, s < UN - 2 or c < DCH - 1)
                    nc.tensor.matmul(ps[:, 4 + c, 0:T], g["zeros"][:, :], zDT[:, c, :], start=False, stop=True,
                                     skip_group_check=True).then_inc(y_psum, 1)
                pe.wait_ge(yT_ready, DCH)
                for t in range(TC):
                    for k in range(DCH):
                        last = nc.tensor.matmul(ps[:, 6, t * D:(t + 1) * D], yT[:, k, t * P:(t + 1) * P], outwT[:, k, :],
                                                start=(k == 0), stop=(k == DCH - 1))
                last.then_inc(out_psum, 1)

class Moe:

    def __init__(self, name, groups, per, width, shared, unroll):
        self.name, self.groups, self.per, self.width = name, groups, per, width
        self.shared, self.unroll = shared, unroll

    def parts(self, w, width):
        n = KC * width
        return (w[:, 0:n].rearrange("p (k f) -> p k f", k=KC), w[:, n:2 * n].rearrange("p (k f) -> p k f", k=KC),
                w[:, 2 * n:].rearrange("p (c m) -> p c m", m=D))


MOE0 = Moe("c", NG0, EPG0, W0, F0, 4)
MOE1 = Moe("f", NG1, EPG1, W1, W1, 1)


def row_chunks(width):
    return [(c, min(P, width - c * P)) for c in range(-(-width // P))]


def route0(nc, dve, step, r, sem_logits, sem_sel, sem_count, g):
    dve.wait_ge(sem_logits, 1)
    step(nc.vector.tensor_tensor(r.ext[:, :, 0:E0], r.scores[:, :, :],
                                 r.bias[:, :].unsqueeze(1).to_broadcast([P, TC, E0]), ALU.add))
    per = E0 // G0
    for t in range(TC):
        for q in range(G0):
            last = nc.vector.max(r.m8[:, t, q, :], r.ext[:, t, q * per:(q + 1) * per])
    step(last)
    step(nc.vector.tensor_tensor(r.gext[:, :, 0:G0], r.m8[:, :, :, 0], r.m8[:, :, :, 1], ALU.add))
    for t in range(TC):
        step(nc.vector.max(r.top[:, t, :], r.gext[:, t, :]))
        step(nc.vector.match_replace(r.grep[:, t, :], r.top[:, t, :], r.gext[:, t, :], -NEG))
    step(nc.vector.tensor_tensor(r.gmask[:, :, :], r.grep[:, :, 0:G0], r.gext[:, :, 0:G0], ALU.not_equal))
    step(nc.vector.tensor_scalar(r.gneg[:, :, :], r.gmask[:, :, :], NEG, -NEG, ALU.mult, ALU.add))
    e4 = r.ext[:, :, 0:E0].rearrange("p t (q e) -> p t q e", q=G0)
    step(nc.vector.tensor_tensor(e4, e4, r.gmask[:, :, :].unsqueeze(3).to_broadcast([P, TC, G0, per]), ALU.mult))
    step(nc.vector.tensor_tensor(e4, e4, r.gneg[:, :, :].unsqueeze(3).to_broadcast([P, TC, G0, per]), ALU.add))
    for t in range(TC):
        step(nc.vector.max(r.top[:, t, :], r.ext[:, t, :]))
        step(nc.vector.match_replace(r.rep[:, t, :], r.top[:, t, :], r.ext[:, t, :], -3e38))
    step(nc.vector.tensor_tensor(r.sel[:, :, :], r.rep[:, :, 0:E0], r.ext[:, :, 0:E0], ALU.not_equal))
    nc.vector.tensor_copy(r.selb[:, :, :], r.sel[:, :, :]).then_inc(sem_sel, 1)
    step(nc.vector.tensor_tensor(r.w[:, :, :], r.sel[:, :, :], r.scores[:, :, :], ALU.mult))
    step(nc.vector.tensor_reduce(r.sum[:, :], r.w[:, :, :], AX.X, ALU.add))
    step(nc.vector.reciprocal(r.sum[:, :], r.sum[:, :]))
    step(nc.vector.tensor_scalar(r.sum[:, :], r.sum[:, :], SCALE0, None, ALU.mult))
    step(nc.vector.tensor_tensor(r.w[:, :, :], r.w[:, :, :], r.sum[:, :].unsqueeze(2).to_broadcast([P, TC, E0]), ALU.mult))
    dve.wait_ge(sem_count, 1)
    step(nc.vector.tensor_scalar(r.keep[:, :, :], r.count_psum, float(CAP0), None, ALU.is_lt))
    step(nc.vector.tensor_tensor(r.w[:, :, :], r.w[:, :, :], r.keep[:, :, :], ALU.mult))


def route1_logits(nc, dve, step, r, sem_max):
    dve.wait_ge(r.logits_ready, 1)
    step(nc.vector.tensor_reduce(r.nmax[:, :], r.logits_psum, AX.X, ALU.max, negate=True))
    step(nc.vector.tensor_tensor(r.scores[:, :, :], r.logits_psum,
                                 r.nmax[:, :].unsqueeze(2).to_broadcast([P, TC, E1]), ALU.add))
    nc.vector.tensor_copy(r.logit[:, :, :], r.scores[:, :, :]).then_inc(sem_max, 1)


def route1(nc, dve, step, r, sem_exp, g):
    dve.wait_ge(sem_exp, 1)
    step(nc.vector.tensor_reduce(r.sum[:, :], r.scores[:, :, :], AX.X, ALU.add))
    step(nc.vector.reciprocal(r.sum[:, :], r.sum[:, :]))
    step(nc.vector.tensor_tensor(r.ext[:, :, 0:E1], r.scores[:, :, :],
                                 r.sum[:, :].unsqueeze(2).to_broadcast([P, TC, E1]), ALU.mult))
    for t in range(TC):
        step(nc.vector.max(r.top[:, t, :], r.ext[:, t, :]))
        step(nc.vector.match_replace(r.rep[:, t, :], r.top[:, t, :], r.ext[:, t, :], -1.0))
    step(nc.vector.tensor_tensor(r.sel[:, :, :], r.rep[:, :, 0:E1], r.ext[:, :, 0:E1], ALU.not_equal))
    step(nc.vector.tensor_tensor(r.w[:, :, :], r.sel[:, :, :], r.ext[:, :, 0:E1], ALU.mult))


class Space:
    pass


def moe_stage(nc, d, g, moe):
    ctx, sb, banks, sem = scope(nc)
    x, ident = g["x"], g["ident"]
    nm = moe.name
    first = moe is MOE0
    experts, top = (E0, K0) if first else (E1, K1)
    W, UN = moe.width, moe.unroll
    rc = row_chunks(W)
    rc_shared = row_chunks(moe.shared)
    with ctx:
        gate_w = sb(nm + "_gate_w", [P, KC, experts])
        xn = sb(nm + "_xn", [P, TC, D])
        xnT = sb(nm + "_xnT", [P, KC, T])
        silu = [sb(f"{nm}_silu{t}", [P, W]) for t in range(TC)]
        prod = [sb(f"{nm}_prod{t}", [P, W]) for t in range(TC)]
        a = [sb(f"{nm}_a{t}", [P, W]) for t in range(TC)]
        aT = [sb(f"{nm}_aT{t}", [P, DC, P]) for t in range(TC)]
        r = Space()
        r.scores = sb(nm + "_scores", [P, TC, experts])
        r.logit = sb(nm + "_logit", [P, TC, experts])
        pad = 8 - top
        r.ext = sb(nm + "_ext", [P, TC, experts + pad])
        r.rep = sb(nm + "_rep", [P, TC, experts + pad])
        r.sel = sb(nm + "_sel", [P, TC, experts])
        r.w = sb(nm + "_w", [P, TC, experts])
        r.top = sb(nm + "_top", [P, TC, 8])
        r.sum = sb(nm + "_sum", [P, TC])
        r.nmax = sb(nm + "_nmax", [P, TC])
        if first:
            r.bias = sb(nm + "_bias", [P, E0])
            r.m8 = sb(nm + "_m8", [P, TC, G0, 8])
            r.gext = sb(nm + "_gext", [P, TC, G0 + 8 - KG0])
            r.grep = sb(nm + "_grep", [P, TC, G0 + 8 - KG0])
            r.gmask = sb(nm + "_gmask", [P, TC, G0])
            r.gneg = sb(nm + "_gneg", [P, TC, G0])
            r.selb = sb(nm + "_selb", [P, TC, E0], BF16)
            r.keep = sb(nm + "_keep", [P, TC, E0])
            late = sb("w0_late", [P, 2, SLOT0])
            slots = [g["w0_early"][:, 0, :], g["w0_early"][:, 1, :], late[:, 0, :], late[:, 1, :]]
            shared_w = g["shared0"]
        else:
            shared_w = g["shared1"]
        ps = banks(nm + "_psum")
        GU = [[ps[:, 2 * t + u, :] for u in range(2)] for t in range(TC)]
        AT = [ps[:, 4 + t, :] for t in range(TC)]
        ACC = [ps[:, 6 + t, 0:D] for t in range(TC)]
        r.logits_psum = ps[:, 4, 0:TC * experts].rearrange("p (t e) -> p t e", t=TC)
        if first:
            r.count_psum = GU[1][1][:, W:W + TC * experts].rearrange("p (t e) -> p t e", t=TC)
        ln = LayerNorm(nc, sb, sem, nm + "_ln")
        chain = sem(nm + "_dve_chain")
        small_in = sem(nm + "_small_in")
        pads_ready = sem(nm + "_pads_ready")
        xn_ready = sem(nm + "_xn_ready")
        xnT_psum = sem(nm + "_xnT_psum")
        xnT_ready = sem(nm + "_xnT_ready")
        r.logits_ready = sem(nm + "_logits_ready")
        score_ready = sem(nm + "_score_ready")
        max_ready = sem(nm + "_max_ready")
        sel_ready = sem(nm + "_sel_ready")
        count_ready = sem(nm + "_count_ready")
        w_ready = sem(nm + "_w_ready")
        gu_ready = sem(nm + "_gu_ready")
        silu_ready = sem(nm + "_silu_ready")
        prod_ready = sem(nm + "_prod_ready")
        a_ready = sem(nm + "_a_ready")
        aT_psum = sem(nm + "_aT_psum")
        aT_ready = sem(nm + "_aT_ready")
        down_done = sem(nm + "_down_done")
        consts = g["const_sem"]

        def half_steps(eng, body):
            rounds = moe.groups // UN
            with eng.Fori(0, rounds - 1) as i:
                for s in range(UN):
                    for t in range(TC):
                        body(i * UN + s, s, t, i * (2 * UN) + (2 + 2 * s + t), i, False)
            for s in range(UN):
                grp = (rounds - 1) * UN + s
                for t in range(TC):
                    body(grp, s, t, 2 + 2 * grp + t, rounds - 1, s == UN - 1)

        with nc.Block() as block:
            @block.sync
            def _(sp):
                sp.dma_start(gate_w[:, :, :], d[f"gate{nm}"]).then_inc(small_in, 16)
                if first:
                    sp.dma_start(r.bias[:, :], d["bias0"]).then_inc(small_in, 16)
                    for s in range(2, UN):
                        sp.dma_start(slots[s], d["w0"][s]).then_inc(g["w0_in"][s], 16)
                    with sp.Fori(0, moe.groups // UN - 1) as i:
                        for s in range(UN):
                            sp.wait_ge(down_done, i * (2 * UN) + (4 + 2 * s))
                            sp.dma_start(slots[s].unsqueeze(1), d["w0"][ds(i * UN + (UN + s), 1), :, :]
                                         .rearrange("o p f -> p o f")).then_inc(g["w0_in"][s], 16)

            @block.gpsimd
            def _(pool):
                nc.gpsimd.memset(r.ext[:, :, experts:], NEG).then_inc(pads_ready, 1)
                if first:
                    nc.gpsimd.memset(r.gext[:, :, G0:], NEG).then_inc(pads_ready, 1)
                    for spent in g["spent"]:
                        pool.sem_clear(spent)

            @block.vector
            def _(dve):
                step = Steps(dve, chain)
                ln.vector(dve, step, xn, x, xn_ready)
                if not first:
                    route1_logits(nc, dve, step, r, max_ready)
                for t in range(TC):
                    dve.wait_ge(silu_ready, t + 1)
                    nc.vector.tensor_tensor(a[t][:, 0:moe.shared], silu[t][:, 0:moe.shared], GU[t][1][:, 0:moe.shared],
                                            ALU.mult).then_inc(a_ready, 1)
                dve.wait_ge(pads_ready, 2 if first else 1)
                dve.wait_ge(small_in, 32 if first else 16)
                if first:
                    route0(nc, dve, step, r, score_ready, sel_ready, count_ready, g)
                else:
                    route1(nc, dve, step, r, score_ready, g)
                nc.vector.tensor_copy(r.nmax[:, :], r.sum[:, :]).then_inc(w_ready, 1)

                def weigh(grp, s, t, q, i, end):
                    dve.wait_ge(silu_ready, q + 1)
                    nc.vector.tensor_tensor(prod[t][:, :], silu[t][:, :], GU[t][1][:, 0:W], ALU.mult).then_inc(prod_ready, 1)
                    dve.wait_ge(prod_ready, q - 1)
                    dve.wait_ge(aT_psum, q - 1)
                    wv = r.w[:, t, ds(grp * moe.per, moe.per)].unsqueeze(2).to_broadcast([P, moe.per, W // moe.per])
                    nc.vector.tensor_tensor(a[t][:, :].rearrange("p (e f) -> p e f", e=moe.per),
                                            prod[t][:, :].rearrange("p (e f) -> p e f", e=moe.per), wv,
                                            ALU.mult).then_inc(a_ready, 1)
                half_steps(dve, weigh)
                dve.wait_ge(down_done, 2 + 2 * moe.groups)
                for t in range(TC):
                    step(nc.vector.tensor_tensor(x[:, t, :], x[:, t, :], ACC[t], ALU.add))

            @block.scalar
            def _(act):
                ln.scalar(act)
                act.wait_ge(xnT_psum, 1)
                nc.scalar.activation(xnT[:, :, :], ps[:, 6, :].rearrange("p (k t) -> p k t", k=KC),
                                     ACT.Copy).then_inc(xnT_ready, 1)
                if first:
                    act.wait_ge(r.logits_ready, 1)
                    nc.scalar.activation(r.scores[:, :, :], r.logits_psum, ACT.Sigmoid).then_inc(score_ready, 1)
                else:
                    act.preload_act_table(ACT.Exp)
                    act.wait_ge(max_ready, 1)
                    nc.scalar.activation(r.scores[:, :, :], r.logit[:, :, :], ACT.Exp).then_inc(score_ready, 1)
                act.preload_act_table(ACT.Silu)
                for t in range(TC):
                    act.wait_ge(gu_ready, t + 1)
                    nc.scalar.activation(silu[t][:, 0:moe.shared], GU[t][0][:, 0:moe.shared], ACT.Silu).then_inc(silu_ready, 1)

                def copy_aT(t, q, rows):
                    act.wait_ge(aT_psum, q + 1)
                    av = AT[t].rearrange("p (c m) -> p c m", m=P)
                    full = [c for c, k in rows if k == P]
                    if full:
                        last = nc.scalar.activation(aT[t][:, 0:len(full), :], av[:, 0:len(full), :], ACT.Copy)
                    if len(full) < len(rows):
                        c, k = rows[-1]
                        last = nc.scalar.activation(aT[t][0:k, c, :], av[0:k, c, :], ACT.Copy)
                    last.then_inc(aT_ready, 1)

                def silu_of(t, q):
                    act.wait_ge(gu_ready, q + 1)
                    nc.scalar.activation(silu[t][:, :], GU[t][0][:, 0:W], ACT.Silu).then_inc(silu_ready, 1)

                for t in range(TC):
                    copy_aT(t, t, rc_shared)
                    silu_of(t, 2 + t)

                def half(grp, s, t, q, i, end):
                    act.wait_ge(down_done, q - 1)
                    copy_aT(t, q, rc)
                    if not end:
                        silu_of(t, q + 2)
                half_steps(act, half)

            @block.tensor
            def _(pe):
                keep_warm(nc, g, ps[:, 7, :], 14 if first else 17)
                pe.wait_ge(xn_ready, 1)
                transpose_tokens(nc, ps[:, 6, :], xn, ident).then_inc(xnT_psum, 1)
                pe.wait_ge(xnT_ready, 1)
                pe.wait_ge(small_in, 32 if first else 16)
                for t in range(TC):
                    for k in range(KC):
                        last = nc.tensor.matmul(r.logits_psum[:, t, :], xnT[:, k, t * P:(t + 1) * P], gate_w[:, k, :],
                                                start=(k == 0), stop=(k == KC - 1))
                last.then_inc(r.logits_ready, 1)

                def gate_up(t, parts, width):
                    for u in range(2):
                        for k in range(KC):
                            last = nc.tensor.matmul(GU[t][u][:, 0:width], xnT[:, k, t * P:(t + 1) * P], parts[u][:, k, :],
                                                    start=(k == 0), stop=(k == KC - 1))
                    last.then_inc(gu_ready, 1)

                def turn(t, q, rows):
                    pe.wait_ge(a_ready, q + 1)
                    for c, k in rows:
                        last = nc.tensor.transpose(AT[t][0:k, c * P:(c + 1) * P], a[t][:, c * P:c * P + k], ident[:, :])
                    last.then_inc(aT_psum, 1)

                def down(t, q, rows, parts, start, stop):
                    pe.wait_ge(aT_ready, q + 1)
                    for c, k in rows:
                        last = nc.tensor.matmul(ACC[t], aT[t][0:k, c, :], parts[2][0:k, c, :], start=(start and c == 0),
                                                stop=(stop and c == rows[-1][0]), skip_group_check=True)
                    last.then_inc(down_done, 1)

                def weights(grp, s):
                    if first:
                        return moe.parts(slots[s], W)
                    return [v.rearrange("p o k f -> p (o k) f") for v in (
                        g["w1"][:, ds(grp, 1), 0:KC * W].rearrange("p o (k f) -> p o k f", k=KC),
                        g["w1"][:, ds(grp, 1), KC * W:2 * KC * W].rearrange("p o (k f) -> p o k f", k=KC),
                        g["w1"][:, ds(grp, 1), 2 * KC * W:].rearrange("p o (k f) -> p o k f", k=DC))]

                def arrived(s, rnd):
                    if first:
                        pe.wait_ge(g["w0_in"][s], rnd * 16 + 16)

                sparts = moe.parts(shared_w[:, :], moe.shared)
                pe.wait_ge(g["shared_in"][0 if first else 1], 16)
                if not first:
                    pe.wait_ge(g["w1_in"], 16 * NG1)
                for t in range(TC):
                    gate_up(t, sparts, moe.shared)
                pe.wait_ge(score_ready, 1)
                for t in range(TC):
                    turn(t, t, rc_shared)
                    if t == 0:
                        arrived(0, 0)
                    gate_up(t, weights(0, 0), W)
                    down(t, t, rc_shared, sparts, True, False)
                if first:
                    pe.wait_ge(sel_ready, 1)
                    for t in range(TC):
                        if t:
                            nc.tensor.matmul(r.count_psum[:, t, :], g["onesb"][:, :], r.selb[:, 0, :], start=True, stop=False)
                        last = nc.tensor.matmul(r.count_psum[:, t, :], g["before"][:, :], r.selb[:, t, :],
                                                start=(t == 0), stop=True)
                    last.then_inc(count_ready, 1)

                def half(grp, s, t, q, i, end):
                    turn(t, q, rc)
                    if not end:
                        if t == 0:
                            arrived((s + 1) % UN, i + (1 if s == UN - 1 else 0))
                        gate_up(t, weights(grp + 1, (s + 1) % UN), W)
                    down(t, q, rc, weights(grp, s), False, end)
                half_steps(pe, half)

K_PARTS = 3
KPS = 2


def layer1_memory(nc, d, g, sb, sem):
    g["v"] = sb("v", [P, NKC, D])
    g["vam"] = sb("v_absmax", [P, D])
    g["qs"] = sb("qs", [P, TC, H, 100], BF16)
    g["kT_stored"] = [sem(f"kT_stored{s}") for s in range(2)]
    g["w1"] = sb("w1", [P, NG1, SLOT1])
    g["shared1"] = sb("shared1", [P, SLOT1])
    g["w1_in"] = sem("w1_in")
    g["w_inT"] = sb("w_inT", [P, KC, 2 * INNER])
    g["w_inT_in"] = sem("w_inT_in")


PRODUCTS = ((0, 0), (0, 1), (0, 2), (1, 0), (1, 1), (2, 0))
QROWS = len(PRODUCTS) * HD


def quantize_queries(nc, step, src, scaled, out, rest, s, rs, absmax, qs, done):
    f3, i3, q3, r3 = (a[:, :, :].rearrange("p t (h e) -> p (t h) e", e=HD) for a in (src, scaled, out, rest))
    axes = [P, TC * H, HD]
    step(nc.vector.tensor_reduce(absmax, f3, AX.X, ALU.max, apply_absolute_value=True))
    step(nc.vector.tensor_scalar(s, absmax, 1.0 / 127.0, 1e-8, ALU.mult, ALU.max))
    step(nc.vector.reciprocal(rs, s))
    step(nc.vector.tensor_tensor(i3, f3, rs.unsqueeze(2).to_broadcast(axes), ALU.mult))
    step(nc.vector.tensor_scalar(i3, i3, ROUND, ROUND, ALU.add, ALU.subtract))
    step(nc.vector.tensor_tensor(q3, i3, s.unsqueeze(2).to_broadcast(axes), ALU.mult))

    def columns(part):
        return [qs[:, :, :, j * HD:(j + 1) * HD].rearrange("p t h e -> p (t h) e")
                for j, (pq, _) in enumerate(PRODUCTS) if pq == part]

    def part_to(src_, part):
        for c in columns(part):
            step(nc.vector.tensor_copy(c, src_))
        return columns(part)[0]
    p0 = part_to(q3, 0)
    step(nc.vector.tensor_tensor(r3, q3, p0, ALU.subtract))
    p1 = part_to(r3, 1)
    step(nc.vector.tensor_tensor(q3, r3, p1, ALU.subtract))
    nc.vector.tensor_copy(columns(2)[0], q3).then_inc(done, 1)


def kv_stage(nc, d, g):
    ctx, sb, banks, sem = scope(nc)
    x, ident, identb = g["x"], g["ident"], g["identb"]
    STEPS = NKC // KPS
    KEYS = KPS * P
    with ctx:
        wkv = sb("k_wkv", [P, KC, 2 * D])
        bkv = sb("k_bkv", [P, 2 * D])
        cT = [sb(f"k_ctxT{s}", [P, KC, KEYS]) for s in range(2)]
        v, vam = g["v"], g["vam"]
        bias_part = [sb(f"k_bias_part{q}", [P, 2 * D], BF16) for q in range(K_PARTS)]
        bias_rest = [sb(f"k_bias_rest{q}", [P, 2 * D]) for q in range(2)]
        bias_rows = sb("k_bias_rows", [K_PARTS * 32, 2 * D], BF16)
        vstep = sb("k_v_step_max", [P, D])
        ki = sb("k_ki", [P, KPS, D])
        kq = [sb(f"k_kq{s}", [P, KPS, D]) for s in range(2)]
        rest = [sb(f"k_rest{s}", [P, KPS, D]) for s in range(2)]
        parts = [sb(f"k_parts{s}", [P, K_PARTS, KPS, D], BF16) for s in range(2)]
        kT = [sb(f"k_kT{s}", [P, K_PARTS * KC, KEYS], BF16) for s in range(2)]
        am = sb("k_absmax", [P, KPS * H])
        sc = sb("k_scale", [P, KPS * H])
        rs = sb("k_rscale", [P, KPS * H])
        wq = sb("k_wq", [P, KC, D])
        bq = sb("k_bq", [P, D])
        xn = sb("k_xn", [P, TC, D])
        xnT = sb("k_xnT", [P, KC, T])
        qf = sb("k_qf", [P, TC, D])
        qi = sb("k_qi", [P, TC, D])
        qq = sb("k_qq", [P, TC, D])
        qr = sb("k_qrest", [P, TC, D])
        ps = banks("k_psum")
        ln = LayerNorm(nc, sb, sem, "k_ln")
        xn_ready = sem("k_xn_ready")
        xnT_psum = sem("k_xnT_psum")
        xnT_ready = sem("k_xnT_ready")
        q_psum = sem("k_q_psum")
        qs_ready = sem("k_qs_ready")
        w_in = sem("k_w_in")
        bias_in = sem("k_bias_in")
        cT_in = [sem(f"k_ctxT_in{s}") for s in range(2)]
        chain = sem("k_dve_chain")
        kv_psum = sem("k_kv_psum")
        k_read = sem("k_read")
        v_read = sem("k_v_read")
        bias_ready = sem("k_bias_ready")
        vmax_ready = sem("k_vmax_ready")
        kq_ready = sem("k_kq_ready")
        part0_ready = sem("k_part0_ready")
        rest_ready = sem("k_rest_ready")
        part1_ready = sem("k_part1_ready")
        part2_ready = sem("k_part2_ready")
        kT_psum = sem("k_kT_psum")
        kT_ready = sem("k_kT_ready")
        kT_stored = g["kT_stored"]
        CH = 5

        def all_steps(eng, body):
            for s in range(2):
                body(s, s, 0, True)
            with eng.Fori(1, STEPS // 2 - 1) as i:
                for s in range(2):
                    body(i * 2 + s, s, i, True)
            for s in range(2):
                body(STEPS - 2 + s, s, STEPS // 2 - 1, False)

        def psum_kv(s, part):
            return ps[:, 2 * s + part, :].rearrange("p (c n) -> p c n", n=D)

        psT = [ps[:, 4 + 2 * s:6 + 2 * s, :].rearrange("p a b -> p (a b)").bitcast(BF16)[:, 0:K_PARTS * KC * KEYS]
               .rearrange("p (q n) -> p q n", n=KEYS) for s in range(2)]

        with nc.Block() as block:
            @block.sync
            def _(sp):
                sp.dma_start(bkv[:, :], d["bkv"]).then_inc(bias_in, 16)
                for dst, name in ((wq, "wq"), (bq, "bq"), (wkv, "wkv")):
                    sp.dma_start(dst[:], d[name]).then_inc(w_in, 16)
                for s in range(2):
                    sp.dma_start(cT[s][:, :, :], d["ctxT"][:, :, s * KEYS:(s + 1) * KEYS]).then_inc(cT_in[s], 16)

                def load(m, s, i, more):
                    if more:
                        ahead = m * KEYS + 2 * KEYS
                        if not isinstance(m, int):
                            ahead = sp.snap(ahead)
                        sp.wait_ge(kv_psum, m + 1)
                        sp.dma_start(cT[s][:, :, :], d["ctxT"][:, :, ds(ahead, KEYS)]).then_inc(cT_in[s], 16)
                    if s == 0:
                        sp.dma_start(g["w1"][:, ds(i, 1), :], d["w1"][ds(i, 1), :, :].rearrange("o p f -> p o f"))\
                          .then_inc(g["w1_in"], 16)
                assert NG1 == STEPS // 2
                sp.dma_start(g["shared1"][:, :], d["shared1"]).then_inc(g["shared_in"][1], 16)
                all_steps(sp, load)

            @block.vector
            def _(dve):
                step = Steps(dve, chain)
                dve.sem_inc(k_read, 2)
                nc.vector.memset(vam[:, :], 0.0).then_inc(vmax_ready, 1)
                ln.vector(dve, step, xn, x, xn_ready)
                dve.wait_ge(w_in, 48)
                step(nc.vector.tensor_scalar(bq[:, :], bq[:, :], HD ** -0.5, None, ALU.mult))
                dve.wait_ge(q_psum, 1)
                step(nc.vector.scalar_tensor_tensor(qf[:, :, :], ps[:, 5, :].rearrange("p (t c) -> p t c", t=TC), HD ** -0.5,
                                                    bq[:, :].unsqueeze(1).to_broadcast([P, TC, D]), ALU.mult, ALU.add))
                quantize_queries(nc, step, qf, qi, qq, qr, sc[:, :], rs[:, :], am[:, :], g["qs"], qs_ready)
                lead = step.n

                def copy_turned(m, s, i):
                    dve.wait_ge(kT_psum, m + 3)
                    dve.wait_ge(kT_ready, m + 2)
                    dve.wait_ge(kT_stored[s], i * 16 + 16)
                    nc.vector.tensor_copy(kT[s][:, :, :], psT[s]).then_inc(kT_ready, 1)

                def quantize_keys(m, s, i, more):
                    step.n = m * CH + lead
                    k4 = psum_kv(s, 0).rearrange("p c (h e) -> p c h e", e=HD)
                    i3 = ki[:, :, :].rearrange("p c (h e) -> p (c h) e", e=HD)
                    i4 = ki[:, :, :].rearrange("p c (h e) -> p c h e", e=HD)
                    am4 = am[:, :].rearrange("p (c h) -> p c h", c=KPS)
                    rs4 = rs[:, :].rearrange("p (c h) -> p c h", c=KPS)
                    dve.wait_ge(kv_psum, m + 1)
                    step(nc.vector.tensor_reduce(am4, k4, AX.X, ALU.max, apply_absolute_value=True))
                    step(nc.vector.tensor_scalar(sc[:, :], am[:, :], 1.0 / 127.0, 1e-8, ALU.mult, ALU.max))
                    step(nc.vector.reciprocal(rs[:, :], sc[:, :]))
                    nc.vector.tensor_tensor(i4, k4, rs4.unsqueeze(3).to_broadcast([P, KPS, H, HD]), ALU.mult).then_inc(k_read, 1)
                    dve.wait_ge(k_read, m + 3)
                    step(nc.vector.tensor_scalar(i3, i3, ROUND, ROUND, ALU.add, ALU.subtract))
                    dve.wait_ge(rest_ready, m + 1)
                    nc.vector.tensor_tensor(kq[s][:, :, :].rearrange("p c (h e) -> p (c h) e", e=HD), i3,
                                            sc[:, :].unsqueeze(2).to_broadcast([P, KPS * H, HD]), ALU.mult).then_inc(kq_ready, 1)
                    if isinstance(m, int) and m == STEPS - 1:
                        dve.wait_ge(part2_ready, m)
                        dve.wait_ge(part0_ready, m + 1)
                        dve.wait_ge(kq_ready, m + 1)
                        nc.vector.tensor_tensor(rest[s][:, :, :], kq[s][:, :, :], parts[s][:, 0],
                                                ALU.subtract).then_inc(rest_ready, 1)
                        copy_turned(m - 1, 1 - s, i - 1 + s)
                        dve.wait_ge(part1_ready, m + 1)
                        dve.wait_ge(rest_ready, m + 3)
                        nc.vector.tensor_tensor(parts[s][:, 2], rest[s][:, :, :], parts[s][:, 1],
                                                ALU.subtract).then_inc(part2_ready, 1)
                    dve.wait_ge(v_read, m + 3)
                    dve.wait_ge(vmax_ready, m + 1)
                    step(nc.vector.tensor_reduce(vstep[:, :], v[:, ds(m * KPS, KPS), :].rearrange("p c n -> p n c"), AX.X,
                                                 ALU.max, apply_absolute_value=True))
                    nc.vector.tensor_tensor(vam[:, :], vam[:, :], vstep[:, :], ALU.max).then_inc(vmax_ready, 1)
                all_steps(dve, quantize_keys)
                copy_turned(STEPS - 1, 1, STEPS // 2 - 1)
                dve.wait_ge(vmax_ready, STEPS + 1)
                dve.wait_ge(qs_ready, 1)

            @block.gpsimd
            def _(pool):
                nc.gpsimd.memset(bias_rows[:, :], 0.0).then_inc(bias_ready, 1)
                pool.wait_ge(bias_in, 16)
                for q in range(K_PARTS - 1):
                    pool.wait_ge(bias_ready, 2 + 2 * q)
                    nc.gpsimd.tensor_tensor(bias_rest[q][:, :], ([bkv] + bias_rest)[q][:, :], bias_part[q][:, :],
                                            ALU.subtract).then_inc(bias_ready, 1)
                pool.sem_inc(rest_ready, 2)

                def split(m, s, i, more):
                    if isinstance(m, int) and m == STEPS - 1:
                        return
                    pool.wait_ge(part0_ready, m + 1)
                    nc.gpsimd.tensor_tensor(rest[s][:, :, :], kq[s][:, :, :], parts[s][:, 0], ALU.subtract).then_inc(rest_ready, 1)
                    pool.wait_ge(part1_ready, m + 1)
                    nc.gpsimd.tensor_tensor(parts[s][:, 2], rest[s][:, :, :], parts[s][:, 1], ALU.subtract).then_inc(part2_ready, 1)
                all_steps(pool, split)

            @block.scalar
            def _(act):
                ln.scalar(act)
                act.wait_ge(bias_ready, 1)
                act.wait_ge(bias_in, 16)
                nc.scalar.activation(bias_part[0][:, :], bkv[:, :], ACT.Copy).then_inc(bias_ready, 1)
                for q in range(1, K_PARTS):
                    act.wait_ge(bias_ready, 1 + 2 * q)
                    nc.scalar.activation(bias_part[q][:, :], bias_rest[q - 1][:, :], ACT.Copy).then_inc(bias_ready, 1)
                    if q == 1:
                        act.wait_ge(xnT_psum, 1)
                        nc.scalar.activation(xnT[:, :, :], ps[:, 4, :].rearrange("p (k t) -> p k t", k=KC),
                                             ACT.Copy).then_inc(xnT_ready, 1)
                act.wait_ge(bias_ready, 2 * K_PARTS)
                for q in range(K_PARTS):
                    row = slice(32 * q, 32 * q + 1)
                    nc.scalar.activation(bias_rows[row, :], bias_part[q][row, :], ACT.Copy).then_inc(bias_ready, 1)
                act.preload_act_table(ACT.Copy)
                act.sem_inc(kT_ready, 2)
                act.sem_inc(v_read, 2)

                def copy_values(m, s):
                    act.wait_ge(kv_psum, m + 1)
                    nc.scalar.activation(v[:, ds(m * KPS, KPS), :], psum_kv(s, 1), ACT.Copy).then_inc(v_read, 1)

                def copy_turned(m, s, i):
                    act.wait_ge(kT_psum, m + 3)
                    act.wait_ge(kT_stored[s], i * 16 + 16)
                    nc.scalar.activation(kT[s][:, :, :], psT[s], ACT.Copy).then_inc(kT_ready, 1)

                def store(m, s):
                    act.wait_ge(kT_ready, m + 3)
                    act.dma_start(g["kT_store"][:, :, ds(m * KEYS, KEYS)], kT[s][:, :, :]).then_inc(kT_stored[s], 16)

                def split(m, s, i, more):
                    act.wait_ge(kq_ready, m + 1)
                    act.wait_ge(kT_psum, m + 1)
                    nc.scalar.activation(parts[s][:, 0], kq[s][:, :, :], ACT.Copy).then_inc(part0_ready, 1)
                    if more or s == 0:
                        copy_values(m + 1, 1 - s)
                    before = not (isinstance(m, int) and m == 0)
                    final = isinstance(m, int) and m == STEPS - 1
                    if before and not final:
                        copy_turned(m - 1, 1 - s, i - 1 + s)
                    act.wait_ge(rest_ready, m + 3)
                    nc.scalar.activation(parts[s][:, 1], rest[s][:, :, :], ACT.Copy).then_inc(part1_ready, 1)
                    if before:
                        store(m - 1, 1 - s)
                for s in range(2):
                    act.sem_inc(kT_stored[s], 16)
                copy_values(0, 0)
                all_steps(act, split)
                store(STEPS - 1, 1)
                act.wait_ge(v_read, STEPS + 2)

            @block.tensor
            def _(pe):
                pe.sem_inc(kT_psum, 2)
                keep_warm(nc, g, ps[:, 7, :], 10)
                pe.wait_ge(xn_ready, 1)
                transpose_tokens(nc, ps[:, 4, :], xn, ident).then_inc(xnT_psum, 1)
                pe.wait_ge(xnT_ready, 1)
                pe.wait_ge(w_in, 48)
                for t in range(TC):
                    for k in range(KC):
                        last = nc.tensor.matmul(ps[:, 5, t * D:(t + 1) * D], xnT[:, k, t * P:(t + 1) * P], wq[:, k, :],
                                                start=(k == 0), stop=(k == KC - 1))
                last.then_inc(q_psum, 1)

                def project(m, s, i):
                    pe.wait_ge(cT_in[s], i * 16 + 16)
                    pe.wait_ge(k_read, m + 1)
                    pe.wait_ge(v_read, m + 1)
                    for part in range(2):
                        cols = slice(part * D, (part + 1) * D)
                        for j in range(KPS):
                            for k in range(KC):
                                nc.tensor.matmul(psum_kv(s, part)[:, j, :], cT[s][:, k, j * P:(j + 1) * P], wkv[:, k, cols],
                                                 start=(k == 0), stop=False)
                            last = nc.tensor.matmul(psum_kv(s, part)[:, j, :], g["onesb"][0:K_PARTS * 32, :],
                                                    bias_rows[:, cols], start=False, stop=True)
                    last.then_inc(kv_psum, 1)

                def turn(m, s, i, more):
                    if more:
                        project(m + 2, s, i + 1)
                    else:
                        pe.wait_ge(k_read, STEPS + 1)
                        keep_warm(nc, g, ps[:, 0, :], 12 if s == 0 else 6)
                    pe.wait_ge(part2_ready, m + 1)
                    pe.wait_ge(kT_ready, m + 1)
                    for q in range(K_PARTS):
                        for k in range(KC):
                            for j in range(KPS):
                                last = nc.tensor.transpose(psT[s][:, q * KC + k, j * P:(j + 1) * P],
                                                           parts[s][:, q, j, k * P:(k + 1) * P], identb[:, :])
                    last.then_inc(kT_psum, 1)
                pe.wait_ge(bias_ready, 3 * K_PARTS)
                for s in range(2):
                    project(s, s, 0)
                all_steps(pe, turn)

LOG255 = 5.541263545158426


def xattn1_stage(nc, d, g):
    ctx, sb, banks, sem = scope(nc)
    x, ident, identb = g["x"], g["ident"], g["identb"]
    ROWS = QROWS + K_PARTS
    QT = 4
    QUARTER = NK // QT
    HPB = 4
    APH = TC * QT
    CPT = 4
    TPH = NKC // CPT
    with ctx:
        wp = sb("d_wp", [P, KC, D])
        bp = sb("d_bp", [P, D])
        spent = g["w0_early"][:, :, :].rearrange("p s f -> p (s f)")
        junk = [spent.bitcast(BF16)[:, f * QUARTER:(f + 1) * QUARTER] for f in range(QT)]
        qs = g["qs"]
        qT = sb("d_qT", [P, H, T], BF16)
        LOADED = 16 * K_PARTS
        kst = [sb(f"d_kst{s}", [ROWS, NK], BF16) for s in range(2)]
        nm = sb("d_nmax", [P, TC, H, QT])
        zp = sb("d_zpart", [P, TC, H, QT])
        mm = sb("d_mm", [P, TC, H])
        mx = sb("d_minus_max", [P, TC, H])
        mr = sb("d_mrest", [P, TC, H])
        rz = sb("d_rz", [P, TC, H])
        dm = sb("d_dm", [P, TC, H, QT])
        e = [sb(f"d_e{s}", [P, CPT * T])[:, :] for s in range(2)] \
            + [spent[:, (2 + s) * CPT * T:(3 + s) * CPT * T] for s in range(2)]
        pr = [sb(f"d_probs{s}", [P, CPT * T], BF16) for s in range(4)]
        vall = sb("d_v_absmax", [P, D])
        sv = sb("d_v_scale", [P, D])
        rsv = sb("d_v_rscale", [P, D])
        vhf = [sb(f"d_vh_scaled{s}", [P, NKC, HD]) for s in range(2)]
        vh = [sb(f"d_vh{s}", [P, NKC, HD], BF16) for s in range(2)]
        o = sb("d_o", [P, TC, D])
        oT = sb("d_oT", [P, KC, T])
        ps = banks("d_psum")
        flat = ps[:, :, :].rearrange("p a b -> p (a b)")
        flatb = flat.bitcast(BF16)
        chain = sem("d_dve_chain")
        w_in = sem("d_w_in")
        k_in = [sem(f"d_k_in{s}") for s in range(2)]
        ones_ready = sem("d_ones_ready")
        qs_ready = sem("d_qs_ready")
        qT_psum = sem("d_qT_psum")
        qTa_ready = sem("d_qTa_ready")
        qTv_ready = sem("d_qTv_ready")
        sA_ready = sem("d_sA_ready")
        nm_ready = sem("d_nm_ready")
        zp_ready = sem("d_zp_ready")
        dm_ready = sem("d_dm_ready")
        de_ready = sem("d_de_ready")
        sB_ready = sem("d_sB_ready")
        e_ready = sem("d_e_ready")
        p_ready = sem("d_p_ready")
        av_done = sem("d_av_done")
        vall_ready = sem("d_vall_ready")
        rsv_ready = sem("d_rsv_ready")
        vhf_ready = sem("d_vhf_ready")
        vh_ready = sem("d_vh_ready")
        o_ready = sem("d_o_ready")
        oT_psum = sem("d_oT_psum")
        oT_ready = sem("d_oT_ready")
        out_psum = sem("d_out_psum")

        def heads(eng, body):
            with eng.Fori(0, H // 2 - 1) as i:
                for s in range(2):
                    body(i * 2 + s, s, i, True)
            for s in range(2):
                body(H - 2 + s, s, H // 2 - 1, False)

        def turned(rnd):
            return flatb[:, rnd * H * T:(rnd + 1) * H * T]

        def transpose_q(pe, rows, rnd):
            for hd in range(H):
                for t in range(TC):
                    q = hd * TC + t
                    last = nc.tensor.transpose(turned(rnd)[0:rows, q * P:(q + 1) * P], qs[:, t, hd, 0:rows], identb[:, :])
                if hd % HPB == HPB - 1:
                    last.then_inc(qT_psum, 1)

        def copy_q(eng, copy, rows, some, rnd, done):
            for b in some:
                eng.wait_ge(qT_psum, rnd * (H // HPB) + b + 1)
                copy(qT[0:rows, b * HPB:(b + 1) * HPB, :],
                     turned(rnd)[0:rows, b * HPB * T:(b + 1) * HPB * T].rearrange("p (h t) -> p h t", h=HPB)).then_inc(done, 1)

        with nc.Block() as block:
            @block.sync
            def _(sp):
                for s in range(2):
                    sp.wait_ge(g["kT_stored"][s], 16 * (NKC // KPS // 2 + 1))

                parts = d["kT_scratch"].rearrange("(q c) n -> q c n", q=K_PARTS)

                def load_keys(row, s):
                    at = 0
                    for pq in range(K_PARTS):
                        n = K_PARTS - pq
                        sp.dma_start(kst[s][at * HD:(at + n) * HD, :],
                                     parts[0:n, ds(row, HD), :]).then_inc(k_in[s], 16)
                        at += n
                for s in range(2):
                    load_keys(s * HD, s)

                def refill_a(m, s, i, more):
                    row = sp.snap(m * HD + 2 * HD) if more else s * HD
                    sp.wait_ge(sA_ready, m * APH + APH)
                    load_keys(row, s)
                for dst, name in ((wp, "wp"), (bp, "bp")):
                    sp.dma_start(dst[:], d[name]).then_inc(w_in, 16)
                sp.dma_start(g["w_inT"][:, :, :], d["w_inT"]).then_inc(g["w_inT_in"], 16)
                heads(sp, refill_a)

                def refill_b(m, s, i, more):
                    if more:
                        row = sp.snap(m * HD + 2 * HD)
                        sp.wait_ge(sB_ready, m * TPH + TPH)
                        load_keys(row, s)
                heads(sp, refill_b)

            @block.gpsimd
            def _(pool):
                nc.gpsimd.partition_all_reduce(vall[:, :], g["vam"][:, :], P, RMAX).then_inc(vall_ready, 1)
                pool.wait_ge(rsv_ready, 1)
                for s in range(2):
                    nc.gpsimd.memset(kst[s][QROWS:ROWS, :], 1.0).then_inc(ones_ready, 1)
                pool.wait_ge(ones_ready, 2)
                for s in range(2):
                    nc.gpsimd.tensor_tensor(vhf[s][:, :, :], g["v"][:, :, s * HD:(s + 1) * HD],
                                            rsv[:, s * HD:(s + 1) * HD].unsqueeze(1).to_broadcast([P, NKC, HD]),
                                            ALU.mult).then_inc(vhf_ready, 1)

                def scale_values(m, s, i, more):
                    if more:
                        at = pool.snap(m * HD + 2 * HD)
                        pool.wait_ge(vh_ready, m + 1)
                        nc.gpsimd.tensor_tensor(vhf[s][:, :, :], g["v"][:, :, ds(at, HD)],
                                                rsv[:, ds(at, HD)].unsqueeze(1).to_broadcast([P, NKC, HD]),
                                                ALU.mult).then_inc(vhf_ready, 1)
                heads(pool, scale_values)

            @block.vector
            def _(dve):
                step = Steps(dve, chain)
                dve.wait_ge(vall_ready, 1)
                step(nc.vector.tensor_scalar(sv[:, :], vall[:, :], 1.0 / 127.0, 1e-8, ALU.mult, ALU.max))
                nc.vector.reciprocal(rsv[:, :], sv[:, :]).then_inc(rsv_ready, 1)

                copy_q(dve, nc.vector.tensor_copy, QROWS, (1, 3), 0, qTv_ready)

                def round_values(m, s):
                    dve.wait_ge(vhf_ready, m + 1)
                    nc.vector.tensor_scalar(vh[s][:, :, :], vhf[s][:, :, :], ROUND, ROUND, ALU.add, ALU.subtract)\
                      .then_inc(vh_ready, 1)

                def search(m, s, i, more):
                    for t in range(TC):
                        for f in range(QT):
                            dve.wait_ge(sA_ready, m * APH + (QT * t + f + 1))
                            nc.vector.tensor_reduce(nm[:, t, ds(m, 1), f:f + 1], flat[:, f * QUARTER:(f + 1) * QUARTER].unsqueeze(1),
                                                    AX.X, ALU.max, negate=True).then_inc(nm_ready, 1)
                heads(dve, search)
                dve.wait_ge(nm_ready, APH * H)
                step(nc.vector.tensor_reduce(mm[:, :, :], nm[:, :, :, :], AX.X, ALU.min))
                part = [qs[:, :, :, QROWS + q] for q in range(K_PARTS)]
                nc.vector.tensor_scalar(part[0], mm[:, :, :], LOG255, None, ALU.add)
                step(nc.vector.tensor_scalar(mx[:, :, :], mm[:, :, :], LOG255, None, ALU.add))
                nc.vector.tensor_tensor(part[1], mx[:, :, :], part[0], ALU.subtract)
                step(nc.vector.tensor_tensor(mr[:, :, :], mx[:, :, :], part[0], ALU.subtract))
                nc.vector.tensor_tensor(part[2], mr[:, :, :], part[1], ALU.subtract).then_inc(qs_ready, 1)
                nc.vector.tensor_tensor(dm[:, :, :, :], mm[:, :, :].unsqueeze(3).to_broadcast([P, TC, H, QT]), nm[:, :, :, :],
                                        ALU.subtract).then_inc(dm_ready, 1)
                copy_q(dve, nc.vector.tensor_copy, ROWS, (1, 2, 3), 1, qTv_ready)
                round_values(0, 0)
                round_values(1, 1)
                dve.wait_ge(de_ready, 1)
                dve.wait_ge(zp_ready, APH * H + QT)
                step(nc.vector.tensor_tensor(zp[:, :, :, :], zp[:, :, :, :], dm[:, :, :, :], ALU.mult))
                step(nc.vector.tensor_reduce(rz[:, :, :], zp[:, :, :, :], AX.X, ALU.add))
                step(nc.vector.tensor_scalar(rz[:, :, :], rz[:, :, :], 255.0, None, ALU.mult))
                step(nc.vector.reciprocal(rz[:, :, :], rz[:, :, :]))

                def finish(m, s, more):
                    dve.wait_ge(av_done, m * TPH + (TPH + 4))
                    nc.vector.tensor_tensor(o[:, :, ds(m * HD, HD)], ps[:, 4 + 2 * s:6 + 2 * s, 0:HD],
                                            rz[:, :, ds(m, 1)].to_broadcast([P, TC, HD]), ALU.mult).then_inc(o_ready, 1)
                    if more:
                        round_values(m + 2, s)

                def rounds(m, s, first, last):
                    for u in range(TPH):
                        b = m * TPH + u
                        dve.wait_ge(e_ready, b + 1)
                        dve.wait_ge(av_done, b + 1)
                        nc.vector.tensor_scalar(pr[u % 4][:, :], e[u % 4], ROUND, ROUND, ALU.add,
                                                ALU.subtract).then_inc(p_ready, 1)
                        if u == 2 and not first:
                            finish(m - 1, 1 - s, not last)
                for s in range(2):
                    rounds(s, s, s == 0, False)
                with dve.Fori(1, H // 2 - 1) as i:
                    for s in range(2):
                        rounds(i * 2 + s, s, False, False)
                for s in range(2):
                    rounds(H - 2 + s, s, False, s == 1)
                dve.wait_ge(w_in, 32)

                def scale(cols, n):
                    nc.vector.tensor_tensor(o[:, :, cols], o[:, :, cols], sv[:, cols].unsqueeze(1).to_broadcast([P, TC, n]),
                                            ALU.mult).then_inc(o_ready, 1)
                dve.wait_ge(o_ready, H - 1)
                scale(slice(0, D - HD), D - HD)
                finish(H - 1, 1, False)
                dve.wait_ge(o_ready, H + 1)
                scale(slice(D - HD, D), HD)
                step(nc.vector.tensor_tensor(x[:, :, :], x[:, :, :], bp[:, :].unsqueeze(1).to_broadcast([P, TC, D]), ALU.add))
                dve.wait_ge(out_psum, 1)
                step(nc.vector.tensor_tensor(x[:, :, :], x[:, :, :], ps[:, 1, :].rearrange("p (t c) -> p t c", t=TC), ALU.add))

            @block.scalar
            def _(act):
                act.preload_act_table(ACT.Exp)
                def copy(out, in_):
                    return nc.scalar.activation(out, in_, ACT.Copy)
                copy_q(act, copy, QROWS, (0, 2), 0, qTa_ready)
                act.sem_inc(zp_ready, QT)

                def sums(m, s, i, more):
                    for t in range(TC):
                        for f in range(QT):
                            act.wait_ge(nm_ready, m * APH + (QT * t + f + 1))
                            act.wait_ge(zp_ready, m * APH + (QT * t + f + 1))
                            nc.scalar.activation(junk[f].unsqueeze(1), flat[:, f * QUARTER:(f + 1) * QUARTER].unsqueeze(1), ACT.Exp,
                                                 bias=nm[:, t, ds(m, 1), f], accum_out=zp[:, t, ds(m, 1), f])\
                              .then_inc(zp_ready, 1)
                heads(act, sums)
                act.wait_ge(dm_ready, 1)
                nc.scalar.activation(dm[:, :, :, :], dm[:, :, :, :], ACT.Exp).then_inc(de_ready, 1)
                copy_q(act, copy, ROWS, (0,), 1, qTa_ready)

                def exps(m, s, i, more):
                    for u in range(TPH):
                        b = m * TPH + u
                        act.wait_ge(sB_ready, b + 1)
                        nc.scalar.activation(e[u % 4], flat[:, (u % 2) * CPT * T:(u % 2 + 1) * CPT * T],
                                             ACT.Exp).then_inc(e_ready, 1)
                heads(act, exps)
                act.wait_ge(oT_psum, 1)
                nc.scalar.activation(oT[:, :, :], ps[:, 0, :].rearrange("p (k t) -> p k t", k=KC),
                                     ACT.Copy).then_inc(oT_ready, 1)

            @block.tensor
            def _(pe):
                transpose_q(pe, QROWS, 0)
                pe.wait_ge(qTa_ready, 2)
                pe.wait_ge(qTv_ready, 2)

                def scores_a(m, s, i, more):
                    pe.wait_ge(k_in[s], i * LOADED + LOADED)
                    for t in range(TC):
                        for f in range(QT):
                            pe.wait_ge(zp_ready, m * APH + (QT * t + f + 1))
                            for c in range(QUARTER // 512):
                                at = f * QUARTER + c * 512
                                last = nc.tensor.matmul(flat[:, at:at + 512], qT[0:QROWS, ds(m, 1), t * P:(t + 1) * P],
                                                        kst[s][0:QROWS, at:at + 512], start=True, stop=True)
                            last.then_inc(sA_ready, 1)
                heads(pe, scores_a)
                pe.wait_ge(zp_ready, APH * H + QT - 1)
                keep_warm(nc, g, ps[:, 4, :], 6)
                pe.wait_ge(qs_ready, 1)
                pe.wait_ge(zp_ready, APH * H + QT)
                transpose_q(pe, ROWS, 1)
                pe.wait_ge(qTa_ready, 3)
                pe.wait_ge(ones_ready, 2)
                pe.sem_inc(av_done, 4)

                def tile_b(m, s, u):
                    keep_warm(nc, g, ps[:, (u % 2) * 2, :], 1, 2)
                    for c in range(CPT):
                        key = (u * CPT + c) * P
                        last = nc.tensor.matmul(flat[:, (u % 2) * CPT * T + c * T:(u % 2) * CPT * T + (c + 1) * T],
                                                kst[s][0:ROWS, key:key + P], qT[0:ROWS, ds(m, 1), :], start=True, stop=True)
                    last.then_inc(sB_ready, 1)

                def values_b(m, s, u):
                    pe.wait_ge(p_ready, m * TPH + (u + 1))
                    if u == 0:
                        pe.wait_ge(vh_ready, m + 1)
                    for c in range(CPT):
                        for t in range(TC):
                            last = nc.tensor.matmul(ps[:, 4 + 2 * s + t, 0:HD], pr[u % 4][:, c * T + t * P:c * T + (t + 1) * P],
                                                    vh[s][:, u * CPT + c, :], start=(u == 0 and c == 0),
                                                    stop=(u == TPH - 1 and c == CPT - 1))
                    last.then_inc(av_done, 1)

                def head_b(m, s, i, more, first=False):
                    for u in range(TPH):
                        b = m * TPH + u
                        if u + 2 < TPH or more or s == 0:
                            pe.wait_ge(e_ready, b + 1)
                            if u + 2 < TPH:
                                tile_b(m, s, u + 2)
                            else:
                                if u + 2 == TPH:
                                    pe.wait_ge(k_in[1 - s], i * LOADED + LOADED * (H // 2 + 1 + s))
                                tile_b(m + 1, 1 - s, u + 2 - TPH)
                        if u > 0:
                            values_b(m, s, u - 1)
                        elif not first:
                            values_b(m - 1, 1 - s, TPH - 1)
                pe.wait_ge(k_in[0], LOADED * (H // 2 + 1))
                tile_b(0, 0, 0)
                tile_b(0, 0, 1)
                pe.wait_ge(qTv_ready, 5)
                for s in range(2):
                    head_b(s, s, 0, True, s == 0)
                with pe.Fori(1, H // 2 - 1) as i:
                    for s in range(2):
                        head_b(i * 2 + s, s, i, True)
                for s in range(2):
                    head_b(H - 2 + s, s, H // 2 - 1, False)
                values_b(H - 1, 1, TPH - 1)
                keep_warm(nc, g, ps[:, 4, :], 3)
                pe.wait_ge(o_ready, H + 2)
                transpose_tokens(nc, ps[:, 0, :], o, ident).then_inc(oT_psum, 1)
                keep_warm(nc, g, ps[:, 4, :], 2)
                pe.wait_ge(oT_ready, 1)
                for t in range(TC):
                    for k in range(KC):
                        last = nc.tensor.matmul(ps[:, 1, t * D:(t + 1) * D], oT[:, k, t * P:(t + 1) * P], wp[:, k, :],
                                                start=(k == 0), stop=(k == KC - 1))
                last.then_inc(out_psum, 1)

def rms_norm(nc, dve, step, out, in_, ss, root_ready, count, done):
    dve.wait_ge(root_ready, count)
    step(nc.vector.tensor_scalar(ss[:, :, 1], ss[:, :, 1], 1e-12, None, ALU.max))
    step(nc.vector.reciprocal(ss[:, :, 1], ss[:, :, 1]))
    step(nc.vector.tensor_scalar(ss[:, :, 1], ss[:, :, 1], D ** 0.5, None, ALU.mult))
    nc.vector.tensor_tensor(out[:, :, :], in_[:, :, :], ss[:, :, 1:2].to_broadcast([P, TC, D]), ALU.mult).then_inc(done, 1)


def conv_stage(nc, d, g):
    ctx, sb, banks, sem = scope(nc)
    x, ident = g["x"], g["ident"]
    EC = INNER // P
    MC = MLP // P
    with ctx:
        w_in = g["w_inT"]
        w_out = sb("e_w_outT", [P, EC, D])
        mlp1 = sb("e_mlp1T", [P, KC, MLP])
        mlp2 = sb("e_mlp2T", [P, MC, D])
        conv = sb("e_conv", [P, EC, CONV + 1])
        y = sb("e_y", [P, TC, D])
        y1 = sb("e_y1", [P, TC, D])
        hn = sb("e_hn", [P, TC, D])
        sq = sb("e_sq", [P, TC, D])
        ss = sb("e_ss", [P, TC, 2])
        hT = sb("e_hT", [P, KC, T])
        h2T = sb("e_h2T", [P, KC, T])
        xc = sb("e_xc", [P, EC, T])
        sx = sb("e_sx", [P, EC, T])
        sz = sb("e_sz", [P, EC, T])
        gy = sb("e_gated", [P, EC, T])
        mh = sb("e_mlp_hidden", [P, MC, T])
        ps = banks("e_psum")
        ln = LayerNorm(nc, sb, sem, "e_ln")
        chain = sem("e_dve_chain")
        weights_in = sem("e_weights_in")
        y_ready = sem("e_y_ready")
        ss_ready = sem("e_ss_ready")
        root_ready = sem("e_root_ready")
        hn_ready = sem("e_hn_ready")
        hT_psum = sem("e_hT_psum")
        hT_ready = sem("e_hT_ready")
        xz_psum = sem("e_xz_psum")
        xc_ready = sem("e_xc_ready")
        sx_ready = sem("e_sx_ready")
        sz_ready = sem("e_sz_ready")
        gy_ready = sem("e_gy_ready")
        out_psum = sem("e_out_psum")
        m_psum = sem("e_m_psum")
        mh_ready = sem("e_mh_ready")
        mlp_psum = sem("e_mlp_psum")

        def xz(c):
            return ps[:, c // 2, (c % 2) * T:(c % 2 + 1) * T]

        with nc.Block() as block:
            @block.sync
            def _(sp):
                for dst, name in ((conv, "conv"), (w_out, "w_outT"), (mlp1, "mlp1T"), (mlp2, "mlp2T")):
                    sp.dma_start(dst[:], d[name]).then_inc(weights_in, 16)

            @block.vector
            def _(dve):
                step = Steps(dve, chain)
                ln.vector(dve, step, y, x, each=y_ready)
                rms_norm(nc, dve, step, hn, y, ss, root_ready, 1, hn_ready)
                dve.wait_ge(weights_in, 64)

                def gate(c):
                    dve.wait_ge(sx_ready, c + 1)
                    dve.wait_ge(sz_ready, EC // 2)
                    nc.vector.tensor_tensor(gy[:, c, :], sx[:, c, :], sz[:, c, :], ALU.mult).then_inc(gy_ready, 1)
                for c in range(EC):
                    dve.wait_ge(xz_psum, c // 2 + 1)
                    step(nc.vector.tensor_scalar(xc[:, c, :], xz(c), conv[:, c, CONV - 1:CONV], conv[:, c, CONV:CONV + 1],
                                                 ALU.mult, ALU.add))
                    acc = xc[:, c, :].rearrange("p (b l) -> p b l", l=L)
                    src = xz(c).rearrange("p (b l) -> p b l", l=L)
                    for j in range(1, CONV):
                        ins = nc.vector.scalar_tensor_tensor(acc[:, :, j:L], src[:, :, 0:L - j],
                                                             conv[:, c, CONV - 1 - j:CONV - j], acc[:, :, j:L],
                                                             ALU.mult, ALU.add)
                        if j < CONV - 1:
                            step(ins)
                    ins.then_inc(xc_ready, 1)
                    if c:
                        gate(c - 1)
                gate(EC - 1)
                dve.wait_ge(out_psum, 1)
                for t in range(TC):
                    nc.vector.tensor_tensor(y1[:, t, :], y[:, t, :], ps[:, 4 + t, 0:D], ALU.add).then_inc(y_ready, 1)
                rms_norm(nc, dve, step, hn, y1, ss, root_ready, 2, hn_ready)
                step(nc.vector.tensor_tensor(x[:, :, :], x[:, :, :], y1[:, :, :], ALU.add))
                for c in range(MC // 2):
                    dve.wait_ge(m_psum, c + 1)
                    nc.vector.tensor_scalar(mh[:, 2 * c:2 * c + 2, :], ps[:, c, :].rearrange("p (c t) -> p c t", c=2), 0.0,
                                            None, ALU.max).then_inc(mh_ready, 1)
                dve.wait_ge(mlp_psum, 1)
                step(nc.vector.tensor_tensor(x[:, :, :], x[:, :, :], ps[:, 6:8, 0:D], ALU.add))

            @block.scalar
            def _(act):
                def root(in_, count):
                    for t in range(TC):
                        act.wait_ge(y_ready, (count - 1) * TC + t + 1)
                        nc.scalar.activation(sq[:, t, :], in_[:, t, :], ACT.Square, accum_out=ss[:, t, 0:1]).then_inc(ss_ready, 1)
                    act.wait_ge(ss_ready, count * TC)
                    nc.scalar.activation(ss[:, :, 1], ss[:, :, 0], ACT.Sqrt).then_inc(root_ready, 1)

                def copy_hT(dst, count):
                    act.wait_ge(hT_psum, count)
                    nc.scalar.activation(dst[:, :, :], ps[:, 6 + count - 1, :].rearrange("p (k t) -> p k t", k=KC),
                                         ACT.Copy).then_inc(hT_ready, 1)
                ln.scalar(act)
                root(y, 1)
                copy_hT(hT, 1)
                act.preload_act_table(ACT.Silu)
                for c in range(EC // 2):
                    act.wait_ge(xz_psum, EC // 2 + c + 1)
                    nc.scalar.activation(sz[:, 2 * c:2 * c + 2, :], ps[:, 2 + c, :].rearrange("p (c t) -> p c t", c=2),
                                         ACT.Silu).then_inc(sz_ready, 1)
                for c in range(EC):
                    act.wait_ge(xc_ready, c + 1)
                    nc.scalar.activation(sx[:, c, :], xc[:, c, :], ACT.Silu).then_inc(sx_ready, 1)
                act.preload_act_table(ACT.Sqrt)
                root(y1, 2)
                copy_hT(h2T, 2)

            @block.tensor
            def _(pe):
                keep_warm(nc, g, ps[:, 5, :], 28)
                pe.wait_ge(hn_ready, 1)
                transpose_tokens(nc, ps[:, 6, :], hn, ident).then_inc(hT_psum, 1)
                keep_warm(nc, g, ps[:, 5, :], 3)
                pe.wait_ge(hT_ready, 1)
                pe.wait_ge(g["w_inT_in"], 16)
                for c in range(2 * EC):
                    for k in range(KC):
                        last = nc.tensor.matmul(xz(c), w_in[:, k, c * P:(c + 1) * P], hT[:, k, :], start=(k == 0),
                                                stop=(k == KC - 1))
                    if c % 2:
                        last.then_inc(xz_psum, 1)
                keep_warm(nc, g, ps[:, 5, :], 12)
                pe.wait_ge(weights_in, 64)
                for c in range(EC):
                    pe.wait_ge(gy_ready, c + 1)
                    for t in range(TC):
                        last = nc.tensor.matmul(ps[:, 4 + t, 0:D], gy[:, c, t * P:(t + 1) * P], w_out[:, c, :],
                                                start=(c == 0), stop=(c == EC - 1))
                last.then_inc(out_psum, 1)
                keep_warm(nc, g, ps[:, 6, :], 12)
                pe.wait_ge(hn_ready, 2)
                transpose_tokens(nc, ps[:, 7, :], hn, ident).then_inc(hT_psum, 1)
                keep_warm(nc, g, ps[:, 6, :], 3)
                pe.wait_ge(hT_ready, 2)
                for c in range(MC):
                    for k in range(KC):
                        last = nc.tensor.matmul(xz(c), mlp1[:, k, c * P:(c + 1) * P], h2T[:, k, :], start=(k == 0),
                                                stop=(k == KC - 1))
                    if c % 2:
                        last.then_inc(m_psum, 1)
                for c in range(MC):
                    pe.wait_ge(mh_ready, c // 2 + 1)
                    for t in range(TC):
                        last = nc.tensor.matmul(ps[:, 6 + t, 0:D], mh[:, c, t * P:(t + 1) * P], mlp2[:, c, :],
                                                start=(c == 0), stop=(c == MC - 1))
                last.then_inc(mlp_psum, 1)
def store_stage(nc, d, g):
    ctx, sb, banks, sem = scope(nc)
    with ctx:
        out_done = sem("out_done")
        with nc.Block() as block:
            @block.sync
            def _(sp):
                sp.dma_start(d["out"].rearrange("(t p) c -> p t c", p=P), g["x"][:, :, :]).then_inc(out_done, 16)
                sp.wait_ge(out_done, 16)




def build(nc, d):
    ctx, sb, banks, sem = scope(nc)
    g = {}
    with ctx:
        setup_stage(nc, d, g, sb, sem)
        d["kT_scratch"] = d["kT_scratch"].rearrange("q c n -> (q c) n")
        g["kT_store"] = d["kT_scratch"].rearrange("(a p) n -> p a n", p=P)
        stages = [xattn0_stage, scan_stage, lambda *a: moe_stage(*a, MOE0), kv_stage, xattn1_stage, conv_stage, lambda *a: moe_stage(*a, MOE1)]
        for stage in stages:
            if stage is kv_stage:
                layer1_memory(nc, d, g, sb, sem)
            stage(nc, d, g)
        store_stage(nc, d, g)


def kernel(**inputs):
    import numpy as np
    import concourse.bacc as bacc
    from concourse.bass_utils import run_bass_kernel_spmd

    def rows(a):
        return np.ascontiguousarray(np.broadcast_to(a.reshape(1, -1), (P, a.size)))

    def chunks(a):
        return np.ascontiguousarray(a.reshape(-1, P, a.shape[-1]).transpose(1, 0, 2))

    i = {k: np.asarray(v) for k, v in inputs.items()}
    ctxt = i["ctx_2048"].reshape(NK, D)
    mask = np.pad(i["mask_BxS2_bk0"].view(np.uint8)[..., None], ((0, 0), (0, 0), (0, 3))).view(np.int32)
    mask = mask.reshape(TC, B // TC, 1, S)
    arrays = {
        "x": np.ascontiguousarray(i["x"].reshape(T, D)),
        "ctx": chunks(ctxt),
        "ctxT": chunks(np.ascontiguousarray(ctxt.T)),
        "mask": np.ascontiguousarray(np.broadcast_to(mask, (TC, B // TC, L, S)).reshape(TC, P, S).transpose(1, 0, 2)),
    }
    def by_channel(*rows_):
        return np.ascontiguousarray(np.stack([r.reshape(KC, P) for r in rows_]).transpose(2, 0, 1))

    arrays |= {
        "xprojT": chunks(np.ascontiguousarray(i["L0_attn_x_proj_w"].T)),
        "dtwT": np.ascontiguousarray(i["L0_attn_dt_proj_w"].T),
        "outwT": chunks(np.ascontiguousarray(i["L0_attn_out_proj_w"].T)),
        "cols0": by_channel(i["L0_attn_norm_w"], i["L0_attn_norm_b"], i["L0_attn_dt_proj_b"], i["L0_attn_D_param"]),
        "A_log": chunks(i["L0_attn_A_log"]),
    }
    def groups(name, experts, per, f):
        n = experts // per
        gate, up = (i[name + w].reshape(n, per, KC, P, f).transpose(0, 3, 2, 1, 4).reshape(n, P, KC * per * f)
                    for w in ("gate", "up"))
        down = i[name + "down"].reshape(n, per * f, D)
        rows_ = -(-per * f // P) * P
        down = np.concatenate([down, np.zeros((n, rows_ - per * f, D), down.dtype)], axis=1)
        down = down.reshape(n, rows_ // P, P, D).transpose(0, 2, 1, 3).reshape(n, P, -1)
        return np.ascontiguousarray(np.concatenate([gate, up, down], axis=2))

    def shared(name):
        f = i[name + "gate"].shape[1]
        one = {name + w: i[name + w][None] for w in ("gate", "up", "down")}
        i.update(one)
        return groups(name, 1, 1, f)[0]

    arrays |= {
        "w_inT": chunks(np.ascontiguousarray(i["L1_attn_W_in"].T)),
        "w_outT": chunks(np.ascontiguousarray(i["L1_attn_W_out"].T)),
        "mlp1T": chunks(np.ascontiguousarray(i["L1_attn_W_mlp1"].T)),
        "mlp2T": chunks(np.ascontiguousarray(i["L1_attn_W_mlp2"].T)),
        "conv": chunks(np.ascontiguousarray(np.concatenate([i["L1_attn_conv_w"].reshape(INNER, CONV),
                                                            i["L1_attn_conv_b"].reshape(INNER, 1)], axis=1))),
        "gatef": chunks(np.ascontiguousarray(i["L1_ffn_gate_weight"].T)),
        "wq": chunks(i["L1_xattn_Wq"]),
        "bq": rows(i["L1_xattn_bq"]),
        "wp": chunks(i["L1_xattn_Wp"]),
        "bp": rows(i["L1_xattn_bp"]),
        "w1": groups("L1_ffn_w_", E1, EPG1, F1),
        "shared1": shared("L1_ffn_ws_"),
        "wkv": chunks(i["L1_xattn_Wkv"]),
        "bkv": rows(i["L1_xattn_bkv"]),
        "w0": groups("L0_ffn_w_", E0, EPG0, F0),
        "shared0": shared("L0_ffn_ws_"),
        "gatec": chunks(i["L0_ffn_gate_w"]),
        "bias0": rows(i["L0_ffn_bias"]),
    }
    nc = bacc.Bacc("TRN2", target_bir_lowering=False, num_devices=1)
    d = {n: nc.dram_tensor(f"in_{n}", a.shape, mybir.dt.from_np(a.dtype), kind="ExternalInput").ap()
         for n, a in arrays.items()}
    d["out"] = nc.dram_tensor("out", (T, D), F32, kind="ExternalOutput").ap()
    d["c_scratch"] = nc.dram_tensor("c_scratch", (N, T), F32).ap()
    d["kT_scratch"] = nc.dram_tensor("kT_scratch", (3, D, NK), BF16).ap()
    build(nc, d)
    r = run_bass_kernel_spmd(nc, [{f"in_{n}": a for n, a in arrays.items()}], core_ids=[0])
    return r.results[0]["out"].reshape(B, L, D)
```
